# Optimizing a Trainium2 kernel written in Bass

```python
import numpy as np
import jax
import jax.numpy as jnp

def _softmax(x, axis=-1):
    return jax.nn.softmax(x, axis=axis)

def _gelu(x):
    return jax.nn.gelu(x, approximate=True)

def _silu(x):
    return jax.nn.silu(x)

def _sigmoid(x):
    return jax.nn.sigmoid(x)

def _layernorm(x, axis=-1, eps=1e-05):
    m = jnp.mean(x, axis=axis, keepdims=True)
    v = jnp.var(x, axis=axis, keepdims=True)
    return (x - m) / jnp.sqrt(v + eps)

def _scatter_add(tgt, idx, src, axis=0):
    return tgt.at[idx].add(src)

def _segment_sum(src, seg, n):
    return jax.ops.segment_sum(src, seg, n)
kernel_name = 'mk_xattn_ffn_d1_seqx_r4_1e1269'

def setup_inputs(seed: int=0):
    np.random.seed(seed)
    _w = jnp.asarray

    def _rec_inputs():
        import jax
        import jax.numpy as jnp
        _rk = jax.random.key(seed)
        x = 0.01048 + 0.1018 * jax.random.normal(jax.random.fold_in(_rk, 1), (4, 512, 512), jnp.float32)
        _lenS = 512 - jax.random.randint(jax.random.fold_in(_rk, 7), (4,), 0, max(1, 512 // 4) + 1, jnp.int32)
        _lenS2 = 512 - jax.random.randint(jax.random.fold_in(_rk, 8), (4,), 0, max(1, 512 // 4) + 1, jnp.int32)
        _ctx_512P = jax.random.normal(jax.random.fold_in(_rk, 11), (4, 16, 128), jnp.float32)
        _ctx_512c = jax.random.dirichlet(jax.random.fold_in(_rk, 511), 0.3 * jnp.ones((16,), jnp.float32), (4, 512))
        _ctx_512t = jnp.einsum('bsk,bkd->bsd', _ctx_512c, _ctx_512P)
        _ctx_512t = _ctx_512t * jax.lax.rsqrt(jnp.mean(jnp.square(_ctx_512t)) + 1e-12) * 0.953939
        ctx_512 = -0.000292821 + 1.00034 * (_ctx_512t + 0.3 * jax.random.normal(jax.random.fold_in(_rk, 611), (4, 512, 128), jnp.float32))
        return (x, ctx_512)
    x, ctx_512 = _rec_inputs()

    def _L0_xattn_setup():
        import jax, jax.numpy as jnp
        import numpy as np
        LRELU_ALPHA = 0.2
        MASK_VAL = -10000000000.0
        B, N, F_IN = (4, 512, 128)
        H, F_OUT = (8, 64)
        F_HID = H * F_OUT

        def gat_layer(x, adj, W, a_self, a_neigh, b):
            feat = jnp.einsum('nf,hfo->hno', x, W)
            attn_self = jnp.einsum('hno,ho->hn', feat, a_self)
            attn_neigh = jnp.einsum('hno,ho->hn', feat, a_neigh)
            e = attn_self[:, :, None] + attn_neigh[:, None, :]
            e = jax.nn.leaky_relu(e, LRELU_ALPHA)
            e = e + MASK_VAL * (1.0 - adj)[None, :, :]
            alpha = jax.nn.softmax(e, axis=-1)
            out = jnp.einsum('hnm,hmo->hno', alpha, feat) + b[:, None, :]
            out = jnp.transpose(out, (1, 0, 2)).reshape(out.shape[1], -1)
            return jax.nn.elu(out)
        key = jax.random.key(seed)
        ks = jax.random.split(key, 10)
        feats = jax.random.normal(ks[0], (B, N, F_IN), dtype=jnp.float32)
        a = (jax.random.uniform(ks[1], (B, N, N)) < 0.01).astype(jnp.float32)
        adj = jnp.maximum(a, jnp.eye(N, dtype=jnp.float32)[None])
        s0 = 1.0 / np.sqrt(F_IN)
        s1 = 1.0 / np.sqrt(F_HID)
        return {'feats': feats, 'adj': adj, 'W0': jax.random.normal(ks[2], (H, F_IN, F_OUT), dtype=jnp.float32) * s0, 'a_self0': jax.random.normal(ks[3], (H, F_OUT), dtype=jnp.float32) * 0.1, 'a_neigh0': jax.random.normal(ks[4], (H, F_OUT), dtype=jnp.float32) * 0.1, 'b0': jnp.zeros((H, F_OUT), dtype=jnp.float32), 'W1': jax.random.normal(ks[5], (H, F_HID, F_OUT), dtype=jnp.float32) * s1, 'a_self1': jax.random.normal(ks[6], (H, F_OUT), dtype=jnp.float32) * 0.1, 'a_neigh1': jax.random.normal(ks[7], (H, F_OUT), dtype=jnp.float32) * 0.1, 'b1': jnp.zeros((H, F_OUT), dtype=jnp.float32)}
    _L0_xattn_all = _L0_xattn_setup()
    _L0_xattn_in = {k: v for k, v in _L0_xattn_all.items() if k in ('W0', 'a_self0', 'a_neigh0', 'b0', 'W1', 'a_self1', 'a_neigh1', 'b1')}
    del _L0_xattn_all

    def _L0_ffn_setup():
        import jax, jax.numpy as jnp
        import numpy as np
        NUM_EXPERTS = 4
        key = jax.random.key(seed)
        k1, k2, k3 = jax.random.split(key, 3)
        B, N, H = (8, 512, 512)
        E = NUM_EXPERTS
        I = H * 4 // E
        x = jax.random.normal(k1, (B, N, H), dtype=jnp.float32)
        gate_up_proj = jax.random.normal(k2, (E, H, 2 * I), dtype=jnp.float32) * 0.02
        down_proj = jax.random.normal(k3, (E, I, H), dtype=jnp.float32) * 0.02
        return {'x': x, 'gate_up_proj': gate_up_proj, 'down_proj': down_proj}
    _L0_ffn_all = _L0_ffn_setup()
    _L0_ffn_in = {k: v for k, v in _L0_ffn_all.items() if k in ('gate_up_proj', 'down_proj')}
    del _L0_ffn_all
    return {'x': x, 'ctx_512': ctx_512, 'L0_xattn_W0': _L0_xattn_in['W0'], 'L0_xattn_a_self0': _L0_xattn_in['a_self0'], 'L0_xattn_a_neigh0': _L0_xattn_in['a_neigh0'], 'L0_xattn_b0': _L0_xattn_in['b0'], 'L0_xattn_W1': _L0_xattn_in['W1'], 'L0_xattn_a_self1': _L0_xattn_in['a_self1'], 'L0_xattn_a_neigh1': _L0_xattn_in['a_neigh1'], 'L0_xattn_b1': _L0_xattn_in['b1'], 'L0_ffn_gate_up_proj': _L0_ffn_in['gate_up_proj'], 'L0_ffn_down_proj': _L0_ffn_in['down_proj']}

def reference(x, ctx_512, L0_xattn_W0, L0_xattn_a_self0, L0_xattn_a_neigh0, L0_xattn_b0, L0_xattn_W1, L0_xattn_a_self1, L0_xattn_a_neigh1, L0_xattn_b1, L0_ffn_gate_up_proj, L0_ffn_down_proj):
    import jax
    import jax.numpy as jnp

    def _L0_xattn_ref(feats, adj, W0, a_self0, a_neigh0, b0, W1, a_self1, a_neigh1, b1):
        import jax, jax.numpy as jnp
        import numpy as np
        LRELU_ALPHA = 0.2
        MASK_VAL = -10000000000.0
        B, N, F_IN = (4, 512, 128)
        H, F_OUT = (8, 64)
        F_HID = H * F_OUT

        def gat_layer(x, adj, W, a_self, a_neigh, b):
            feat = jnp.einsum('nf,hfo->hno', x, W)
            attn_self = jnp.einsum('hno,ho->hn', feat, a_self)
            attn_neigh = jnp.einsum('hno,ho->hn', feat, a_neigh)
            e = attn_self[:, :, None] + attn_neigh[:, None, :]
            e = jax.nn.leaky_relu(e, LRELU_ALPHA)
            e = e + MASK_VAL * (1.0 - adj)[None, :, :]
            alpha = jax.nn.softmax(e, axis=-1)
            out = jnp.einsum('hnm,hmo->hno', alpha, feat) + b[:, None, :]
            out = jnp.transpose(out, (1, 0, 2)).reshape(out.shape[1], -1)
            return jax.nn.elu(out)

        def per_graph(x, a):
            h = gat_layer(x, a, W0, a_self0, a_neigh0, b0)
            return gat_layer(h, a, W1, a_self1, a_neigh1, b1)
        return jax.vmap(per_graph)(feats, adj)

    def _L0_ffn_ref(x, gate_up_proj, down_proj):
        import jax, jax.numpy as jnp
        import numpy as np
        NUM_EXPERTS = 4
        B, N, H = x.shape
        E, _, two_I = gate_up_proj.shape
        I = two_I // 2
        G = N // E
        x4 = x.reshape(B, G, E, H)
        gu = jnp.einsum('bgeh,ehd->bged', x4, gate_up_proj)
        gate, up = (gu[..., :I], gu[..., I:])
        inter = jax.nn.silu(gate) * up
        out = jnp.einsum('bgei,eih->bgeh', inter, down_proj)
        return out.reshape(B, N, H)
    x = x + _L0_xattn_ref(ctx_512, _layernorm(x, axis=-1), L0_xattn_W0, L0_xattn_a_self0, L0_xattn_a_neigh0, L0_xattn_b0, L0_xattn_W1, L0_xattn_a_self1, L0_xattn_a_neigh1, L0_xattn_b1)
    x = x + _L0_ffn_ref(_layernorm(x, axis=-1), L0_ffn_gate_up_proj, L0_ffn_down_proj)
    return x

_drawn_inputs = setup_inputs


def setup_inputs(seed=0):
    import zlib

    import numpy as np

    out = dict(_drawn_inputs(seed))
    spreads = {'L0_xattn_b0': (0.0, 0.1), 'L0_xattn_b1': (0.0, 0.1)}
    factors = {}
    for name, (base, spread) in spreads.items():
        noise = np.random.default_rng([zlib.crc32(name.encode()), seed]).standard_normal(out[name].shape)
        drawn = base * np.exp(spread * noise) if base else spread * noise
        out[name] = jnp.asarray(drawn.astype(out[name].dtype))
    for name, factor in factors.items():
        out[name] = (out[name] * factor).astype(out[name].dtype)
    return out
```

```python
from contextlib import ExitStack

import concourse.bass as bass
from concourse import mybir

F32 = mybir.dt.float32
F32R = mybir.dt.float32r
BF16 = mybir.dt.bfloat16
I32 = mybir.dt.int32
ALU = mybir.AluOpType
ACT = mybir.ActivationFunctionType
AX = mybir.AxisListType
RMAX = bass.bass_isa.ReduceOp.max

P = 128
HI, LO = 0, 1
TERMS = ((HI, HI), (HI, LO), (LO, HI))
LN_EPS = 1e-5
MASK = 1e10
ROUNDINGS = 2.0 ** -20
UNDERFLOW = 110.0


GENERAL_SIGNALS = (
    "x_loaded", "layer_loaded", "x2_stored", "ffn_loaded", "out_stored",
    "consts", "ident", "veps", "rstd",
    "feat_made", "z_made", "prob_made", "probT_made", "att_exp", "silu_made",
    "stat", "mv", "adj", "one_minus", "mask", "inT_made", "prod", "score", "diag", "leaky", "logit",
    "neg_max", "inverse", "att", "att_neg", "elu", "x2", "xn", "inner", "out",
    "dve_waited", "pool_waited", "pe_waited", "sp_waited",
    "turned", "feat", "spread", "prob_turned", "att_done", "gate", "up", "down",
)


class General:

    def __init__(self, nc, gen, sems, bank, dram, sizes):
        self.nc, self.t, self.s, self.bank, self.dram = nc, gen, sems, bank, dram
        self.B, self.N, self.D, self.F_IN, self.H, self.FO, self.E, self.KC, self.DI = sizes
        self.loads = (4, self.KC + 3)

    def layer_no(self, b, layer):
        return b * 2 + layer

    def head_no(self, b, layer, h):
        return b * (2 * self.H) + h + layer * self.H

    def unit(self, b, layer, h, e):
        return b * (2 * self.H * self.E) + h * self.E + (layer * self.H * self.E + e)

    def chunk_no(self, b, layer, c):
        return b * (1 + self.KC) + layer + c

    def sync(self, sp):
        t, s, d, B, E, KC, H = self.t, self.s, self.dram, self.B, self.E, self.KC, self.H
        flat = lambda v: v.rearrange("h o -> (h o)").partition_broadcast(P)
        heads = lambda v: v.rearrange("p (h o) -> p h o", h=H)
        with sp.Fori(0, B) as b:
            sp.wait_ge(s["x2_stored"], b * 16)
            sp.sem_inc(s["sp_waited"], 1)
            sp.wait_ge(s["turned"], b * (1 + KC))
            sp.dma_start(t["x"][:, :, :], d["x"][b]).then_inc(s["x_loaded"], 16)
            sp.dma_start(t["ctx"][:, :, :], d["ctx"][b]).then_inc(s["x_loaded"], 16)
            for layer in range(2):
                sp.wait_ge(s["att"], self.unit(b, layer, 0, 0))
                if layer == 0:
                    sp.dma_start(heads(t["W"][:, 0, :]), d["W0"].rearrange("h f o -> f h o"))\
                        .then_inc(s["layer_loaded"], 16)
                else:
                    for c in range(KC):
                        sp.dma_start(heads(t["W"][:, c, :]), d["W1"][:, c]).then_inc(s["layer_loaded"], 16)
                for j, name in enumerate(("a_self", "a_neigh")):
                    sp.dma_start(t["a"][:, j, :], flat(d[f"{name}{layer}"])).then_inc(s["layer_loaded"], 16)
                sp.dma_start(t["bias"][:, :], flat(d[f"b{layer}"])).then_inc(s["layer_loaded"], 16)
            sp.wait_ge(s["x2"], b + 1)
            sp.dma_start(d["out"].rearrange("b (g e) d -> b g e d", e=E)[b], t["x"][:, :, :])\
                .then_inc(s["x2_stored"], 16)
        sp.wait_ge(s["x2_stored"], 16 * B)
        rows = d["out"].rearrange("b (g e) d -> e g b d", e=E)
        with sp.Fori(0, E) as e:
            sp.wait_ge(s["out_stored"], e * 16)
            sp.sem_inc(s["sp_waited"], 1)
            sp.wait_ge(s["down"], e * B)
            sp.sem_inc(s["sp_waited"], 1)
            sp.dma_start(t["x"][:, :, :], rows[e]).then_inc(s["ffn_loaded"], 16)
            sp.dma_start(t["gate_up"][:, :, :], d["gate_up"][e]).then_inc(s["ffn_loaded"], 16)
            sp.dma_start(t["down"][:, :, :], d["down"][e]).then_inc(s["ffn_loaded"], 16)
            sp.wait_ge(s["out"], e * B + B)
            sp.sem_inc(s["sp_waited"], 1)
            sp.dma_start(rows[e], t["x"][:, :, :]).then_inc(s["out_stored"], 16)
        sp.wait_ge(s["out_stored"], 16 * E)

    def gpsimd(self, pool):
        t, s, B, E, nc = self.t, self.s, self.B, self.E, self.nc
        nc.gpsimd.memset(t["ones"][:, :], 1.0).then_inc(s["consts"], 1)
        nc.gpsimd.memset(t["ident"][:, :], 0.0).then_inc(s["consts"], 1)
        nc.gpsimd.memset(t["power"][:, :], -0.5).then_inc(s["consts"], 1)
        pool.wait_ge(s["consts"], 3)
        nc.gpsimd.affine_select(out=t["ident"][:, :], in_=t["ident"][:, :], compare_op=ALU.not_equal, fill=1.0,
                                base=0, pattern=[[-1, P]], channel_multiplier=1).then_inc(s["ident"], 1)
        with pool.Fori(0, B + E) as i:
            pool.wait_ge(s["mv"], i * 4 + 4)
            pool.sem_inc(s["pool_waited"], 1)
            nc.gpsimd.tensor_scalar(t["veps"][:, :], t["mv"][:, :, 1], LN_EPS, None, ALU.add)\
                .then_inc(s["veps"], 1)
            pool.wait_ge(s["veps"], i + 1)
            nc.gpsimd.tensor_tensor(t["rstd"][:, :], t["veps"][:, :], t["power"][:, :], ALU.pow)\
                .then_inc(s["rstd"], 1)

    def scalar(self, act):
        t, s, B, E, KC, H, nc, bank = self.t, self.s, self.B, self.E, self.KC, self.H, self.nc, self.bank
        with act.Fori(0, B) as b:
            for layer in range(2):
                for m in range(E):
                    n = self.layer_no(b, layer) * E + m
                    act.wait_ge(s["feat"], n + 1)
                    if m == 0:
                        act.wait_ge(s["att"], self.unit(b, layer, 0, 0))
                    nc.scalar.copy(t["feat"][:, m, :], bank[1][:, :]).then_inc(s["feat_made"], 1)
                with act.Fori(0, H) as h:
                    act.wait_ge(s["spread"], self.head_no(b, layer, h) + 1)
                    act.wait_ge(s["score"], self.layer_no(b, layer) * (2 * E) + 2 * E)
                    for e in range(E):
                        u = self.unit(b, layer, h, e)
                        act.wait_ge(s["leaky"], u)
                        nc.scalar.activation(t["z"][:, :], bank[2][:, :], ACT.Identity,
                                             bias=t["score"][:, 0, e, bass.ds(h, 1)]).then_inc(s["z_made"], 1)
                        act.wait_ge(s["neg_max"], u + 1)
                        act.wait_ge(s["prob_turned"], u)
                        act.wait_ge(s["inverse"], u)
                        nc.scalar.activation(t["prob"][:, :], t["logit"][:, :], ACT.Exp, bias=t["row"][:, 1:2],
                                             accum_out=t["row"][:, 2:3]).then_inc(s["prob_made"], 1)
                        act.wait_ge(s["prob_turned"], u + 1)
                        nc.scalar.copy(t["probT"][:, :, :].rearrange("p m g -> p (m g)"), bank[3][:, :])\
                            .then_inc(s["probT_made"], 1)
                act.wait_ge(s["att"], self.unit(b, layer, 0, 0) + H * E)
                act.wait_ge(s["elu"], self.layer_no(b, layer))
                nc.scalar.activation(t["exp"][:, :, :], t["att"][:, :, :], ACT.Exp).then_inc(s["att_exp"], 1)
        with act.Fori(0, E) as e:
            for c in range(KC):
                act.wait_ge(s["gate"], e * KC + (c + 1))
                act.wait_ge(s["inner"], e * KC + c)
                nc.scalar.activation(t["silu"][:, :], bank[1][:, :], ACT.Silu).then_inc(s["silu_made"], 1)

    def normalize(self, dve, i, load, loaded, free, dst):
        t, s, nc = self.t, self.s, self.nc
        dve.wait_ge(load, loaded)
        for e in range(self.E):
            nc.vector.bn_stats(t["stat"][:, e, :], t["x"][:, e, :]).then_inc(s["stat"], 1)
        dve.wait_ge(s["rstd"], i)
        dve.wait_ge(s["stat"], i * 4 + 4)
        dve.sem_inc(s["dve_waited"], 1)
        for e in range(self.E):
            nc.vector.bn_aggr(t["mv"][:, e, :], t["stat"][:, e, :]).then_inc(s["mv"], 1)
        dve.wait_ge(s["rstd"], i + 1)
        dve.wait_ge(s["mv"], i * 4 + 4)
        free()
        for e in range(self.E):
            src, to, signal = dst(e)
            nc.vector.tensor_scalar(to, src, t["mv"][:, e, 0:1], t["rstd"][:, e:e + 1], ALU.subtract, ALU.mult)\
                .then_inc(signal, 1)

    def vector(self, dve):
        t, s, B, E, KC, H, FO = self.t, self.s, self.B, self.E, self.KC, self.H, self.FO
        nc, bank, unit = self.nc, self.bank, self.unit
        every = lambda v: v.rearrange("p e d -> p (e d)")
        mask = t["mask"][:, :, :, :].rearrange("p e r g -> p (e r g)")
        dve.wait_ge(s["ident"], 1)
        with dve.Fori(0, B) as b:
            def adj(e):
                return (t["x"][:, e, :].rearrange("p (g r) -> p g r", r=E),
                        t["mask"][:, e, :, :].rearrange("p r g -> p g r"), s["adj"])

            self.normalize(dve, b, s["x_loaded"], b * 32 + 32, lambda: None, adj)
            dve.wait_ge(s["adj"], b * E + E)
            nc.vector.tensor_scalar(mask, mask, -1.0, 1.0, ALU.mult, ALU.add).then_inc(s["one_minus"], 1)
            dve.wait_ge(s["one_minus"], b + 1)
            nc.vector.tensor_scalar(mask, mask, -MASK, None, ALU.mult).then_inc(s["mask"], 1)
            dve.wait_ge(s["mask"], b + 1)
            for layer in range(2):
                for c in range(1 if layer == 0 else KC):
                    n = self.chunk_no(b, layer, c)
                    dve.wait_ge(s["turned"], n + 1)
                    nc.vector.tensor_copy(t["inT"][:, c, :], bank[0][:, :]).then_inc(s["inT_made"], 1)
                for m in range(E):
                    dve.wait_ge(s["feat_made"], self.layer_no(b, layer) * E + (m + 1))
                    for j in range(2):
                        n = self.layer_no(b, layer) * (2 * E) + (2 * m + j)
                        dve.wait_ge(s["score"], n)
                        nc.vector.tensor_tensor(t["prod"][:, :], t["feat"][:, m, :], t["a"][:, j, :], ALU.mult)\
                            .then_inc(s["prod"], 1)
                        dve.wait_ge(s["prod"], n + 1)
                        nc.vector.tensor_reduce(t["score"][:, j, m, :],
                                                t["prod"][:, :].rearrange("p (h o) -> p h o", h=H), AX.X, ALU.add)\
                            .then_inc(s["score"], 1)
                dve.wait_ge(s["score"], self.layer_no(b, layer) * (2 * E) + 2 * E)
                dve.sem_inc(s["dve_waited"], 1)
                with dve.Fori(0, H) as h:
                    dve.wait_ge(s["spread"], self.head_no(b, layer, h))
                    for m in range(E):
                        nc.vector.tensor_scalar(t["diag"][:, m, :], t["ident"][:, :],
                                                t["score"][:, 1, m, bass.ds(h, 1)], None, ALU.mult)\
                            .then_inc(s["diag"], 1)
                    for e in range(E):
                        u = unit(b, layer, h, e)
                        dve.wait_ge(s["z_made"], u + 1)
                        nc.vector.scalar_tensor_tensor(t["leaky"][:, :], t["z"][:, :], 0.2, t["z"][:, :],
                                                       ALU.mult, ALU.max).then_inc(s["leaky"], 1)
                        dve.wait_ge(s["leaky"], u + 1)
                        dve.wait_ge(s["prob_made"], u)
                        dve.sem_inc(s["dve_waited"], 1)
                        nc.vector.tensor_tensor_reduce(
                            t["logit"][:, :], t["leaky"][:, :],
                            t["mask"][:, e, :, :].rearrange("p r g -> p (r g)"), 1.0, -3e38, ALU.add, ALU.max,
                            t["row"][:, 0:1]).then_inc(s["logit"], 1)
                        dve.wait_ge(s["logit"], u + 1)
                        nc.vector.tensor_scalar(t["row"][:, 1:2], t["row"][:, 0:1], -1.0, None, ALU.mult)\
                            .then_inc(s["neg_max"], 1)
                        dve.wait_ge(s["prob_made"], u + 1)
                        nc.vector.reciprocal(t["row"][:, 3:4], t["row"][:, 2:3]).then_inc(s["inverse"], 1)
                        dve.wait_ge(s["inverse"], u + 1)
                        dve.wait_ge(s["att_done"], u + 1)
                        cols = bass.ds(h * FO, FO)
                        nc.vector.scalar_tensor_tensor(t["att"][:, e, cols], bank[4][:, 0:FO], t["row"][:, 3:4],
                                                       t["bias"][:, cols], ALU.mult, ALU.add).then_inc(s["att"], 1)
                n = self.layer_no(b, layer)
                dve.wait_ge(s["att_exp"], n + 1)
                nc.vector.tensor_scalar(every(t["exp"]), every(t["exp"]), 1.0, -1.0, ALU.min, ALU.add)\
                    .then_inc(s["att_neg"], 1)
                dve.wait_ge(s["att_neg"], n + 1)
                dve.wait_ge(s["att"], unit(b, layer, 0, 0) + H * E)
                nc.vector.tensor_tensor(every(t["att"]), every(t["att"]), every(t["exp"]), ALU.max)\
                    .then_inc(s["elu"], 1)
            dve.wait_ge(s["elu"], b * 2 + 2)
            nc.vector.tensor_tensor(every(t["x"]), every(t["x"]), every(t["att"]), ALU.add).then_inc(s["x2"], 1)
        with dve.Fori(0, E) as g:
            def free():
                dve.wait_ge(s["turned"], g * KC + B * (1 + KC))

            self.normalize(dve, g + B, s["ffn_loaded"], g * 48 + 48, free,
                           lambda b: (t["x"][:, b, :], t["xn"][:, b, :], s["xn"]))
            for k in range(KC):
                n = g * KC + (B * (1 + KC) + k)
                dve.wait_ge(s["turned"], n + 1)
                nc.vector.tensor_copy(t["inT"][:, k, :], bank[0][:, :]).then_inc(s["inT_made"], 1)
            for c in range(KC):
                dve.wait_ge(s["silu_made"], g * KC + (c + 1))
                dve.wait_ge(s["up"], g * KC + (c + 1))
                nc.vector.tensor_tensor(t["inner"][:, c, :], bank[2][:, :], t["silu"][:, :], ALU.mult)\
                    .then_inc(s["inner"], 1)
            for b in range(B):
                dve.wait_ge(s["down"], g * B + (b + 1))
                nc.vector.tensor_tensor(t["x"][:, b, :], t["x"][:, b, :], bank[3][:, :], ALU.add)\
                    .then_inc(s["out"], 1)

    def tensor(self, pe):
        t, s, B, E, KC, H, FO, DI = self.t, self.s, self.B, self.E, self.KC, self.H, self.FO, self.DI
        nc, bank = self.nc, self.bank
        pe.wait_ge(s["ident"], 1)
        pe.wait_ge(s["consts"], 3)
        with pe.Fori(0, B) as b:
            pe.wait_ge(s["x_loaded"], b * 32 + 32)
            for layer in range(2):
                chunks = 1 if layer == 0 else KC
                if layer == 1:
                    pe.wait_ge(s["elu"], b * 2 + 1)
                for c in range(chunks):
                    n = self.chunk_no(b, layer, c)
                    pe.wait_ge(s["inT_made"], n)
                    for m in range(E):
                        src = t["ctx"][:, m, :] if layer == 0 else t["att"][:, m, c * P:(c + 1) * P]
                        last = nc.tensor.transpose(bank[0][:, m * P:(m + 1) * P], src, t["ident"][:, :])
                    last.then_inc(s["turned"], 1)
                pe.wait_ge(s["inT_made"], self.chunk_no(b, layer, chunks))
                before = 0 if layer == 0 else self.loads[0]
                pe.wait_ge(s["layer_loaded"], b * (16 * sum(self.loads)) + 16 * (before + self.loads[layer]))
                for m in range(E):
                    pe.wait_ge(s["feat_made"], self.layer_no(b, layer) * E + m)
                    for c in range(chunks):
                        last = nc.tensor.matmul(bank[1][:, :], t["inT"][:, c, m * P:(m + 1) * P], t["W"][:, c, :],
                                                start=(c == 0), stop=(c == chunks - 1))
                    last.then_inc(s["feat"], 1)
                pe.wait_ge(s["feat_made"], self.layer_no(b, layer) * E + E)
                pe.sem_inc(s["pe_waited"], 1)
                with pe.Fori(0, H) as h:
                    pe.wait_ge(s["diag"], self.head_no(b, layer, h) * E + E)
                    pe.wait_ge(s["z_made"], self.unit(b, layer, h, 0))
                    nc.tensor.matmul(bank[2][:, :], t["ones"][:, :],
                                     t["diag"][:, :, :].rearrange("p m g -> p (m g)"), start=True, stop=True)\
                        .then_inc(s["spread"], 1)
                    for e in range(E):
                        u = self.unit(b, layer, h, e)
                        pe.wait_ge(s["prob_made"], u + 1)
                        for m in range(E):
                            last = nc.tensor.transpose(bank[3][:, m * P:(m + 1) * P],
                                                       t["prob"][:, m * P:(m + 1) * P], t["ident"][:, :])
                        last.then_inc(s["prob_turned"], 1)
                        pe.wait_ge(s["probT_made"], u + 1)
                        pe.wait_ge(s["att"], u)
                        for m in range(E):
                            last = nc.tensor.matmul(bank[4][:, 0:FO], t["probT"][:, m, :],
                                                    t["feat"][:, m, bass.ds(h * FO, FO)],
                                                    start=(m == 0), stop=(m == E - 1))
                        last.then_inc(s["att_done"], 1)
        with pe.Fori(0, E) as g:
            pe.wait_ge(s["ffn_loaded"], g * 48 + 48)
            pe.wait_ge(s["xn"], g * B + B)
            for k in range(KC):
                n = g * KC + (B * (1 + KC) + k)
                pe.wait_ge(s["inT_made"], n)
                for b in range(B):
                    last = nc.tensor.transpose(bank[0][:, b * P:(b + 1) * P], t["xn"][:, b, k * P:(k + 1) * P],
                                               t["ident"][:, :])
                last.then_inc(s["turned"], 1)
            pe.wait_ge(s["inT_made"], g * KC + (B * (1 + KC) + KC))
            for c in range(KC):
                pe.wait_ge(s["inner"], g * KC + c)
                for half, name in enumerate(("gate", "up")):
                    for k in range(KC):
                        last = nc.tensor.matmul(bank[1 + half][:, :],
                                                t["gate_up"][:, k, half * DI + c * P:half * DI + (c + 1) * P],
                                                t["inT"][:, k, :], start=(k == 0), stop=(k == KC - 1))
                    last.then_inc(s[name], 1)
            pe.wait_ge(s["inner"], g * KC + KC)
            for b in range(B):
                pe.wait_ge(s["out"], g * B + b)
                for i in range(KC):
                    last = nc.tensor.matmul(bank[3][:, :], t["inner"][:, i, b * P:(b + 1) * P], t["down"][:, i, :],
                                            start=(i == 0), stop=(i == KC - 1))
                last.then_inc(s["down"], 1)


def build(nc, x, ctx, W0, a_self0, a_neigh0, b0, W1, a_self1, a_neigh1, b1, gate_up, down, out):
    B, N, D = x.shape
    F_IN = ctx.shape[2]
    H, _, FO = W0.shape
    E = gate_up.shape[0]
    KC = D // P
    DI = down.shape[1]
    D2 = 2 * DI
    assert N == E * P and D == N == DI == H * FO and F_IN == P and KC == E == B

    x_rows = x.rearrange("b (g e) d -> b g e d", e=E)
    out_rows = out.rearrange("b (g e) d -> b e g d", e=E)
    ctx_rows = ctx.rearrange("b (g e) f -> b g e f", e=E)

    with ExitStack() as stack:
        def sem(name):
            return stack.enter_context(nc.semaphore(name))

        def sb_in(where):
            return lambda name, shape, dt=F32: where.enter_context(nc.sbuf_tensor(name, shape, dt))

        main = ExitStack()
        sb = sb_in(main)

        x_sb = sb("x_sb", [P, B, E, D])
        sel_ctx = sb("sel_ctx", [P, 2, E, B, P], F32R)
        W0p = sb("W0p", [P, 2, D], F32R)
        W1p = sb("W1p", [P, KC, 2, D], F32R)
        xnT = sb("xnT", [P, KC, 2, B * P], F32R)
        ctx_xn = sb("ctx_xn", [P, B, D])
        stage = sb("stage", [P, 4, 2 * D])
        ident = sb("ident", [P, P])
        ident_bf = sb("ident_bf", [P, P], BF16)
        ones = sb("ones", [P, P])
        ones_bf = sb("ones_bf", [P, P], BF16)
        b0_col = sb("b0_col", [P, KC])
        b1_rows = sb("b1_rows", [P, D])
        a_abs = sb("a_abs", [H, 4, FO])
        top8 = sb("top8", [P, B, E, 8])
        xstat = sb("xstat", [P, B, E, 6])
        xmv = sb("xmv", [P, B * E, 2])
        x2stat = sb("x2stat", [P, B, 6])
        x2mv = sb("x2mv", [P, B, 2])
        veps = sb("veps", [P, B * E])
        rstd = sb("rstd", [P, B])
        xrstd = sb("xrstd", [P, B * E])
        minus_half = sb("minus_half", [P, B * E])
        rowmax = sb("rowmax", [P, 4])
        allmax = sb("allmax", [P, 4])
        colmax = sb("colmax", [P, 2])
        bound = sb("bound", [P, 6])
        gap = sb("gap", [P, B * E])
        lead = sb("lead", [P, B * E])
        sure = sb("sure", [P, B * E])
        sure_n = sb("sure_n", [P, 1])
        flag = sb("flag", [1, 1], I32)
        ctx_sb = ctx_xn[:, :, :].rearrange("p b (e f) -> p b e f", e=E)
        xn = ctx_xn

        with ExitStack() as early:
            sbe = sb_in(early)
            G = sbe("G", [P, 2, E, N], BF16)
            GT = sbe("GT", [P, 2, E, N], F32R)
            ctxp = sbe("ctxp", [P, 2, E, 2, F_IN], F32R)
            sel1 = sbe("sel1", [P, 2, E, 2, F_IN], F32R)
            absw = sbe("absw", [P, 1 + KC, D], BF16)
        sbl = sb
        GUp = sbl("GUp", [P, KC, 2, D2], F32R)
        DNp = sbl("DNp", [P, KC, 2, D], F32R)
        hTp = sbl("hTp", [P, KC, 2, B * P], F32R)
        ex = sbl("ex", [P, 2, D])
        val = sbl("val", [P, 4, D])

        main.close()

        gsb = sb_in(stack)
        gen = {
            "x": gsb("gen_x", [P, E, D]),
            "mask": gsb("gen_mask", [P, E, E, P]),
            "ctx": gsb("gen_ctx", [P, E, F_IN]),
            "W": gsb("gen_W", [P, KC, D]),
            "a": gsb("gen_a", [P, 2, D]),
            "bias": gsb("gen_bias", [P, D]),
            "inT": gsb("gen_inT", [P, KC, N]),
            "feat": gsb("gen_feat", [P, E, D]),
            "prod": gsb("gen_prod", [P, D]),
            "score": gsb("gen_score", [P, 2, E, H]),
            "diag": gsb("gen_diag", [P, E, P]),
            "z": gsb("gen_z", [P, N]),
            "leaky": gsb("gen_leaky", [P, N]),
            "logit": gsb("gen_logit", [P, N]),
            "prob": gsb("gen_prob", [P, N]),
            "probT": gsb("gen_probT", [P, E, P]),
            "row": gsb("gen_row", [P, 4]),
            "att": gsb("gen_att", [P, E, D]),
            "exp": gsb("gen_exp", [P, E, D]),
            "ident": gsb("gen_ident", [P, P]),
            "ones": gsb("gen_ones", [P, P]),
            "stat": gsb("gen_stat", [P, E, 6]),
            "mv": gsb("gen_mv", [P, E, 2]),
            "veps": gsb("gen_veps", [P, E]),
            "rstd": gsb("gen_rstd", [P, E]),
            "power": gsb("gen_power", [P, E]),
            "gate_up": gsb("gen_gate_up", [P, KC, D2]),
            "down": gsb("gen_down", [P, KC, D]),
            "xn": gsb("gen_xn", [P, B, D]),
            "silu": gsb("gen_silu", [P, D]),
            "inner": gsb("gen_inner", [P, KC, B * P]),
        }

        bank = [stack.enter_context(nc.psum_tensor(f"bank{i}", [P, 512], F32)) for i in range(8)]

        x_loaded = [sem(f"x_loaded{b}") for b in range(B)]
        ctx_loaded = [sem(f"ctx_loaded{b}") for b in range(B)]
        small_loaded = sem("small_loaded")
        stage_loaded = [sem(f"stage_loaded{s}") for s in range(4)]
        out_stored = sem("out_stored")
        consts_made = sem("consts_made")
        ident_made = sem("ident_made")
        ctx_lo = sem("ctx_lo")
        w_lo = sem("w_lo")
        veps_made = sem("veps_made")
        rstd_made = sem("rstd_made")
        allmax_made = sem("allmax_made")
        in_lo = sem("in_lo")
        ctx_hi = sem("ctx_hi")
        w_hi = sem("w_hi")
        abs_made = sem("abs_made")
        GT_even = sem("GT_even")
        sel1_front = sem("sel1_front")
        sel_hi = sem("sel_hi")
        h_exp = sem("h_exp")
        h_hi = sem("h_hi")
        y_exp = sem("y_exp")
        xnT_hi = sem("xnT_hi")
        silu_made = sem("silu_made")
        in_hi = sem("in_hi")
        top_found = sem("top_found")
        G_made = sem("G_made")
        GT_odd = sem("GT_odd")
        sel1_back = sem("sel1_back")
        sel_lo = sem("sel_lo")
        rowmax_clear = sem("rowmax_clear")
        rowmax_made = sem("rowmax_made")
        colmax_made = sem("colmax_made")
        h_neg = sem("h_neg")
        h_made = sem("h_made")
        h_lo = sem("h_lo")
        y_made = sem("y_made")
        y_neg = sem("y_neg")
        y_elu = sem("y_elu")
        x2_made = sem("x2_made")
        xstat_made = sem("xstat_made")
        x2stat_made = sem("x2stat_made")
        x2mv_made = sem("x2mv_made")
        xmv_made = sem("xmv_made")
        xn_made = sem("xn_made")
        xnT_lo = sem("xnT_lo")
        in_made = sem("in_made")
        out_made = sem("out_made")
        bound_step = sem("bound_step")
        sure_made = sem("sure_made")
        flag_made = sem("flag_made")
        GT_turned = sem("GT_turned")
        sel1_done = sem("sel1_done")
        sel_done = sem("sel_done")
        colsum_done = sem("colsum_done")
        h_done = sem("h_done")
        y_done = sem("y_done")
        xn_turned = sem("xn_turned")
        gate_done = sem("gate_done")
        up_done = sem("up_done")
        down_done = sem("down_done")
        sure_counted = sem("sure_counted")

        W1_v = W1.rearrange("h (c p) o -> p c h o", p=P)
        GU_v = gate_up.rearrange("e (k p) d -> e p k d", p=P)
        DN_v = down.rearrange("e (i p) d -> e p i d", p=P)

        def halves(t):
            return t.rearrange("p (c d) -> p c d", c=2)

        fills = []
        fills.append(dict(
            dma=[(stage[:, 0, 0:D].rearrange("p (h o) -> p h o", h=H), W0.rearrange("h f o -> f h o"))],
            raw=stage[:, 0, 0:D], hi=W0p[:, HI, :], lo=W0p[:, LO, :], kind="W0"))
        for j in range(KC // 2):
            s = len(fills) % 4
            fills.append(dict(
                dma=[(stage[:, s, c * D:(c + 1) * D].rearrange("p (h o) -> p h o", h=H), W1_v[:, 2 * j + c])
                     for c in range(2)],
                raw=halves(stage[:, s, :]), hi=W1p[:, 2 * j:2 * j + 2, HI, :], lo=W1p[:, 2 * j:2 * j + 2, LO, :],
                kind="W1"))
        FIRST = len(fills)
        for e in range(E):
            for k in range(KC):
                s = len(fills) % 4
                fills.append(dict(dma=[(stage[:, s, :], GU_v[e, :, k, :])], raw=stage[:, s, :],
                                  hi=GUp[:, k, HI, :], lo=GUp[:, k, LO, :], kind="GU"))
            for j in range(KC // 2):
                s = len(fills) % 4
                fills.append(dict(dma=[(halves(stage[:, s, :]), DN_v[e, :, 2 * j:2 * j + 2, :])],
                                  raw=halves(stage[:, s, :]), hi=DNp[:, 2 * j:2 * j + 2, HI, :],
                                  lo=DNp[:, 2 * j:2 * j + 2, LO, :], kind="DN"))
        PER_E = KC + KC // 2
        slot_total = [0] * 4
        for f, fill in enumerate(fills):
            slot_total[f % 4] += 16 * len(fill["dma"])
            fill["landed"] = slot_total[f % 4]

        def gu_fill(e, k):
            return FIRST + PER_E * e + k

        def dn_fill(e, j):
            return FIRST + PER_E * e + KC + j

        gen_sems = {name: sem("gen_" + name) for name in GENERAL_SIGNALS}
        general = General(nc, gen, gen_sems, bank, dict(
            x=x_rows, ctx=ctx_rows, W0=W0, a_self0=a_self0, a_neigh0=a_neigh0, b0=b0, W1=W1_v, a_self1=a_self1,
            a_neigh1=a_neigh1, b1=b1, gate_up=GU_v, down=DN_v, out=out), (B, N, D, F_IN, H, FO, E, KC, DI))

        def unless_sure(engine, program):
            engine.wait_ge(flag_made, 1)
            engine.wait_ge(out_stored, 16 * B * E)
            n_sure = engine.value_load(flag[0:1, 0:1])
            with engine.If(n_sure < B * N):
                program(engine)

        block = stack.enter_context(nc.Block())

        @block.sync
        def _(sp):
            def load_fill(f):
                if f >= 4:
                    sp.wait_ge(w_lo, f - 3)
                if f in (4, 5, 6):
                    sp.wait_ge(abs_made, {4: 1, 5: 2, 6: 3}[f])
                for dst, src in fills[f]["dma"]:
                    sp.dma_start(dst, src).then_inc(stage_loaded[f % 4], 16)

            sp.dma_start(x_sb[:, 0, :, :], x_rows[0]).then_inc(x_loaded[0], 16)
            sp.dma_start(ctx_sb[:, 0, :, :], ctx_rows[0]).then_inc(ctx_loaded[0], 16)
            for b in range(1, B):
                sp.dma_start(x_sb[:, b, :, :], x_rows[b]).then_inc(x_loaded[b], 16)
                sp.dma_start(ctx_sb[:, b, :, :], ctx_rows[b]).then_inc(ctx_loaded[b], 16)
            for f in range(4):
                load_fill(f)
            sp.dma_start(b0_col[:, :], b0.rearrange("h o -> (h o)").rearrange("(c p) -> p c", p=P),
                         allow_slow_non_contiguous=True).then_inc(small_loaded, 16)
            sp.dma_start(b1_rows[:, :], b1.rearrange("h o -> (h o)").partition_broadcast(P))\
              .then_inc(small_loaded, 16)
            for j, a in enumerate((a_self0, a_neigh0, a_self1, a_neigh1)):
                sp.dma_start(a_abs[:, j, :], a).then_inc(small_loaded, 16)
            for f in range(4, len(fills)):
                load_fill(f)
            sp.wait_ge(out_stored, 16 * B * E)
            unless_sure(sp, general.sync)

        @block.gpsimd
        def _(pool):
            nc.gpsimd.memset(ident[:, :], 0.0).then_inc(consts_made, 1)
            nc.gpsimd.memset(ident_bf[:, :], 0.0).then_inc(consts_made, 1)
            nc.gpsimd.memset(ones[:, :], 1.0).then_inc(consts_made, 1)
            nc.gpsimd.memset(ones_bf[:, :], 1.0).then_inc(consts_made, 1)
            nc.gpsimd.memset(minus_half[:, :], -0.5).then_inc(consts_made, 1)
            pool.wait_ge(consts_made, 5)
            for m in (ident_bf, ident):
                nc.gpsimd.affine_select(out=m[:, :], in_=m[:, :], compare_op=ALU.not_equal, fill=1.0, base=0,
                                        pattern=[[-1, P]], channel_multiplier=1).then_inc(ident_made, 1)

            def w_low(f):
                pool.wait_ge(w_hi, f + 1)
                nc.gpsimd.tensor_tensor(fills[f]["lo"], fills[f]["raw"], fills[f]["hi"].bitcast(F32),
                                        ALU.subtract).then_inc(w_lo, 1)

            def ctx_low(b):
                pool.wait_ge(ctx_hi, b + 1)
                if b >= 2:
                    pool.wait_ge(sel1_done, 2 * (b - 1))
                nc.gpsimd.tensor_tensor(ctxp[:, b % 2, :, LO, :], ctx_sb[:, b, :, :],
                                        ctxp[:, b % 2, :, HI, :].bitcast(F32), ALU.subtract).then_inc(ctx_lo, 1)

            def inverse_std(mv, n, dst, ready, need, turn):
                pool.wait_ge(ready, need)
                nc.gpsimd.tensor_scalar(veps[:, 0:n], mv[:, :, 1], LN_EPS, None, ALU.add).then_inc(veps_made, 1)
                pool.wait_ge(veps_made, turn)
                nc.gpsimd.tensor_tensor(dst[:, :], veps[:, 0:n], minus_half[:, 0:n], ALU.pow)\
                    .then_inc(rstd_made, 1)

            def inner_low(e, c):
                pool.wait_ge(in_hi, KC * e + c + 1)
                nc.gpsimd.tensor_tensor(hTp[:, c, LO, :], val[:, c, :], hTp[:, c, HI, :].bitcast(F32),
                                        ALU.subtract).then_inc(in_lo, 1)

            for b in range(B):
                ctx_low(b)
            for f in range(FIRST + PER_E):
                w_low(f)
            pool.wait_ge(rowmax_made, 4)
            nc.gpsimd.partition_all_reduce(allmax[:, :], rowmax[:, :], P, RMAX).then_inc(allmax_made, 1)
            inverse_std(x2mv, B, rstd, x2mv_made, B, 1)
            for e in range(E):
                if e + 1 < E:
                    inverse_std(x2mv, B, rstd, x2mv_made, B * (e + 2), e + 2)
                for c in range(KC):
                    inner_low(e, c)
                if e + 1 < E:
                    for f in range(gu_fill(e + 1, 0), gu_fill(e + 1, 0) + PER_E):
                        w_low(f)
            inverse_std(xmv, B * E, xrstd, xmv_made, B * E, E + 1)
            unless_sure(pool, general.gpsimd)

        @block.scalar
        def _(act):
            def w_high(f):
                act.wait_ge(stage_loaded[f % 4], fills[f]["landed"])
                if fills[f]["kind"] == "GU":
                    e = (f - FIRST) // PER_E
                    if e == 0:
                        act.wait_ge(sel_done, 2 * B)
                        act.wait_ge(colsum_done, 2)
                    else:
                        act.wait_ge(up_done, KC * e)
                if fills[f]["kind"] == "DN":
                    e = (f - FIRST) // PER_E
                    if e > 0:
                        act.wait_ge(down_done, B * e)
                nc.scalar.copy(fills[f]["hi"], fills[f]["raw"]).then_inc(w_hi, 1)

            def weights_abs():
                for f in range(FIRST):
                    n = 0 if f == 0 else 2 * f - 1
                    dst = absw[:, 0, :] if f == 0 else absw[:, n:n + 2, :]
                    nc.scalar.activation(dst, fills[f]["raw"], ACT.Abs).then_inc(abs_made, 1)

            def ctx_high(b):
                act.wait_ge(ctx_loaded[b], 16)
                if b >= 2:
                    act.wait_ge(sel1_done, 2 * (b - 1))
                nc.scalar.copy(ctxp[:, b % 2, :, HI, :], ctx_sb[:, b, :, :]).then_inc(ctx_hi, 1)

            def turn_even(b):
                for m in (0, 2):
                    act.wait_ge(GT_turned, E * b + m + 1)
                    if b >= 2:
                        act.wait_ge(sel_done, 2 * (b - 1))
                    nc.scalar.copy(GT[:, b % 2, m, :], bank[m][:, 0:N // 2].bitcast(BF16)).then_inc(GT_even, 1)

            def sel1_evac(b):
                act.wait_ge(sel1_done, 2 * b + 1)
                nc.scalar.copy(sel1[:, b % 2, 0:2, :, :].rearrange("p e r f -> p (e r f)"), bank[4][:, :])\
                    .then_inc(sel1_front, 1)

            def sel_evac(b):
                act.wait_ge(sel_done, 2 * b + 1)
                nc.scalar.copy(sel_ctx[:, HI, :, b, :], bank[6][:, :].rearrange("p (e g) -> p e g", e=E))\
                    .then_inc(sel_hi, 1)

            ctx_high(0)
            ctx_high(1)
            for b in range(B):
                turn_even(b)
                if b >= 1:
                    sel_evac(b - 1)
                sel1_evac(b)
                if b < FIRST:
                    w_high(b)
                if b + 2 < B:
                    ctx_high(b + 2)
            sel_evac(B - 1)
            weights_abs()

            def h_exps(e):
                for c in range(KC + 1):
                    if c < KC:
                        n = KC * e + c
                        act.wait_ge(h_done, n + 1)
                        if e == 0 and c == 0:
                            act.wait_ge(small_loaded, 96)
                        if c >= 2:
                            act.wait_ge(h_made, n - 1)
                        elif e == 1:
                            act.wait_ge(y_elu, B * e - 1 + c)
                        elif e >= 2:
                            act.wait_ge(in_made, KC * (e - 1) - 1 + c)
                        nc.scalar.activation(ex[:, c % 2, :], bank[4 + c][:, :], ACT.Exp, bias=b0_col[:, c:c + 1])\
                            .then_inc(h_exp, 1)
                    if c > 0:
                        act.wait_ge(h_made, KC * e + c)
                        nc.scalar.copy(hTp[:, c - 1, HI, :], val[:, c - 1, :]).then_inc(h_hi, 1)

            def y_exps(e):
                for b in range(B):
                    act.wait_ge(y_made, B * e + b + 1)
                    if b >= 2:
                        act.wait_ge(y_elu, B * e + b - 1)
                    else:
                        act.wait_ge(h_made, KC * (e + 1) - 1 + b)
                    nc.scalar.activation(ex[:, b % 2, :], val[:, b, :], ACT.Exp).then_inc(y_exp, 1)

            def turned(e):
                for b in range(B):
                    act.wait_ge(xn_turned, B * e + b + 1)
                    if e > 0:
                        act.wait_ge(up_done, KC * e)
                    nc.scalar.copy(xnT[:, :, HI, b * P:(b + 1) * P],
                                   bank[4 + b][:, :].rearrange("p (k g) -> p k g", k=KC)).then_inc(xnT_hi, 1)

            def silus(e):
                for c in range(KC + 1):
                    if c < KC:
                        n = KC * e + c
                        act.wait_ge(gate_done, n + 1)
                        if c >= 2 or e == E - 1:
                            act.wait_ge(in_made, n - 1)
                        else:
                            act.wait_ge(y_elu, B * (e + 2) - 1 + c)
                        nc.scalar.activation(ex[:, c % 2, :], bank[4 + 2 * (c % 2)][:, :], ACT.Silu)\
                            .then_inc(silu_made, 1)
                    if c > 0:
                        act.wait_ge(in_made, KC * e + c)
                        nc.scalar.copy(hTp[:, c - 1, HI, :], val[:, c - 1, :]).then_inc(in_hi, 1)

            def store(e):
                for b in range(B):
                    act.wait_ge(out_made, B * e + b + 1)
                    act.dma_start(out_rows[b, e], x_sb[:, b, e, :]).then_inc(out_stored, 16)

            h_exps(0)
            y_exps(0)
            for f in range(FIRST, FIRST + PER_E):
                w_high(f)
            h_exps(1)
            y_exps(1)
            turned(0)
            for e in range(E):
                silus(e)
                if e + 1 < E:
                    turned(e + 1)
                    for k in range(KC):
                        w_high(gu_fill(e + 1, k))
                    for j in range(KC // 2):
                        w_high(dn_fill(e + 1, j))
                store(e)
                if e + 2 < E:
                    h_exps(e + 2)
                    y_exps(e + 2)
            unless_sure(act, general.scalar)

        @block.vector
        def _(dve):
            nc.vector.memset(rowmax[:, :], 0.0).then_inc(rowmax_clear, 1)

            def select(b):
                dve.wait_ge(x_loaded[b], 16)
                for e in range(E):
                    nc.vector.max(top8[:, b, e, :], x_sb[:, b, e, :]).then_inc(top_found, 1)
                for e in range(E):
                    dve.wait_ge(top_found, E * b + e + 1)
                    if b >= 2 and e == 0:
                        dve.wait_ge(GT_turned, E * (b - 1))
                    nc.vector.tensor_scalar(G[:, b % 2, e, :], x_sb[:, b, e, :], top8[:, b, e, 0:1], None,
                                            ALU.is_equal).then_inc(G_made, 1)

            def turn_odd(b):
                for m in (1, 3):
                    dve.wait_ge(GT_turned, E * b + m + 1)
                    if b >= 2:
                        dve.wait_ge(sel_done, 2 * (b - 1))
                    nc.vector.tensor_copy(GT[:, b % 2, m, :], bank[m][:, 0:N // 2].bitcast(BF16))\
                        .then_inc(GT_odd, 1)

            def sel1_evac(b):
                dve.wait_ge(sel1_done, 2 * b + 2)
                nc.vector.tensor_copy(sel1[:, b % 2, 2:4, :, :].rearrange("p e r f -> p (e r f)"), bank[5][:, :])\
                    .then_inc(sel1_back, 1)

            def sel_evac(b):
                dve.wait_ge(sel_done, 2 * b + 2)
                nc.vector.tensor_copy(sel_ctx[:, LO, :, b, :], bank[7][:, :].rearrange("p (e g) -> p e g", e=E))\
                    .then_inc(sel_lo, 1)

            select(0)
            for b in range(B):
                if b + 1 < B:
                    select(b + 1)
                turn_odd(b)
                if b >= 1:
                    sel_evac(b - 1)
                sel1_evac(b)
            sel_evac(B - 1)

            def magnitudes():
                for b in range(B):
                    dve.wait_ge(ctx_loaded[b], 16)
                dve.wait_ge(small_loaded, 96)
                dve.wait_ge(rowmax_clear, 1)
                nc.vector.tensor_reduce(rowmax[:, 0:1], ctx_xn[:, :, :], AX.XY, ALU.max,
                                        apply_absolute_value=True).then_inc(rowmax_made, 1)
                for layer in range(2):
                    nc.vector.tensor_reduce(rowmax[0:H, 1 + layer:2 + layer], a_abs[:, 2 * layer:2 * layer + 2, :],
                                            AX.XY, ALU.add, apply_absolute_value=True).then_inc(rowmax_made, 1)
                nc.vector.tensor_reduce(rowmax[:, 3:4], b0_col[:, :], AX.X, ALU.max,
                                        apply_absolute_value=True).then_inc(rowmax_made, 1)
                for j in range(2):
                    dve.wait_ge(colsum_done, j + 1)
                    nc.vector.tensor_reduce(colmax[:, j:j + 1], bank[2 + j][:, :], AX.X, ALU.max)\
                        .then_inc(colmax_made, 1)

            def h_values(e):
                for c in range(KC + 1):
                    if c < KC:
                        n = KC * e + c
                        dve.wait_ge(h_exp, n + 1)
                        nc.vector.tensor_scalar(ex[:, c % 2, :], ex[:, c % 2, :], 1.0, -1.0, ALU.min, ALU.add)\
                            .then_inc(h_neg, 1)
                        dve.wait_ge(h_neg, n + 1)
                        if e > 0 and c == 0:
                            dve.wait_ge(x2_made, B * e)
                        if e >= 2:
                            dve.wait_ge(in_lo, KC * (e - 2) + c + 1)
                        nc.vector.scalar_tensor_tensor(val[:, c, :], bank[4 + c][:, :], b0_col[:, c:c + 1],
                                                       ex[:, c % 2, :], ALU.add, ALU.max).then_inc(h_made, 1)
                    if c > 0:
                        dve.wait_ge(h_hi, KC * e + c)
                        nc.vector.tensor_tensor(hTp[:, c - 1, LO, :], val[:, c - 1, :],
                                                hTp[:, c - 1, HI, :].bitcast(F32), ALU.subtract).then_inc(h_lo, 1)

            def y_values(e):
                for b in range(B):
                    dve.wait_ge(y_done, B * e + b + 1)
                    dve.wait_ge(h_lo, KC * e + KC)
                    nc.vector.tensor_tensor(val[:, b, :], bank[b][:, :], b1_rows[:, :], ALU.add).then_inc(y_made, 1)
                    nc.vector.bn_stats(xstat[:, b, e, :], x_sb[:, b, e, :]).then_inc(xstat_made, 1)
                for b in range(B):
                    n = B * e + b
                    dve.wait_ge(y_exp, n + 1)
                    nc.vector.tensor_scalar(ex[:, b % 2, :], ex[:, b % 2, :], 1.0, -1.0, ALU.min, ALU.add)\
                        .then_inc(y_neg, 1)
                    dve.wait_ge(y_neg, n + 1)
                    nc.vector.tensor_tensor(val[:, b, :], val[:, b, :], ex[:, b % 2, :], ALU.max)\
                        .then_inc(y_elu, 1)
                    dve.wait_ge(y_elu, n + 1)
                    dve.wait_ge(xstat_made, n + 1)
                    nc.vector.tensor_tensor(x_sb[:, b, e, :], x_sb[:, b, e, :], val[:, b, :], ALU.add)\
                        .then_inc(x2_made, 1)
                    dve.wait_ge(x2_made, n + 1)
                    nc.vector.bn_stats(x2stat[:, b, :], x_sb[:, b, e, :]).then_inc(x2stat_made, 1)
                    dve.wait_ge(x2stat_made, n + 1)
                    if e > 0 and b == 0:
                        dve.wait_ge(rstd_made, e)
                        dve.wait_ge(xn_made, B * e)
                    nc.vector.bn_aggr(x2mv[:, b, :], x2stat[:, b, :]).then_inc(x2mv_made, 1)

            def normalize(e):
                dve.wait_ge(rstd_made, e + 1)
                dve.wait_ge(x2mv_made, B * (e + 1))
                for b in range(B):
                    if e > 0:
                        dve.wait_ge(xn_turned, B * (e - 1) + b + 1)
                    elif b == 0:
                        dve.wait_ge(rowmax_made, 1)
                    nc.vector.tensor_scalar(xn[:, b, :], x_sb[:, b, e, :], x2mv[:, b, 0:1], rstd[:, b:b + 1],
                                            ALU.subtract, ALU.mult).then_inc(xn_made, 1)

            def turned_low(e):
                for b in range(B):
                    dve.wait_ge(xnT_hi, B * e + b + 1)
                    nc.vector.tensor_tensor(xnT[:, :, LO, b * P:(b + 1) * P],
                                            bank[4 + b][:, :].rearrange("p (k g) -> p k g", k=KC),
                                            xnT[:, :, HI, b * P:(b + 1) * P].bitcast(F32), ALU.subtract)\
                        .then_inc(xnT_lo, 1)

            def inner(e):
                for c in range(KC):
                    n = KC * e + c
                    dve.wait_ge(silu_made, n + 1)
                    dve.wait_ge(up_done, n + 1)
                    if e == E - 1:
                        dve.wait_ge(in_lo, n - KC + 1)
                    nc.vector.tensor_tensor(val[:, c, :], bank[5 + 2 * (c % 2)][:, :], ex[:, c % 2, :], ALU.mult)\
                        .then_inc(in_made, 1)

            def outputs(e):
                for b in range(B):
                    n = B * e + b
                    dve.wait_ge(down_done, n + 1)
                    dve.wait_ge(xn_made, n + 1)
                    nc.vector.tensor_tensor(x_sb[:, b, e, :], x_sb[:, b, e, :], bank[b][:, :], ALU.add)\
                        .then_inc(out_made, 1)

            h_values(0)
            magnitudes()
            y_values(0)
            normalize(0)
            h_values(1)
            y_values(1)
            turned_low(0)
            normalize(1)
            for e in range(E):
                inner(e)
                if e + 1 < E:
                    turned_low(e + 1)
                outputs(e)
                if e + 2 < E:
                    h_values(e + 2)
                    y_values(e + 2)
                    normalize(e + 2)

            steps = [0]

            def step(ins):
                steps[0] += 1
                ins.then_inc(bound_step, 1)
                dve.wait_ge(bound_step, steps[0])

            for t in range(B * E):
                nc.vector.bn_aggr(xmv[:, t, :], xstat[:, t // E, t % E, :]).then_inc(xmv_made, 1)
            dve.wait_ge(allmax_made, 1)
            dve.wait_ge(colmax_made, 2)
            step(nc.vector.tensor_tensor(bound[:, 0:1], allmax[:, 0:1], colmax[:, 0:1], ALU.mult))
            step(nc.vector.tensor_tensor(bound[:, 1:2], bound[:, 0:1], allmax[:, 1:2], ALU.mult))
            step(nc.vector.scalar_tensor_tensor(bound[:, 2:3], bound[:, 0:1], 1.0, allmax[:, 3:4], ALU.add, ALU.add))
            step(nc.vector.tensor_tensor(bound[:, 3:4], bound[:, 2:3], colmax[:, 1:2], ALU.mult))
            step(nc.vector.tensor_tensor(bound[:, 4:5], bound[:, 3:4], allmax[:, 2:3], ALU.mult))
            step(nc.vector.tensor_tensor(bound[:, 5:6], bound[:, 1:2], bound[:, 4:5], ALU.add))
            step(nc.vector.tensor_scalar(bound[:, 5:6], bound[:, 5:6], 2.1, UNDERFLOW, ALU.mult, ALU.add))
            tops = top8[:, :, :, :].rearrange("p b e t -> p (b e) t")
            step(nc.vector.tensor_tensor(gap[:, :], tops[:, :, 0], tops[:, :, 1], ALU.subtract))
            step(nc.vector.tensor_tensor(lead[:, :], tops[:, :, 0], xmv[:, :, 0], ALU.subtract))
            dve.wait_ge(rstd_made, E + 1)
            step(nc.vector.scalar_tensor_tensor(gap[:, :], gap[:, :], MASK, xrstd[:, :], ALU.mult, ALU.mult))
            step(nc.vector.tensor_tensor(lead[:, :], lead[:, :], xrstd[:, :], ALU.mult))
            step(nc.vector.tensor_scalar(lead[:, :], lead[:, :], 1.0, MASK * ROUNDINGS, ALU.add, ALU.mult))
            step(nc.vector.scalar_tensor_tensor(sure[:, :], lead[:, :], bound[:, 5:6], gap[:, :], ALU.add, ALU.is_lt))
            nc.vector.tensor_reduce(sure_n[:, :], sure[:, :], AX.X, ALU.add).then_inc(sure_made, 1)
            dve.wait_ge(sure_counted, 1)
            nc.vector.tensor_copy(flag[:, :], bank[4][0:1, 0:1]).then_inc(flag_made, 1)
            unless_sure(dve, general.vector)

        @block.tensor
        def _(pe):
            def turn(b):
                for m in range(E):
                    if b > 0:
                        if m % 2 == 0:
                            pe.wait_ge(GT_even, 2 * (b - 1) + m // 2 + 1)
                        else:
                            pe.wait_ge(GT_odd, 2 * (b - 1) + m // 2 + 1)
                    for e in range(E):
                        if m == 0:
                            pe.wait_ge(G_made, E * b + e + 1)
                        last = nc.tensor.transpose(bank[m][:, 0:N // 2].bitcast(BF16)[:, e * P:(e + 1) * P],
                                                   G[:, b % 2, e, m::E], ident_bf[:, :])
                    last.then_inc(GT_turned, 1)

            def select1(b):
                pe.wait_ge(ctx_lo, b + 1)
                pe.wait_ge(GT_even, 2 * b + 2)
                pe.wait_ge(GT_odd, 2 * b + 2)
                if b > 0:
                    pe.wait_ge(sel1_front, b)
                    pe.wait_ge(sel1_back, b)
                for e in range(E):
                    dst = bank[4 + e // 2][:, (e % 2) * 2 * F_IN:(e % 2 + 1) * 2 * F_IN]
                    for k in range(E):
                        last = nc.tensor.matmul(dst, GT[:, b % 2, k, e * P:(e + 1) * P],
                                                ctxp[:, b % 2, k, :, :].rearrange("p r f -> p (r f)"),
                                                start=(k == 0), stop=(k == E - 1))
                    if e % 2:
                        last.then_inc(sel1_done, 1)

            def select2(b):
                pe.wait_ge(sel1_front, b + 1)
                pe.wait_ge(sel1_back, b + 1)
                if b > 0:
                    pe.wait_ge(sel_hi, b)
                    pe.wait_ge(sel_lo, b)
                for part in (HI, LO):
                    for k in range(E):
                        last = nc.tensor.matmul(bank[6 + part][:, :], sel1[:, b % 2, k, part, :], GT[:, b % 2, k, :],
                                                start=(k == 0), stop=(k == E - 1))
                    last.then_inc(sel_done, 1)

            def column_sums():
                pe.wait_ge(abs_made, 3)
                pe.wait_ge(GT_even, 2 * B)
                pe.wait_ge(GT_odd, 2 * B)
                nc.tensor.matmul(bank[2][:, :], ones_bf[:, :], absw[:, 0, :], start=True, stop=True)\
                    .then_inc(colsum_done, 1)
                for c in range(KC):
                    last = nc.tensor.matmul(bank[3][:, :], ones_bf[:, :], absw[:, 1 + c, :],
                                            start=(c == 0), stop=(c == KC - 1))
                last.then_inc(colsum_done, 1)

            pe.wait_ge(ident_made, 2)
            for b in range(B):
                turn(b)
                if b >= 1:
                    select2(b - 1)
                select1(b)
            select2(B - 1)
            column_sums()

            def layer0(e):
                if e == 0:
                    pe.wait_ge(sel_hi, B)
                    pe.wait_ge(sel_lo, B)
                    pe.wait_ge(w_lo, 1)
                elif e == 1:
                    pe.wait_ge(h_made, KC)
                else:
                    pe.wait_ge(xnT_lo, B * e)
                for c in range(KC):
                    for j, (w, v) in enumerate(TERMS):
                        last = nc.tensor.matmul(bank[4 + c][:, :], W0p[:, w, c * P:(c + 1) * P],
                                                sel_ctx[:, v, e, :, :].rearrange("p b g -> p (b g)"),
                                                start=(j == 0), stop=(j == 2))
                    last.then_inc(h_done, 1)

            def layer1(e):
                if e == 0:
                    pe.wait_ge(w_lo, FIRST)
                    pe.wait_ge(colmax_made, 2)
                for c in range(KC):
                    pe.wait_ge(h_lo, KC * e + c + 1)
                    for b in range(B):
                        if c == 0 and e == 1:
                            pe.wait_ge(y_made, B * (e - 1) + b + 1)
                        if c == 0 and e >= 2:
                            pe.wait_ge(out_made, B * (e - 2) + b + 1)
                        for j, (w, v) in enumerate(TERMS):
                            last = nc.tensor.matmul(bank[b][:, :], hTp[:, c, w, b * P:(b + 1) * P], W1p[:, c, v, :],
                                                    start=(c == 0 and j == 0), stop=(c == KC - 1 and j == 2))
                        if c == KC - 1:
                            last.then_inc(y_done, 1)

            def turn_xn(e):
                if e == 0:
                    pe.wait_ge(h_made, 2 * KC)
                else:
                    pe.wait_ge(in_made, KC * e)
                for b in range(B):
                    pe.wait_ge(xn_made, B * e + b + 1)
                    for k in range(KC):
                        last = nc.tensor.transpose(bank[4 + b][:, k * P:(k + 1) * P], xn[:, b, k * P:(k + 1) * P],
                                                   ident[:, :])
                    last.then_inc(xn_turned, 1)

            def gate_and_up(e):
                for c in range(KC):
                    if c == 0:
                        pe.wait_ge(xnT_lo, B * (e + 1))
                        if e + 1 < E and e > 0:
                            pe.wait_ge(h_made, KC * (e + 2))
                    if c >= 2:
                        pe.wait_ge(in_made, KC * e + c - 1)
                    for half, done in ((0, gate_done), (1, up_done)):
                        col = half * DI + c * P
                        for k in range(KC):
                            if c == 0 and half == 0:
                                pe.wait_ge(w_lo, gu_fill(e, k) + 1)
                            for j, (w, v) in enumerate(TERMS):
                                last = nc.tensor.matmul(bank[4 + 2 * (c % 2) + half][:, :],
                                                        GUp[:, k, w, col:col + P], xnT[:, k, v, :],
                                                        start=(k == 0 and j == 0), stop=(k == KC - 1 and j == 2))
                        last.then_inc(done, 1)

            def project_down(e):
                pe.wait_ge(w_lo, dn_fill(e, KC // 2 - 1) + 1)
                for b in range(B):
                    pe.wait_ge(y_made, B * min(e + 1, E - 1) + b + 1)
                for i in range(KC):
                    pe.wait_ge(in_lo, KC * e + i + 1)
                    for b in range(B):
                        if e == E - 1 and i == 0:
                            pe.wait_ge(out_made, B * (e - 1) + b + 1)
                        for j, (w, v) in enumerate(TERMS):
                            last = nc.tensor.matmul(bank[b][:, :], hTp[:, i, w, b * P:(b + 1) * P], DNp[:, i, v, :],
                                                    start=(i == 0 and j == 0), stop=(i == KC - 1 and j == 2))
                        if i == KC - 1:
                            last.then_inc(down_done, 1)

            layer0(0)
            layer1(0)
            layer0(1)
            layer1(1)
            turn_xn(0)
            for e in range(E):
                gate_and_up(e)
                if e + 1 < E:
                    turn_xn(e + 1)
                project_down(e)
                if e + 2 < E:
                    layer0(e + 2)
                    layer1(e + 2)

            pe.wait_ge(sure_made, 1)
            nc.tensor.matmul(bank[4][0:1, 0:1], sure_n[:, 0:1], ones[:, 0:1], start=True, stop=True)\
                .then_inc(sure_counted, 1)
            unless_sure(pe, general.tensor)


_INS = ['x', 'ctx_512', 'L0_xattn_W0', 'L0_xattn_a_self0', 'L0_xattn_a_neigh0', 'L0_xattn_b0', 'L0_xattn_W1',
        'L0_xattn_a_self1', 'L0_xattn_a_neigh1', 'L0_xattn_b1', 'L0_ffn_gate_up_proj', 'L0_ffn_down_proj']


def kernel(**inputs):
    import numpy as _np
    import concourse.bacc as _bacc
    from concourse import mybir as _mybir
    from concourse.bass_utils import run_bass_kernel_spmd as _run

    nc = _bacc.Bacc("TRN2", target_bir_lowering=False, num_devices=1)
    arrays, args = {}, []
    for name in _INS:
        a = _np.ascontiguousarray(inputs[name])
        arrays[f"in_{name}"] = a
        args.append(nc.dram_tensor(f"in_{name}", a.shape, _mybir.dt.from_np(a.dtype), kind="ExternalInput").ap())
    shape = inputs['x'].shape
    args.append(nc.dram_tensor("out_0", shape, _mybir.dt.float32, kind="ExternalOutput").ap())
    build(nc, *args)
    r = _run(nc, [arrays], core_ids=[0])
    return r.results[0]["out_0"]
```

```python
from contextlib import ExitStack

import concourse.bass as bass
from concourse import mybir

F32 = mybir.dt.float32
F32R = mybir.dt.float32r
BF16 = mybir.dt.bfloat16
I32 = mybir.dt.int32
ALU = mybir.AluOpType
ACT = mybir.ActivationFunctionType
AX = mybir.AxisListType
RMAX = bass.bass_isa.ReduceOp.max

P = 128
RING = 6
HI, LO = 0, 1
TERMS = ((HI, HI), (HI, LO), (LO, HI))
LN_EPS = 1e-5
MASK = 1e10
ROUNDINGS = 2.0 ** -20
UNDERFLOW = 110.0


GENERAL_SIGNALS = (
    "x_loaded", "layer_loaded", "x2_stored", "ffn_loaded", "out_stored",
    "consts", "ident", "veps", "rstd",
    "feat_made", "z_made", "prob_made", "probT_made", "att_exp", "silu_made",
    "stat", "mv", "adj", "one_minus", "mask", "inT_made", "prod", "score", "diag", "leaky", "logit",
    "neg_max", "inverse", "att", "att_neg", "elu", "x2", "xn", "inner", "out",
    "dve_waited", "pool_waited", "pe_waited", "sp_waited",
    "turned", "feat", "spread", "prob_turned", "att_done", "gate", "up", "down",
)


class General:

    def __init__(self, nc, gen, sems, bank, dram, sizes):
        self.nc, self.t, self.s, self.bank, self.dram = nc, gen, sems, bank, dram
        self.B, self.N, self.D, self.F_IN, self.H, self.FO, self.E, self.KC, self.DI = sizes
        self.loads = (4, self.KC + 3)

    def layer_no(self, b, layer):
        return b * 2 + layer

    def head_no(self, b, layer, h):
        return b * (2 * self.H) + h + layer * self.H

    def unit(self, b, layer, h, e):
        return b * (2 * self.H * self.E) + h * self.E + (layer * self.H * self.E + e)

    def chunk_no(self, b, layer, c):
        return b * (1 + self.KC) + layer + c

    def sync(self, sp):
        t, s, d, B, E, KC, H = self.t, self.s, self.dram, self.B, self.E, self.KC, self.H
        flat = lambda v: v.rearrange("h o -> (h o)").partition_broadcast(P)
        heads = lambda v: v.rearrange("p (h o) -> p h o", h=H)
        for name in GENERAL_SIGNALS:
            sp.sem_inc(s[name], 1)
        with sp.Fori(0, B) as b:
            sp.wait_ge(s["x2_stored"], 1 + b * 16)
            sp.sem_inc(s["sp_waited"], 1)
            sp.wait_ge(s["turned"], 1 + b * (1 + KC))
            sp.dma_start(t["x"][:, :, :], d["x"][b]).then_inc(s["x_loaded"], 16)
            sp.dma_start(t["ctx"][:, :, :], d["ctx"][b]).then_inc(s["x_loaded"], 16)
            for layer in range(2):
                sp.wait_ge(s["att"], 1 + self.unit(b, layer, 0, 0))
                if layer == 0:
                    sp.dma_start(heads(t["W"][:, 0, :]), d["W0"].rearrange("h f o -> f h o"))\
                        .then_inc(s["layer_loaded"], 16)
                else:
                    for c in range(KC):
                        sp.dma_start(heads(t["W"][:, c, :]), d["W1"][:, c]).then_inc(s["layer_loaded"], 16)
                for j, name in enumerate(("a_self", "a_neigh")):
                    sp.dma_start(t["a"][:, j, :], flat(d[f"{name}{layer}"])).then_inc(s["layer_loaded"], 16)
                sp.dma_start(t["bias"][:, :], flat(d[f"b{layer}"])).then_inc(s["layer_loaded"], 16)
            sp.wait_ge(s["x2"], 1 + b + 1)
            sp.dma_start(d["out"].rearrange("b (g e) d -> b g e d", e=E)[b], t["x"][:, :, :])\
                .then_inc(s["x2_stored"], 16)
        sp.wait_ge(s["x2_stored"], 1 + 16 * B)
        rows = d["out"].rearrange("b (g e) d -> e g b d", e=E)
        with sp.Fori(0, E) as e:
            sp.wait_ge(s["out_stored"], 1 + e * 16)
            sp.sem_inc(s["sp_waited"], 1)
            sp.wait_ge(s["down"], 1 + e * B)
            sp.sem_inc(s["sp_waited"], 1)
            sp.dma_start(t["x"][:, :, :], rows[e]).then_inc(s["ffn_loaded"], 16)
            sp.dma_start(t["gate_up"][:, :, :], d["gate_up"][e]).then_inc(s["ffn_loaded"], 16)
            sp.dma_start(t["down"][:, :, :], d["down"][e]).then_inc(s["ffn_loaded"], 16)
            sp.wait_ge(s["out"], 1 + e * B + B)
            sp.sem_inc(s["sp_waited"], 1)
            sp.dma_start(rows[e], t["x"][:, :, :]).then_inc(s["out_stored"], 16)
        sp.wait_ge(s["out_stored"], 1 + 16 * E)

    def gpsimd(self, pool):
        t, s, B, E, nc = self.t, self.s, self.B, self.E, self.nc
        nc.gpsimd.memset(t["ones"][:, :], 1.0).then_inc(s["consts"], 1)
        nc.gpsimd.memset(t["ident"][:, :], 0.0).then_inc(s["consts"], 1)
        nc.gpsimd.memset(t["power"][:, :], -0.5).then_inc(s["consts"], 1)
        pool.wait_ge(s["consts"], 1 + 3)
        nc.gpsimd.affine_select(out=t["ident"][:, :], in_=t["ident"][:, :], compare_op=ALU.not_equal, fill=1.0,
                                base=0, pattern=[[-1, P]], channel_multiplier=1).then_inc(s["ident"], 1)
        with pool.Fori(0, B + E) as i:
            pool.wait_ge(s["mv"], 1 + i * 4 + 4)
            pool.sem_inc(s["pool_waited"], 1)
            nc.gpsimd.tensor_scalar(t["veps"][:, :], t["mv"][:, :, 1], LN_EPS, None, ALU.add)\
                .then_inc(s["veps"], 1)
            pool.wait_ge(s["veps"], 1 + i + 1)
            nc.gpsimd.tensor_tensor(t["rstd"][:, :], t["veps"][:, :], t["power"][:, :], ALU.pow)\
                .then_inc(s["rstd"], 1)

    def scalar(self, act):
        t, s, B, E, KC, H, nc, bank = self.t, self.s, self.B, self.E, self.KC, self.H, self.nc, self.bank
        with act.Fori(0, B) as b:
            for layer in range(2):
                for m in range(E):
                    n = self.layer_no(b, layer) * E + m
                    act.wait_ge(s["feat"], 1 + n + 1)
                    if m == 0:
                        act.wait_ge(s["att"], 1 + self.unit(b, layer, 0, 0))
                    nc.scalar.copy(t["feat"][:, m, :], bank[1][:, :]).then_inc(s["feat_made"], 1)
                with act.Fori(0, H) as h:
                    act.wait_ge(s["spread"], 1 + self.head_no(b, layer, h) + 1)
                    act.wait_ge(s["score"], 1 + self.layer_no(b, layer) * (2 * E) + 2 * E)
                    for e in range(E):
                        u = self.unit(b, layer, h, e)
                        act.wait_ge(s["leaky"], 1 + u)
                        nc.scalar.activation(t["z"][:, :], bank[2][:, :], ACT.Identity,
                                             bias=t["score"][:, 0, e, bass.ds(h, 1)]).then_inc(s["z_made"], 1)
                        act.wait_ge(s["neg_max"], 1 + u + 1)
                        act.wait_ge(s["prob_turned"], 1 + u)
                        act.wait_ge(s["inverse"], 1 + u)
                        nc.scalar.activation(t["prob"][:, :], t["logit"][:, :], ACT.Exp, bias=t["row"][:, 1:2],
                                             accum_out=t["row"][:, 2:3]).then_inc(s["prob_made"], 1)
                        act.wait_ge(s["prob_turned"], 1 + u + 1)
                        nc.scalar.copy(t["probT"][:, :, :].rearrange("p m g -> p (m g)"), bank[3][:, :])\
                            .then_inc(s["probT_made"], 1)
                act.wait_ge(s["att"], 1 + self.unit(b, layer, 0, 0) + H * E)
                act.wait_ge(s["elu"], 1 + self.layer_no(b, layer))
                nc.scalar.activation(t["exp"][:, :, :], t["att"][:, :, :], ACT.Exp).then_inc(s["att_exp"], 1)
        with act.Fori(0, E) as e:
            for c in range(KC):
                act.wait_ge(s["gate"], 1 + e * KC + (c + 1))
                act.wait_ge(s["inner"], 1 + e * KC + c)
                nc.scalar.activation(t["silu"][:, :], bank[1][:, :], ACT.Silu).then_inc(s["silu_made"], 1)

    def normalize(self, dve, i, load, loaded, free, dst):
        t, s, nc = self.t, self.s, self.nc
        dve.wait_ge(load, 1 + loaded)
        for e in range(self.E):
            nc.vector.bn_stats(t["stat"][:, e, :], t["x"][:, e, :]).then_inc(s["stat"], 1)
        dve.wait_ge(s["rstd"], 1 + i)
        dve.wait_ge(s["stat"], 1 + i * 4 + 4)
        dve.sem_inc(s["dve_waited"], 1)
        for e in range(self.E):
            nc.vector.bn_aggr(t["mv"][:, e, :], t["stat"][:, e, :]).then_inc(s["mv"], 1)
        dve.wait_ge(s["rstd"], 1 + i + 1)
        dve.wait_ge(s["mv"], 1 + i * 4 + 4)
        free()
        for e in range(self.E):
            src, to, signal = dst(e)
            nc.vector.tensor_scalar(to, src, t["mv"][:, e, 0:1], t["rstd"][:, e:e + 1], ALU.subtract, ALU.mult)\
                .then_inc(signal, 1)

    def vector(self, dve):
        t, s, B, E, KC, H, FO = self.t, self.s, self.B, self.E, self.KC, self.H, self.FO
        nc, bank, unit = self.nc, self.bank, self.unit
        every = lambda v: v.rearrange("p e d -> p (e d)")
        mask = t["mask"][:, :, :, :].rearrange("p e r g -> p (e r g)")
        dve.wait_ge(s["ident"], 1 + 1)
        with dve.Fori(0, B) as b:
            def adj(e):
                return (t["x"][:, e, :].rearrange("p (g r) -> p g r", r=E),
                        t["mask"][:, e, :, :].rearrange("p r g -> p g r"), s["adj"])

            self.normalize(dve, b, s["x_loaded"], b * 32 + 32, lambda: None, adj)
            dve.wait_ge(s["adj"], 1 + b * E + E)
            nc.vector.tensor_scalar(mask, mask, -1.0, 1.0, ALU.mult, ALU.add).then_inc(s["one_minus"], 1)
            dve.wait_ge(s["one_minus"], 1 + b + 1)
            nc.vector.tensor_scalar(mask, mask, -MASK, None, ALU.mult).then_inc(s["mask"], 1)
            dve.wait_ge(s["mask"], 1 + b + 1)
            for layer in range(2):
                for c in range(1 if layer == 0 else KC):
                    n = self.chunk_no(b, layer, c)
                    dve.wait_ge(s["turned"], 1 + n + 1)
                    nc.vector.tensor_copy(t["inT"][:, c, :], bank[0][:, :]).then_inc(s["inT_made"], 1)
                for m in range(E):
                    dve.wait_ge(s["feat_made"], 1 + self.layer_no(b, layer) * E + (m + 1))
                    for j in range(2):
                        n = self.layer_no(b, layer) * (2 * E) + (2 * m + j)
                        dve.wait_ge(s["score"], 1 + n)
                        nc.vector.tensor_tensor(t["prod"][:, :], t["feat"][:, m, :], t["a"][:, j, :], ALU.mult)\
                            .then_inc(s["prod"], 1)
                        dve.wait_ge(s["prod"], 1 + n + 1)
                        nc.vector.tensor_reduce(t["score"][:, j, m, :],
                                                t["prod"][:, :].rearrange("p (h o) -> p h o", h=H), AX.X, ALU.add)\
                            .then_inc(s["score"], 1)
                dve.wait_ge(s["score"], 1 + self.layer_no(b, layer) * (2 * E) + 2 * E)
                dve.sem_inc(s["dve_waited"], 1)
                with dve.Fori(0, H) as h:
                    dve.wait_ge(s["spread"], 1 + self.head_no(b, layer, h))
                    for m in range(E):
                        nc.vector.tensor_scalar(t["diag"][:, m, :], t["ident"][:, :],
                                                t["score"][:, 1, m, bass.ds(h, 1)], None, ALU.mult)\
                            .then_inc(s["diag"], 1)
                    for e in range(E):
                        u = unit(b, layer, h, e)
                        dve.wait_ge(s["z_made"], 1 + u + 1)
                        nc.vector.scalar_tensor_tensor(t["leaky"][:, :], t["z"][:, :], 0.2, t["z"][:, :],
                                                       ALU.mult, ALU.max).then_inc(s["leaky"], 1)
                        dve.wait_ge(s["leaky"], 1 + u + 1)
                        dve.wait_ge(s["prob_made"], 1 + u)
                        dve.sem_inc(s["dve_waited"], 1)
                        nc.vector.tensor_tensor_reduce(
                            t["logit"][:, :], t["leaky"][:, :],
                            t["mask"][:, e, :, :].rearrange("p r g -> p (r g)"), 1.0, -3e38, ALU.add, ALU.max,
                            t["row"][:, 0:1]).then_inc(s["logit"], 1)
                        dve.wait_ge(s["logit"], 1 + u + 1)
                        nc.vector.tensor_scalar(t["row"][:, 1:2], t["row"][:, 0:1], -1.0, None, ALU.mult)\
                            .then_inc(s["neg_max"], 1)
                        dve.wait_ge(s["prob_made"], 1 + u + 1)
                        nc.vector.reciprocal(t["row"][:, 3:4], t["row"][:, 2:3]).then_inc(s["inverse"], 1)
                        dve.wait_ge(s["inverse"], 1 + u + 1)
                        dve.wait_ge(s["att_done"], 1 + u + 1)
                        cols = bass.ds(h * FO, FO)
                        nc.vector.scalar_tensor_tensor(t["att"][:, e, cols], bank[4][:, 0:FO], t["row"][:, 3:4],
                                                       t["bias"][:, cols], ALU.mult, ALU.add).then_inc(s["att"], 1)
                n = self.layer_no(b, layer)
                dve.wait_ge(s["att_exp"], 1 + n + 1)
                nc.vector.tensor_scalar(every(t["exp"]), every(t["exp"]), 1.0, -1.0, ALU.min, ALU.add)\
                    .then_inc(s["att_neg"], 1)
                dve.wait_ge(s["att_neg"], 1 + n + 1)
                dve.wait_ge(s["att"], 1 + unit(b, layer, 0, 0) + H * E)
                nc.vector.tensor_tensor(every(t["att"]), every(t["att"]), every(t["exp"]), ALU.max)\
                    .then_inc(s["elu"], 1)
            dve.wait_ge(s["elu"], 1 + b * 2 + 2)
            nc.vector.tensor_tensor(every(t["x"]), every(t["x"]), every(t["att"]), ALU.add).then_inc(s["x2"], 1)
        with dve.Fori(0, E) as g:
            def free():
                dve.wait_ge(s["turned"], 1 + g * KC + B * (1 + KC))

            self.normalize(dve, g + B, s["ffn_loaded"], g * 48 + 48, free,
                           lambda b: (t["x"][:, b, :], t["xn"][:, b, :], s["xn"]))
            for k in range(KC):
                n = g * KC + (B * (1 + KC) + k)
                dve.wait_ge(s["turned"], 1 + n + 1)
                nc.vector.tensor_copy(t["inT"][:, k, :], bank[0][:, :]).then_inc(s["inT_made"], 1)
            for c in range(KC):
                dve.wait_ge(s["silu_made"], 1 + g * KC + (c + 1))
                dve.wait_ge(s["up"], 1 + g * KC + (c + 1))
                nc.vector.tensor_tensor(t["inner"][:, c, :], bank[2][:, :], t["silu"][:, :], ALU.mult)\
                    .then_inc(s["inner"], 1)
            for b in range(B):
                dve.wait_ge(s["down"], 1 + g * B + (b + 1))
                nc.vector.tensor_tensor(t["x"][:, b, :], t["x"][:, b, :], bank[3][:, :], ALU.add)\
                    .then_inc(s["out"], 1)

    def tensor(self, pe):
        t, s, B, E, KC, H, FO, DI = self.t, self.s, self.B, self.E, self.KC, self.H, self.FO, self.DI
        nc, bank = self.nc, self.bank
        pe.wait_ge(s["ident"], 1 + 1)
        pe.wait_ge(s["consts"], 1 + 3)
        with pe.Fori(0, B) as b:
            pe.wait_ge(s["x_loaded"], 1 + b * 32 + 32)
            for layer in range(2):
                chunks = 1 if layer == 0 else KC
                if layer == 1:
                    pe.wait_ge(s["elu"], 1 + b * 2 + 1)
                for c in range(chunks):
                    n = self.chunk_no(b, layer, c)
                    pe.wait_ge(s["inT_made"], 1 + n)
                    for m in range(E):
                        src = t["ctx"][:, m, :] if layer == 0 else t["att"][:, m, c * P:(c + 1) * P]
                        last = nc.tensor.transpose(bank[0][:, m * P:(m + 1) * P], src, t["ident"][:, :])
                    last.then_inc(s["turned"], 1)
                pe.wait_ge(s["inT_made"], 1 + self.chunk_no(b, layer, chunks))
                before = 0 if layer == 0 else self.loads[0]
                pe.wait_ge(s["layer_loaded"], 1 + b * (16 * sum(self.loads)) + 16 * (before + self.loads[layer]))
                for m in range(E):
                    pe.wait_ge(s["feat_made"], 1 + self.layer_no(b, layer) * E + m)
                    for c in range(chunks):
                        last = nc.tensor.matmul(bank[1][:, :], t["inT"][:, c, m * P:(m + 1) * P], t["W"][:, c, :],
                                                start=(c == 0), stop=(c == chunks - 1))
                    last.then_inc(s["feat"], 1)
                pe.wait_ge(s["feat_made"], 1 + self.layer_no(b, layer) * E + E)
                pe.sem_inc(s["pe_waited"], 1)
                with pe.Fori(0, H) as h:
                    pe.wait_ge(s["diag"], 1 + self.head_no(b, layer, h) * E + E)
                    pe.wait_ge(s["z_made"], 1 + self.unit(b, layer, h, 0))
                    nc.tensor.matmul(bank[2][:, :], t["ones"][:, :],
                                     t["diag"][:, :, :].rearrange("p m g -> p (m g)"), start=True, stop=True)\
                        .then_inc(s["spread"], 1)
                    for e in range(E):
                        u = self.unit(b, layer, h, e)
                        pe.wait_ge(s["prob_made"], 1 + u + 1)
                        for m in range(E):
                            last = nc.tensor.transpose(bank[3][:, m * P:(m + 1) * P],
                                                       t["prob"][:, m * P:(m + 1) * P], t["ident"][:, :])
                        last.then_inc(s["prob_turned"], 1)
                        pe.wait_ge(s["probT_made"], 1 + u + 1)
                        pe.wait_ge(s["att"], 1 + u)
                        for m in range(E):
                            last = nc.tensor.matmul(bank[4][:, 0:FO], t["probT"][:, m, :],
                                                    t["feat"][:, m, bass.ds(h * FO, FO)],
                                                    start=(m == 0), stop=(m == E - 1))
                        last.then_inc(s["att_done"], 1)
        with pe.Fori(0, E) as g:
            pe.wait_ge(s["ffn_loaded"], 1 + g * 48 + 48)
            pe.wait_ge(s["xn"], 1 + g * B + B)
            for k in range(KC):
                n = g * KC + (B * (1 + KC) + k)
                pe.wait_ge(s["inT_made"], 1 + n)
                for b in range(B):
                    last = nc.tensor.transpose(bank[0][:, b * P:(b + 1) * P], t["xn"][:, b, k * P:(k + 1) * P],
                                               t["ident"][:, :])
                last.then_inc(s["turned"], 1)
            pe.wait_ge(s["inT_made"], 1 + g * KC + (B * (1 + KC) + KC))
            for c in range(KC):
                pe.wait_ge(s["inner"], 1 + g * KC + c)
                for half, name in enumerate(("gate", "up")):
                    for k in range(KC):
                        last = nc.tensor.matmul(bank[1 + half][:, :],
                                                t["gate_up"][:, k, half * DI + c * P:half * DI + (c + 1) * P],
                                                t["inT"][:, k, :], start=(k == 0), stop=(k == KC - 1))
                    last.then_inc(s[name], 1)
            pe.wait_ge(s["inner"], 1 + g * KC + KC)
            for b in range(B):
                pe.wait_ge(s["out"], 1 + g * B + b)
                for i in range(KC):
                    last = nc.tensor.matmul(bank[3][:, :], t["inner"][:, i, b * P:(b + 1) * P], t["down"][:, i, :],
                                            start=(i == 0), stop=(i == KC - 1))
                last.then_inc(s["down"], 1)


def build(nc, x, ctx, W0, a_self0, a_neigh0, b0, W1, a_self1, a_neigh1, b1, gate_up, down, out):
    B, N, D = x.shape
    F_IN = ctx.shape[2]
    H, _, FO = W0.shape
    E = gate_up.shape[0]
    KC = D // P
    DI = down.shape[1]
    D2 = 2 * DI
    assert N == E * P and D == N == DI == H * FO and F_IN == P and KC == E == B

    x_rows = x.rearrange("b (g e) d -> b g e d", e=E)
    out_rows = out.rearrange("b (g e) d -> b e g d", e=E)
    ctx_rows = ctx.rearrange("b (g e) f -> b g e f", e=E)

    with ExitStack() as stack:
        def sem(name):
            return stack.enter_context(nc.semaphore(name))

        def sb_in(where):
            return lambda name, shape, dt=F32: where.enter_context(nc.sbuf_tensor(name, shape, dt))

        main = ExitStack()
        sb = sb_in(main)

        x_sb = sb("x_sb", [P, B, E, D])
        sel_ctx = sb("sel_ctx", [P, 2, E, B, P], F32R)
        W0p = sb("W0p", [P, 2, D], F32R)
        W1p = sb("W1p", [P, KC, 2, D], F32R)
        xnT = sb("xnT", [P, KC, 2, B * P], F32R)
        ctx_xn = sb("ctx_xn", [P, B, D])
        stage = sb("stage", [P, 4, 2 * D])
        ident = sb("ident", [P, P])
        ident_bf = sb("ident_bf", [P, P], BF16)
        ones = sb("ones", [P, 1])
        ones_bf = sb("ones_bf", [P, P], BF16)
        b0_col = sb("b0_col", [P, KC])
        b1_rows = sb("b1_rows", [P, D])
        a_abs = sb("a_abs", [H, 4, FO])
        top8 = sb("top8", [P, B, E, 8])
        xstat = sb("xstat", [P, B, E, 6])
        xmv = sb("xmv", [P, B * E, 2])
        x2stat = sb("x2stat", [P, B, 6])
        x2mv = sb("x2mv", [P, B, 2])
        veps = sb("veps", [P, B * E])
        rstd = sb("rstd", [P, B])
        xrstd = sb("xrstd", [P, B * E])
        minus_half = sb("minus_half", [P, B * E])
        rowmax = sb("rowmax", [P, B + 3])
        allmax = sb("allmax", [P, B + 3])
        ctxmax = sb("ctxmax", [P, 1])
        colmax = sb("colmax", [P, 2])
        bound = sb("bound", [P, 6])
        gap = sb("gap", [P, B * E])
        lead = sb("lead", [P, B * E])
        sure = sb("sure", [P, B * E])
        sure_n = sb("sure_n", [P, 1])
        flag = sb("flag", [1, 1], I32)
        ctx_sb = ctx_xn[:, :, :].rearrange("p b (e f) -> p b e f", e=E)
        xn = ctx_xn

        GUp = sb("GUp", [P, KC, 2, D2], F32R)
        DNp = sb("DNp", [P, KC, 2, D], F32R)

        with ExitStack() as early:
            sbe = sb_in(early)
            G = sbe("G", [P, 2, E, N], BF16)
            GT = sbe("GT", [P, 2, E, N], F32R)
            ctxp = sbe("ctxp", [P, 2, E, 2, F_IN], F32R)
            sel1 = sbe("sel1", [P, 2, E, 2, F_IN], F32R)
            absw = sbe("absw", [P, 1 + KC, D], BF16)
        parts = sb("parts", [P, RING, 2, B * P], F32R)
        ex = sb("ex", [P, 4, D])
        val = sb("val", [P, 4, D])
        sil = sb("sil", [P, 3, D])

        def h_chunk(e, c):
            return (KC * e if e < 2 else 2 * KC * e - KC) + c

        def in_chunk(e, c):
            return (2 * KC * (e + 1) if e < E - 1 else 2 * KC * E - KC) + c

        main.close()

        gsb = sb_in(stack)
        gen = {
            "x": gsb("gen_x", [P, E, D]),
            "mask": gsb("gen_mask", [P, E, E, P]),
            "ctx": gsb("gen_ctx", [P, E, F_IN]),
            "W": gsb("gen_W", [P, KC, D]),
            "a": gsb("gen_a", [P, 2, D]),
            "bias": gsb("gen_bias", [P, D]),
            "inT": gsb("gen_inT", [P, KC, N]),
            "feat": gsb("gen_feat", [P, E, D]),
            "prod": gsb("gen_prod", [P, D]),
            "score": gsb("gen_score", [P, 2, E, H]),
            "diag": gsb("gen_diag", [P, E, P]),
            "z": gsb("gen_z", [P, N]),
            "leaky": gsb("gen_leaky", [P, N]),
            "logit": gsb("gen_logit", [P, N]),
            "prob": gsb("gen_prob", [P, N]),
            "probT": gsb("gen_probT", [P, E, P]),
            "row": gsb("gen_row", [P, 4]),
            "att": gsb("gen_att", [P, E, D]),
            "exp": gsb("gen_exp", [P, E, D]),
            "ident": gsb("gen_ident", [P, P]),
            "ones": gsb("gen_ones", [P, P]),
            "stat": gsb("gen_stat", [P, E, 6]),
            "mv": gsb("gen_mv", [P, E, 2]),
            "veps": gsb("gen_veps", [P, E]),
            "rstd": gsb("gen_rstd", [P, E]),
            "power": gsb("gen_power", [P, E]),
            "gate_up": gsb("gen_gate_up", [P, KC, D2]),
            "down": gsb("gen_down", [P, KC, D]),
            "xn": gsb("gen_xn", [P, B, D]),
            "silu": gsb("gen_silu", [P, D]),
            "inner": gsb("gen_inner", [P, KC, B * P]),
        }

        bank = [stack.enter_context(nc.psum_tensor(f"bank{i}", [P, 512], F32)) for i in range(8)]

        x_loaded = [sem(f"x_loaded{b}") for b in range(B)]
        ctx_loaded = [sem(f"ctx_loaded{b}") for b in range(B)]
        small_loaded = sem("small_loaded")
        stage_loaded = [sem(f"stage_loaded{s}") for s in range(4)]
        out_stored = sem("out_stored")
        consts_made = sem("consts_made")
        ident_made = sem("ident_made")
        ctx_lo = sem("ctx_lo")
        w_lo = sem("w_lo")
        veps_made = sem("veps_made")
        rstd_made = sem("rstd_made")
        allmax_made = sem("allmax_made")
        in_lo = sem("in_lo")
        ctx_hi = sem("ctx_hi")
        w_hi = sem("w_hi")
        abs_made = sem("abs_made")
        GT_made = sem("GT_made")
        sel1_front = sem("sel1_front")
        sel_hi = sem("sel_hi")
        h_exp = sem("h_exp")
        h_hi = sem("h_hi")
        y_exp = sem("y_exp")
        xnT_hi = sem("xnT_hi")
        silu_made = sem("silu_made")
        in_hi = sem("in_hi")
        top_found = sem("top_found")
        G_made = sem("G_made")
        sel1_back = sem("sel1_back")
        sel_lo = sem("sel_lo")
        rowmax_clear = sem("rowmax_clear")
        rowmax_made = sem("rowmax_made")
        colmax_made = sem("colmax_made")
        parts_read = sem("parts_read")
        h_neg = sem("h_neg")
        h_made = sem("h_made")
        h_lo = sem("h_lo")
        y_made = sem("y_made")
        y_neg = sem("y_neg")
        y_elu = sem("y_elu")
        x2_made = sem("x2_made")
        xstat_made = sem("xstat_made")
        x2stat_made = sem("x2stat_made")
        x2mv_made = sem("x2mv_made")
        xmv_made = sem("xmv_made")
        xn_made = sem("xn_made")
        xnT_lo = sem("xnT_lo")
        in_made = sem("in_made")
        out_made = sem("out_made")
        bound_step = sem("bound_step")
        sure_made = sem("sure_made")
        flag_made = sem("flag_made")
        GT_turned = sem("GT_turned")
        sel1_done = sem("sel1_done")
        sel_done = sem("sel_done")
        colsum_done = sem("colsum_done")
        h_done = sem("h_done")
        y_done = sem("y_done")
        xn_turned = sem("xn_turned")
        gate_done = sem("gate_done")
        up_done = sem("up_done")
        down_done = sem("down_done")
        sure_counted = sem("sure_counted")

        W1_v = W1.rearrange("h (c p) o -> p c h o", p=P)
        GU_v = gate_up.rearrange("e (k p) d -> e p k d", p=P)
        DN_v = down.rearrange("e (i p) d -> e p i d", p=P)

        def halves(t):
            return t.rearrange("p (c d) -> p c d", c=2)

        fills = []
        fills.append(dict(
            dma=[(stage[:, 0, 0:D].rearrange("p (h o) -> p h o", h=H), W0.rearrange("h f o -> f h o"))],
            raw=stage[:, 0, 0:D], hi=W0p[:, HI, :], lo=W0p[:, LO, :], kind="W0"))
        for j in range(KC // 2):
            s = len(fills) % 4
            fills.append(dict(
                dma=[(stage[:, s, c * D:(c + 1) * D].rearrange("p (h o) -> p h o", h=H), W1_v[:, 2 * j + c])
                     for c in range(2)],
                raw=halves(stage[:, s, :]), hi=W1p[:, 2 * j:2 * j + 2, HI, :], lo=W1p[:, 2 * j:2 * j + 2, LO, :],
                kind="W1"))
        FIRST = len(fills)
        for e in range(E):
            for k in range(KC):
                s = len(fills) % 4
                fills.append(dict(dma=[(stage[:, s, :], GU_v[e, :, k, :])], raw=stage[:, s, :],
                                  hi=GUp[:, k, HI, :], lo=GUp[:, k, LO, :], kind="GU"))
            for j in range(KC // 2):
                s = len(fills) % 4
                fills.append(dict(dma=[(halves(stage[:, s, :]), DN_v[e, :, 2 * j:2 * j + 2, :])],
                                  raw=halves(stage[:, s, :]), hi=DNp[:, 2 * j:2 * j + 2, HI, :],
                                  lo=DNp[:, 2 * j:2 * j + 2, LO, :], kind="DN"))
        PER_E = KC + KC // 2
        slot_total = [0] * 4
        for f, fill in enumerate(fills):
            slot_total[f % 4] += 16 * len(fill["dma"])
            fill["landed"] = slot_total[f % 4]

        def gu_fill(e, k):
            return FIRST + PER_E * e + k

        def dn_fill(e, j):
            return FIRST + PER_E * e + KC + j

        gen_sems = {name: sem("gen_" + name) for name in GENERAL_SIGNALS}
        general = General(nc, gen, gen_sems, bank, dict(
            x=x_rows, ctx=ctx_rows, W0=W0, a_self0=a_self0, a_neigh0=a_neigh0, b0=b0, W1=W1_v, a_self1=a_self1,
            a_neigh1=a_neigh1, b1=b1, gate_up=GU_v, down=DN_v, out=out), (B, N, D, F_IN, H, FO, E, KC, DI))

        def unless_sure(engine, program):
            engine.wait_ge(flag_made, 1)
            n_sure = engine.value_load(flag[0:1, 0:1])
            with engine.If(n_sure < B * N):
                engine.wait_ge(out_stored, 16 * B * E)
                program(engine)

        block = stack.enter_context(nc.Block())

        @block.sync
        def _(sp):
            def load_fill(f):
                if f >= 4:
                    sp.wait_ge(w_lo, f - 3)
                if 4 <= f < 4 + FIRST:
                    sp.wait_ge(abs_made, f - 3)
                for dst, src in fills[f]["dma"]:
                    sp.dma_start(dst, src).then_inc(stage_loaded[f % 4], 16)

            for b in range(B):
                sp.dma_start(x_sb[:, b, :, :], x_rows[b]).then_inc(x_loaded[b], 16)
                sp.dma_start(ctx_sb[:, b, :, :], ctx_rows[b]).then_inc(ctx_loaded[b], 16)
            for f in range(4):
                load_fill(f)
            sp.dma_start(b0_col[:, :], b0.rearrange("h o -> (h o)").rearrange("(c p) -> p c", p=P),
                         allow_slow_non_contiguous=True).then_inc(small_loaded, 16)
            sp.dma_start(b1_rows[:, :], b1.rearrange("h o -> (h o)").partition_broadcast(P))\
              .then_inc(small_loaded, 16)
            for j, a in enumerate((a_self0, a_neigh0, a_self1, a_neigh1)):
                sp.dma_start(a_abs[:, j, :], a).then_inc(small_loaded, 16)
            for f in range(4, len(fills)):
                load_fill(f)
            sp.wait_ge(out_stored, 16 * B * E)
            unless_sure(sp, general.sync)

        @block.gpsimd
        def _(pool):
            nc.gpsimd.memset(ident_bf[:, :], 0.0).then_inc(consts_made, 1)
            nc.gpsimd.memset(ident[:, :], 0.0).then_inc(consts_made, 1)
            nc.gpsimd.memset(ones[:, :], 1.0).then_inc(consts_made, 1)
            nc.gpsimd.memset(ones_bf[:, :], 1.0).then_inc(consts_made, 1)
            nc.gpsimd.memset(minus_half[:, :], -0.5).then_inc(consts_made, 1)
            pool.wait_ge(consts_made, 5)
            for m in (ident_bf, ident):
                nc.gpsimd.affine_select(out=m[:, :], in_=m[:, :], compare_op=ALU.not_equal, fill=1.0, base=0,
                                        pattern=[[-1, P]], channel_multiplier=1).then_inc(ident_made, 1)

            def w_low(f):
                pool.wait_ge(w_hi, f + 1)
                nc.gpsimd.tensor_tensor(fills[f]["lo"], fills[f]["raw"], fills[f]["hi"].bitcast(F32),
                                        ALU.subtract).then_inc(w_lo, 1)

            def ctx_low(b):
                pool.wait_ge(ctx_hi, b + 1)
                if b >= 2:
                    pool.wait_ge(sel1_done, 2 * (b - 1))
                nc.gpsimd.tensor_tensor(ctxp[:, b % 2, :, LO, :], ctx_sb[:, b, :, :],
                                        ctxp[:, b % 2, :, HI, :].bitcast(F32), ALU.subtract).then_inc(ctx_lo, 1)

            def residual(e, b):
                n = B * e + b
                pool.wait_ge(y_elu, n + 1)
                pool.wait_ge(xstat_made, n + 1)
                nc.gpsimd.tensor_tensor(x_sb[:, b, e, :], x_sb[:, b, e, :], val[:, b, :], ALU.add)\
                    .then_inc(x2_made, 1)

            def inverse_std(mv, n, dst, ready, need, turn):
                pool.wait_ge(ready, need)
                nc.gpsimd.tensor_scalar(veps[:, 0:n], mv[:, :, 1], LN_EPS, None, ALU.add).then_inc(veps_made, 1)
                pool.wait_ge(veps_made, turn)
                nc.gpsimd.tensor_tensor(dst[:, :], veps[:, 0:n], minus_half[:, 0:n], ALU.pow)\
                    .then_inc(rstd_made, 1)

            def inner_low(e, c):
                n, m = KC * e + c, in_chunk(e, c)
                pool.wait_ge(in_hi, n + 1)
                nc.gpsimd.tensor_tensor(parts[:, m % RING, LO, :], sil[:, n % 3, :],
                                        parts[:, m % RING, HI, :].bitcast(F32), ALU.subtract).then_inc(in_lo, 1)

            for b in range(B):
                ctx_low(b)
            for f in range(FIRST + PER_E):
                w_low(f)
            for b in range(B):
                residual(0, b)
            inverse_std(x2mv, B, rstd, x2mv_made, B, 1)
            for e in range(E):
                for c in range(KC):
                    if e + 1 < E:
                        residual(e + 1, c)
                    if c == KC - 1 and e + 1 < E:
                        inverse_std(x2mv, B, rstd, x2mv_made, B * (e + 2), e + 2)
                    inner_low(e, c)
                if e == 0:
                    pool.wait_ge(rowmax_made, B + 3)
                    nc.gpsimd.partition_all_reduce(allmax[:, :], rowmax[:, :], P, RMAX).then_inc(allmax_made, 1)
                if e + 1 < E:
                    for f in range(gu_fill(e + 1, 0), gu_fill(e + 1, 0) + PER_E):
                        w_low(f)
                if e == E - 2:
                    inverse_std(xmv, B * E, xrstd, xmv_made, B * E, E + 1)
            unless_sure(pool, general.gpsimd)

        @block.scalar
        def _(act):
            def w_high(f):
                act.wait_ge(stage_loaded[f % 4], fills[f]["landed"])
                e = (f - FIRST) // PER_E
                if fills[f]["kind"] == "GU" and e > 0:
                    act.wait_ge(up_done, KC * e)
                if fills[f]["kind"] == "DN" and e > 0:
                    act.wait_ge(down_done, B * e)
                nc.scalar.copy(fills[f]["hi"], fills[f]["raw"]).then_inc(w_hi, 1)

            def weights_abs(f):
                dst = absw[:, 0, :] if f == 0 else absw[:, 2 * f - 1:2 * f + 1, :]
                nc.scalar.activation(dst, fills[f]["raw"], ACT.Abs).then_inc(abs_made, 1)

            def ctx_high(b):
                act.wait_ge(ctx_loaded[b], 16)
                if b >= 2:
                    act.wait_ge(sel1_done, 2 * (b - 1))
                nc.scalar.copy(ctxp[:, b % 2, :, HI, :], ctx_sb[:, b, :, :]).then_inc(ctx_hi, 1)

            def turned_G(b):
                for m in range(E):
                    act.wait_ge(GT_turned, E * b + m + 1)
                    if b >= 2:
                        act.wait_ge(sel_done, 2 * (b - 1))
                    nc.scalar.copy(GT[:, b % 2, m, :], bank[m][:, 0:N // 2].bitcast(BF16)).then_inc(GT_made, 1)

            def sel1_evac(b):
                act.wait_ge(sel1_done, 2 * b + 1)
                nc.scalar.copy(sel1[:, b % 2, 0:2, :, :].rearrange("p e r f -> p (e r f)"), bank[4][:, :])\
                    .then_inc(sel1_front, 1)

            def sel_evac(b):
                act.wait_ge(sel_done, 2 * b + 1)
                nc.scalar.copy(sel_ctx[:, HI, :, b, :], bank[6][:, :].rearrange("p (e g) -> p e g", e=E))\
                    .then_inc(sel_hi, 1)

            ctx_high(0)
            ctx_high(1)
            turned_G(0)
            for b in range(B):
                if b + 1 < B:
                    turned_G(b + 1)
                sel1_evac(b)
                if b + 2 < B:
                    ctx_high(b + 2)
                sel_evac(b)
                if b < FIRST:
                    w_high(b)
                    weights_abs(b)

            def h_exp_of(e, c):
                act.wait_ge(h_done, KC * e + c + 1)
                if e == 0 and c == 0:
                    act.wait_ge(small_loaded, 96)
                    act.wait_ge(colsum_done, 2)
                if e == 1:
                    act.wait_ge(h_made, c + 1)
                if e >= 2:
                    act.wait_ge(y_elu, B * (e - 1) + c + 1)
                nc.scalar.activation(ex[:, c, :], bank[4 + c][:, :], ACT.Exp, bias=b0_col[:, c:c + 1])\
                    .then_inc(h_exp, 1)

            def h_high(e, c):
                n = h_chunk(e, c)
                act.wait_ge(h_made, KC * e + c + 1)
                if n >= RING:
                    act.wait_ge(parts_read, n - RING + 1)
                nc.scalar.copy(parts[:, n % RING, HI, :], val[:, c, :]).then_inc(h_hi, 1)

            def y_exp_of(e):
                for b in range(B):
                    act.wait_ge(y_made, B * e + b + 1)
                    if e == 1:
                        act.wait_ge(y_elu, b + 1)
                    else:
                        act.wait_ge(h_made, KC * max(e + 1, 2) - KC + b + 1)
                    nc.scalar.activation(ex[:, b, :], val[:, b, :], ACT.Exp).then_inc(y_exp, 1)

            def turned_xn(e):
                for b in range(B):
                    act.wait_ge(xn_turned, B * e + b + 1)
                    if e > 0:
                        act.wait_ge(up_done, KC * e)
                    nc.scalar.copy(xnT[:, :, HI, b * P:(b + 1) * P],
                                   bank[4 + b][:, :].rearrange("p (k g) -> p k g", k=KC)).then_inc(xnT_hi, 1)

            def silu_of(e, c):
                n = KC * e + c
                act.wait_ge(gate_done, n + 1)
                if n >= 3:
                    act.wait_ge(in_lo, n - 2)
                nc.scalar.activation(sil[:, n % 3, :], bank[4 + 2 * (c % 2)][:, :], ACT.Silu).then_inc(silu_made, 1)

            def inner_high(e, c):
                n, m = KC * e + c, in_chunk(e, c)
                act.wait_ge(in_made, n + 1)
                act.wait_ge(parts_read, m - RING + 1)
                nc.scalar.copy(parts[:, m % RING, HI, :], sil[:, n % 3, :]).then_inc(in_hi, 1)

            def store(e):
                for b in range(B):
                    act.wait_ge(out_made, B * e + b + 1)
                    act.dma_start(out_rows[b, e], x_sb[:, b, e, :]).then_inc(out_stored, 16)

            for n in range(2 * KC + 1):
                if n < 2 * KC:
                    h_exp_of(n // KC, n % KC)
                if n > 0:
                    h_high((n - 1) // KC, (n - 1) % KC)
                if 2 <= n < 2 + PER_E:
                    w_high(FIRST + n - 2)
            y_exp_of(0)
            y_exp_of(1)
            turned_xn(0)
            for e in range(E):
                for c in range(KC + 1):
                    if c < KC:
                        silu_of(e, c)
                    if c > 0:
                        inner_high(e, c - 1)
                if e + 2 < E:
                    for c in range(KC + 1):
                        if c < KC:
                            h_exp_of(e + 2, c)
                        if c > 0:
                            h_high(e + 2, c - 1)
                if e + 1 < E:
                    turned_xn(e + 1)
                    for k in range(KC):
                        w_high(gu_fill(e + 1, k))
                store(e)
                if e + 1 < E:
                    for j in range(KC // 2):
                        w_high(dn_fill(e + 1, j))
                if e + 2 < E:
                    y_exp_of(e + 2)
            unless_sure(act, general.scalar)

        @block.vector
        def _(dve):
            nc.vector.memset(rowmax[:, :], 0.0).then_inc(rowmax_clear, 1)

            def select(b):
                dve.wait_ge(x_loaded[b], 16)
                for e in range(E):
                    nc.vector.max(top8[:, b, e, :], x_sb[:, b, e, :]).then_inc(top_found, 1)
                for e in range(E):
                    dve.wait_ge(top_found, E * b + e + 1)
                    if b >= 2 and e == 0:
                        dve.wait_ge(GT_turned, E * (b - 1))
                    nc.vector.tensor_scalar(G[:, b % 2, e, :], x_sb[:, b, e, :], top8[:, b, e, 0:1], None,
                                            ALU.is_equal).then_inc(G_made, 1)

            def ctx_max(b):
                dve.wait_ge(ctx_loaded[b], 16)
                if b == 0:
                    dve.wait_ge(rowmax_clear, 1)
                nc.vector.tensor_reduce(rowmax[:, b:b + 1], ctx_xn[:, b, :], AX.X, ALU.max,
                                        apply_absolute_value=True).then_inc(rowmax_made, 1)

            def sel1_evac(b):
                dve.wait_ge(sel1_done, 2 * b + 2)
                nc.vector.tensor_copy(sel1[:, b % 2, 2:4, :, :].rearrange("p e r f -> p (e r f)"), bank[5][:, :])\
                    .then_inc(sel1_back, 1)

            def sel_evac(b):
                dve.wait_ge(sel_done, 2 * b + 2)
                nc.vector.tensor_copy(sel_ctx[:, LO, :, b, :], bank[7][:, :].rearrange("p (e g) -> p e g", e=E))\
                    .then_inc(sel_lo, 1)

            select(0)
            select(1)
            for b in range(B):
                sel1_evac(b)
                if b + 2 < B:
                    select(b + 2)
                else:
                    for j in range(2):
                        ctx_max(2 * (b + 2 - B) + j)
                sel_evac(b)

            def small_maxima():
                dve.wait_ge(small_loaded, 96)
                for layer in range(2):
                    nc.vector.tensor_reduce(rowmax[0:H, B + layer:B + layer + 1],
                                            a_abs[:, 2 * layer:2 * layer + 2, :],
                                            AX.XY, ALU.add, apply_absolute_value=True).then_inc(rowmax_made, 1)
                nc.vector.tensor_reduce(rowmax[:, B + 2:B + 3], b0_col[:, :], AX.X, ALU.max,
                                        apply_absolute_value=True).then_inc(rowmax_made, 1)
                for j in range(2):
                    dve.wait_ge(colsum_done, j + 1)
                    nc.vector.tensor_reduce(colmax[:, j:j + 1], bank[j][:, :], AX.X, ALU.max)\
                        .then_inc(colmax_made, 1)

            def h_value(e, c):
                n = KC * e + c
                dve.wait_ge(h_exp, n + 1)
                nc.vector.tensor_scalar(ex[:, c, :], ex[:, c, :], 1.0, -1.0, ALU.min, ALU.add).then_inc(h_neg, 1)
                dve.wait_ge(h_neg, n + 1)
                if e >= 2:
                    dve.wait_ge(x2_made, B * (e - 1) + c + 1)
                nc.vector.scalar_tensor_tensor(val[:, c, :], bank[4 + c][:, :], b0_col[:, c:c + 1], ex[:, c, :],
                                               ALU.add, ALU.max).then_inc(h_made, 1)

            def h_low(e, c):
                m = h_chunk(e, c)
                dve.wait_ge(h_hi, KC * e + c + 1)
                nc.vector.tensor_tensor(parts[:, m % RING, LO, :], val[:, c, :],
                                        parts[:, m % RING, HI, :].bitcast(F32), ALU.subtract).then_inc(h_lo, 1)

            def y_values(e):
                for b in range(B):
                    nc.vector.bn_stats(xstat[:, b, e, :], x_sb[:, b, e, :]).then_inc(xstat_made, 1)
                for b in range(B):
                    dve.wait_ge(y_done, B * e + b + 1)
                    if e == 0 and b == 0:
                        dve.wait_ge(small_loaded, 96)
                    if e == 1:
                        dve.wait_ge(x2_made, b + 1)
                    else:
                        dve.wait_ge(h_lo, KC * max(e + 1, 2) - KC + b + 1)
                    nc.vector.tensor_tensor(val[:, b, :], bank[b][:, :], b1_rows[:, :], ALU.add).then_inc(y_made, 1)

            def y_elus(e, b):
                n = B * e + b
                dve.wait_ge(y_exp, n + 1)
                nc.vector.tensor_scalar(ex[:, b, :], ex[:, b, :], 1.0, -1.0, ALU.min, ALU.add).then_inc(y_neg, 1)
                dve.wait_ge(y_neg, n + 1)
                nc.vector.tensor_tensor(val[:, b, :], val[:, b, :], ex[:, b, :], ALU.max).then_inc(y_elu, 1)

            def x2_stats(e, b):
                n = B * e + b
                dve.wait_ge(x2_made, n + 1)
                nc.vector.bn_stats(x2stat[:, b, :], x_sb[:, b, e, :]).then_inc(x2stat_made, 1)
                dve.wait_ge(x2stat_made, n + 1)
                if e > 0 and b == 0:
                    dve.wait_ge(rstd_made, e)
                    dve.wait_ge(xn_made, B * e)
                nc.vector.bn_aggr(x2mv[:, b, :], x2stat[:, b, :]).then_inc(x2mv_made, 1)

            def normalize(e):
                dve.wait_ge(rstd_made, e + 1)
                dve.wait_ge(x2mv_made, B * (e + 1))
                for b in range(B):
                    if e > 0:
                        dve.wait_ge(xn_turned, B * (e - 1) + b + 1)
                    elif b == 0:
                        dve.wait_ge(rowmax_made, B)
                        dve.wait_ge(ctx_lo, B)
                    nc.vector.tensor_scalar(xn[:, b, :], x_sb[:, b, e, :], x2mv[:, b, 0:1], rstd[:, b:b + 1],
                                            ALU.subtract, ALU.mult).then_inc(xn_made, 1)

            def turned_low(e):
                for b in range(B):
                    dve.wait_ge(xnT_hi, B * e + b + 1)
                    nc.vector.tensor_tensor(xnT[:, :, LO, b * P:(b + 1) * P],
                                            bank[4 + b][:, :].rearrange("p (k g) -> p k g", k=KC),
                                            xnT[:, :, HI, b * P:(b + 1) * P].bitcast(F32), ALU.subtract)\
                        .then_inc(xnT_lo, 1)

            def inner(e, c):
                n = KC * e + c
                dve.wait_ge(silu_made, n + 1)
                dve.wait_ge(up_done, n + 1)
                nc.vector.tensor_tensor(sil[:, n % 3, :], bank[5 + 2 * (c % 2)][:, :], sil[:, n % 3, :], ALU.mult)\
                    .then_inc(in_made, 1)

            def outputs(e):
                for b in range(B):
                    n = B * e + b
                    dve.wait_ge(down_done, n + 1)
                    dve.wait_ge(xn_made, n + 1)
                    nc.vector.tensor_tensor(x_sb[:, b, e, :], x_sb[:, b, e, :], bank[b][:, :], ALU.add)\
                        .then_inc(out_made, 1)

            def check_rows():
                steps = [0]

                def step(ins):
                    steps[0] += 1
                    ins.then_inc(bound_step, 1)
                    dve.wait_ge(bound_step, steps[0])

                dve.wait_ge(allmax_made, 1)
                dve.wait_ge(colmax_made, 2)
                step(nc.vector.tensor_reduce(ctxmax[:, :], allmax[:, 0:B], AX.X, ALU.max))
                step(nc.vector.tensor_tensor(bound[:, 0:1], ctxmax[:, :], colmax[:, 0:1], ALU.mult))
                step(nc.vector.tensor_tensor(bound[:, 1:2], bound[:, 0:1], allmax[:, B:B + 1], ALU.mult))
                step(nc.vector.scalar_tensor_tensor(bound[:, 2:3], bound[:, 0:1], 1.0, allmax[:, B + 2:B + 3],
                                                    ALU.add, ALU.add))
                step(nc.vector.tensor_tensor(bound[:, 3:4], bound[:, 2:3], colmax[:, 1:2], ALU.mult))
                step(nc.vector.tensor_tensor(bound[:, 4:5], bound[:, 3:4], allmax[:, B + 1:B + 2], ALU.mult))
                step(nc.vector.tensor_tensor(bound[:, 5:6], bound[:, 1:2], bound[:, 4:5], ALU.add))
                step(nc.vector.tensor_scalar(bound[:, 5:6], bound[:, 5:6], 2.1, UNDERFLOW, ALU.mult, ALU.add))
                tops = top8[:, :, :, :].rearrange("p b e t -> p (b e) t")
                step(nc.vector.tensor_tensor(gap[:, :], tops[:, :, 0], tops[:, :, 1], ALU.subtract))
                step(nc.vector.tensor_tensor(lead[:, :], tops[:, :, 0], xmv[:, :, 0], ALU.subtract))
                dve.wait_ge(rstd_made, E + 1)
                step(nc.vector.scalar_tensor_tensor(gap[:, :], gap[:, :], MASK, xrstd[:, :], ALU.mult, ALU.mult))
                step(nc.vector.tensor_tensor(lead[:, :], lead[:, :], xrstd[:, :], ALU.mult))
                step(nc.vector.tensor_scalar(lead[:, :], lead[:, :], 1.0, MASK * ROUNDINGS, ALU.add, ALU.mult))
                step(nc.vector.scalar_tensor_tensor(sure[:, :], lead[:, :], bound[:, 5:6], gap[:, :], ALU.add,
                                                    ALU.is_lt))
                nc.vector.tensor_reduce(sure_n[:, :], sure[:, :], AX.X, ALU.add).then_inc(sure_made, 1)

            for n in range(2 * KC + 1):
                if n < 2 * KC:
                    h_value(n // KC, n % KC)
                if n > 0:
                    h_low((n - 1) // KC, (n - 1) % KC)
                if n == 1:
                    small_maxima()
            y_values(0)
            for b in range(B + 1):
                if b < B:
                    y_elus(0, b)
                if b > 0:
                    x2_stats(0, b - 1)
            normalize(0)
            y_values(1)
            turned_low(0)
            for e in range(E):
                for c in range(KC):
                    if e + 1 < E:
                        if c == 0:
                            y_elus(e + 1, 0)
                        if c + 1 < B:
                            y_elus(e + 1, c + 1)
                        x2_stats(e + 1, c)
                    inner(e, c)
                if e + 1 < E:
                    normalize(e + 1)
                if e + 2 < E:
                    for c in range(KC + 1):
                        if c < KC:
                            h_value(e + 2, c)
                        if c > 0:
                            h_low(e + 2, c - 1)
                if e + 1 < E:
                    turned_low(e + 1)
                if e == E - 2:
                    for t in range(B * E):
                        nc.vector.bn_aggr(xmv[:, t, :], xstat[:, t // E, t % E, :]).then_inc(xmv_made, 1)
                if e == E - 1:
                    check_rows()
                outputs(e)
                if e + 2 < E:
                    y_values(e + 2)
            dve.wait_ge(sure_counted, 1)
            nc.vector.tensor_copy(flag[:, :], bank[4][0:1, 0:1]).then_inc(flag_made, 1)
            unless_sure(dve, general.vector)

        @block.tensor
        def _(pe):
            def turn(b):
                for m in range(E):
                    if b > 0:
                        pe.wait_ge(GT_made, E * (b - 1) + m + 1)
                    for e in range(E):
                        if m == 0:
                            pe.wait_ge(G_made, E * b + e + 1)
                        last = nc.tensor.transpose(bank[m][:, 0:N // 2].bitcast(BF16)[:, e * P:(e + 1) * P],
                                                   G[:, b % 2, e, m::E], ident_bf[:, :])
                    last.then_inc(GT_turned, 1)

            def select1(b):
                pe.wait_ge(ctx_lo, b + 1)
                pe.wait_ge(GT_made, E * (b + 1))
                if b > 0:
                    pe.wait_ge(sel1_front, b)
                    pe.wait_ge(sel1_back, b)
                for e in range(E):
                    dst = bank[4 + e // 2][:, (e % 2) * 2 * F_IN:(e % 2 + 1) * 2 * F_IN]
                    for k in range(E):
                        last = nc.tensor.matmul(dst, GT[:, b % 2, k, e * P:(e + 1) * P],
                                                ctxp[:, b % 2, k, :, :].rearrange("p r f -> p (r f)"),
                                                start=(k == 0), stop=(k == E - 1))
                    if e % 2:
                        last.then_inc(sel1_done, 1)

            def select2(b):
                pe.wait_ge(sel1_front, b + 1)
                pe.wait_ge(sel1_back, b + 1)
                if b > 0:
                    pe.wait_ge(sel_hi, b)
                    pe.wait_ge(sel_lo, b)
                for part in (HI, LO):
                    for k in range(E):
                        last = nc.tensor.matmul(bank[6 + part][:, :], sel1[:, b % 2, k, part, :], GT[:, b % 2, k, :],
                                                start=(k == 0), stop=(k == E - 1))
                    last.then_inc(sel_done, 1)

            def column_sums():
                pe.wait_ge(abs_made, 3)
                pe.wait_ge(GT_made, E * B)
                nc.tensor.matmul(bank[0][:, :], ones_bf[:, :], absw[:, 0, :], start=True, stop=True)\
                    .then_inc(colsum_done, 1)
                for c in range(KC):
                    last = nc.tensor.matmul(bank[1][:, :], ones_bf[:, :], absw[:, 1 + c, :],
                                            start=(c == 0), stop=(c == KC - 1))
                last.then_inc(colsum_done, 1)

            pe.wait_ge(ident_made, 2)
            turn(0)
            for b in range(B):
                if b + 1 < B:
                    turn(b + 1)
                select1(b)
                select2(b)
            column_sums()

            def layer0(e, chunks):
                if e == 0:
                    pe.wait_ge(sel_hi, B)
                    pe.wait_ge(sel_lo, B)
                    pe.wait_ge(w_lo, 1)
                for c in chunks:
                    if e == 1:
                        pe.wait_ge(h_made, c + 1)
                    if e >= 2:
                        pe.wait_ge(in_made, KC * (e - 2) + 3 + c // 2)
                    for j, (w, v) in enumerate(TERMS):
                        last = nc.tensor.matmul(bank[4 + c][:, :], W0p[:, w, c * P:(c + 1) * P],
                                                sel_ctx[:, v, e, :, :].rearrange("p b g -> p (b g)"),
                                                start=(j == 0), stop=(j == 2))
                    last.then_inc(h_done, 1)

            def layer1(e, chunks):
                for c in chunks:
                    slot = h_chunk(e, c) % RING
                    if e == 0 and c == 0:
                        pe.wait_ge(w_lo, FIRST)
                        pe.wait_ge(colmax_made, 2)
                    pe.wait_ge(h_lo, KC * e + c + 1)
                    for b in range(B):
                        if c == 0 and e == 1:
                            pe.wait_ge(y_made, B * (e - 1) + b + 1)
                        if c == 0 and e >= 2:
                            pe.wait_ge(out_made, B * (e - 2) + b + 1)
                        for j, (w, v) in enumerate(TERMS):
                            last = nc.tensor.matmul(bank[b][:, :], parts[:, slot, w, b * P:(b + 1) * P],
                                                    W1p[:, c, v, :],
                                                    start=(c == 0 and j == 0), stop=(c == KC - 1 and j == 2))
                        if c == KC - 1:
                            last.then_inc(y_done, 1)
                    pe.drain().then_inc(parts_read, 1)

            def turn_xn(e):
                if e + 1 < E:
                    pe.wait_ge(h_made, KC * (e + 2))
                else:
                    pe.wait_ge(in_made, KC * e)
                for b in range(B):
                    pe.wait_ge(xn_made, B * e + b + 1)
                    for k in range(KC):
                        last = nc.tensor.transpose(bank[4 + b][:, k * P:(k + 1) * P], xn[:, b, k * P:(k + 1) * P],
                                                   ident[:, :])
                    last.then_inc(xn_turned, 1)

            def gate_and_up(e):
                for c in range(KC):
                    if c == 0:
                        pe.wait_ge(xnT_lo, B * (e + 1))
                    if c >= 2:
                        pe.wait_ge(in_made, KC * e + c - 1)
                    for half, done in ((0, gate_done), (1, up_done)):
                        col = half * DI + c * P
                        for k in range(KC):
                            if c == 0 and half == 0:
                                pe.wait_ge(w_lo, gu_fill(e, k) + 1)
                            for j, (w, v) in enumerate(TERMS):
                                last = nc.tensor.matmul(bank[4 + 2 * (c % 2) + half][:, :],
                                                        GUp[:, k, w, col:col + P], xnT[:, k, v, :],
                                                        start=(k == 0 and j == 0), stop=(k == KC - 1 and j == 2))
                        last.then_inc(done, 1)

            def project_down(e, chunks, rows=range(B)):
                for i in chunks:
                    slot = in_chunk(e, i) % RING
                    if i % 2 == 0:
                        pe.wait_ge(w_lo, dn_fill(e, i // 2) + 1)
                    pe.wait_ge(in_lo, KC * e + i + 1)
                    for b in rows:
                        if i == 0:
                            if e < E - 1:
                                pe.wait_ge(y_made, B * (e + 1) + b + 1)
                            else:
                                pe.wait_ge(out_made, B * (e - 1) + b + 1)
                        for j, (w, v) in enumerate(TERMS):
                            last = nc.tensor.matmul(bank[b][:, :], parts[:, slot, w, b * P:(b + 1) * P],
                                                    DNp[:, i, v, :],
                                                    start=(i == 0 and j == 0), stop=(i == KC - 1 and j == 2))
                        if i == KC - 1:
                            last.then_inc(down_done, 1)
                    if len(rows) == B:
                        pe.drain().then_inc(parts_read, 1)

            layer0(0, range(KC))
            layer1(0, (0,))
            layer0(1, (0, 1))
            layer1(0, (1,))
            layer0(1, (2, 3))
            layer1(0, (2, 3))
            layer1(1, range(KC))
            turn_xn(0)
            for e in range(E):
                gate_and_up(e)
                if e + 2 < E:
                    layer0(e + 2, (0, 1))
                    project_down(e, (0,))
                    layer0(e + 2, (2, 3))
                    project_down(e, (1,))
                    turn_xn(e + 1)
                    project_down(e, (2, 3))
                    layer1(e + 2, range(KC))
                elif e + 1 < E:
                    project_down(e, (0, 1))
                    turn_xn(e + 1)
                    project_down(e, (2, 3))
                else:
                    pe.wait_ge(sure_made, 1)
                    pe.wait_ge(in_made, KC * e + 3)
                    nc.tensor.matmul(bank[4][0:1, 0:1], sure_n[:, 0:1], ones[:, 0:1], start=True, stop=True)\
                        .then_inc(sure_counted, 1)
                    for b in range(B):
                        project_down(e, range(KC), (b,))
            unless_sure(pe, general.tensor)


_INS = ['x', 'ctx_512', 'L0_xattn_W0', 'L0_xattn_a_self0', 'L0_xattn_a_neigh0', 'L0_xattn_b0', 'L0_xattn_W1',
        'L0_xattn_a_self1', 'L0_xattn_a_neigh1', 'L0_xattn_b1', 'L0_ffn_gate_up_proj', 'L0_ffn_down_proj']


def kernel(**inputs):
    import numpy as _np
    import concourse.bacc as _bacc
    from concourse import mybir as _mybir
    from concourse.bass_utils import run_bass_kernel_spmd as _run

    nc = _bacc.Bacc("TRN2", target_bir_lowering=False, num_devices=1)
    arrays, args = {}, []
    for name in _INS:
        a = _np.ascontiguousarray(inputs[name])
        arrays[f"in_{name}"] = a
        args.append(nc.dram_tensor(f"in_{name}", a.shape, _mybir.dt.from_np(a.dtype), kind="ExternalInput").ap())
    shape = inputs['x'].shape
    args.append(nc.dram_tensor("out_0", shape, _mybir.dt.float32, kind="ExternalOutput").ap())
    build(nc, *args)
    r = _run(nc, [arrays], core_ids=[0])
    return r.results[0]["out_0"]
```

```python
from contextlib import ExitStack

import concourse.bass as bass
from concourse import mybir

F32 = mybir.dt.float32
F32R = mybir.dt.float32r
BF16 = mybir.dt.bfloat16
I32 = mybir.dt.int32
ALU = mybir.AluOpType
ACT = mybir.ActivationFunctionType
AX = mybir.AxisListType
RMAX = bass.bass_isa.ReduceOp.max

P = 128
EXPS = 5
HI, LO = 0, 1
TERMS = ((HI, HI), (HI, LO), (LO, HI))
LN_EPS = 1e-5
MASK = 1e10
ROUNDINGS = 2.0 ** -20
UNDERFLOW = 110.0


GENERAL_SIGNALS = (
    "x_loaded", "layer_loaded", "x2_stored", "ffn_loaded", "out_stored",
    "consts", "ident", "veps", "rstd",
    "feat_made", "z_made", "prob_made", "probT_made", "att_exp", "silu_made",
    "stat", "mv", "adj", "one_minus", "mask", "inT_made", "prod", "score", "diag", "leaky", "logit",
    "neg_max", "inverse", "att", "att_neg", "elu", "x2", "xn", "inner", "out",
    "dve_waited", "pool_waited", "pe_waited", "sp_waited",
    "turned", "feat", "spread", "prob_turned", "att_done", "gate", "up", "down",
)


class General:

    def __init__(self, nc, gen, sems, bank, dram, sizes):
        self.nc, self.t, self.s, self.bank, self.dram = nc, gen, sems, bank, dram
        self.B, self.N, self.D, self.F_IN, self.H, self.FO, self.E, self.KC, self.DI = sizes
        self.loads = (4, self.KC + 3)

    def layer_no(self, b, layer):
        return b * 2 + layer

    def head_no(self, b, layer, h):
        return b * (2 * self.H) + h + layer * self.H

    def unit(self, b, layer, h, e):
        return b * (2 * self.H * self.E) + h * self.E + (layer * self.H * self.E + e)

    def chunk_no(self, b, layer, c):
        return b * (1 + self.KC) + layer + c

    def sync(self, sp):
        t, s, d, B, E, KC, H = self.t, self.s, self.dram, self.B, self.E, self.KC, self.H
        flat = lambda v: v.rearrange("h o -> (h o)").partition_broadcast(P)
        heads = lambda v: v.rearrange("p (h o) -> p h o", h=H)
        for name in GENERAL_SIGNALS:
            sp.sem_inc(s[name], 1)
        with sp.Fori(0, B) as b:
            sp.wait_ge(s["x2_stored"], 1 + b * 16)
            sp.sem_inc(s["sp_waited"], 1)
            sp.wait_ge(s["turned"], 1 + b * (1 + KC))
            sp.dma_start(t["x"][:, :, :], d["x"][b]).then_inc(s["x_loaded"], 16)
            sp.dma_start(t["ctx"][:, :, :], d["ctx"][b]).then_inc(s["x_loaded"], 16)
            for layer in range(2):
                sp.wait_ge(s["att"], 1 + self.unit(b, layer, 0, 0))
                if layer == 0:
                    sp.dma_start(heads(t["W"][:, 0, :]), d["W0"].rearrange("h f o -> f h o"))\
                        .then_inc(s["layer_loaded"], 16)
                else:
                    for c in range(KC):
                        sp.dma_start(heads(t["W"][:, c, :]), d["W1"][:, c]).then_inc(s["layer_loaded"], 16)
                for j, name in enumerate(("a_self", "a_neigh")):
                    sp.dma_start(t["a"][:, j, :], flat(d[f"{name}{layer}"])).then_inc(s["layer_loaded"], 16)
                sp.dma_start(t["bias"][:, :], flat(d[f"b{layer}"])).then_inc(s["layer_loaded"], 16)
            sp.wait_ge(s["x2"], 1 + b + 1)
            sp.dma_start(d["out"].rearrange("b (g e) d -> b g e d", e=E)[b], t["x"][:, :, :])\
                .then_inc(s["x2_stored"], 16)
        sp.wait_ge(s["x2_stored"], 1 + 16 * B)
        rows = d["out"].rearrange("b (g e) d -> e g b d", e=E)
        with sp.Fori(0, E) as e:
            sp.wait_ge(s["out_stored"], 1 + e * 16)
            sp.sem_inc(s["sp_waited"], 1)
            sp.wait_ge(s["down"], 1 + e * B)
            sp.sem_inc(s["sp_waited"], 1)
            sp.dma_start(t["x"][:, :, :], rows[e]).then_inc(s["ffn_loaded"], 16)
            sp.dma_start(t["gate_up"][:, :, :], d["gate_up"][e]).then_inc(s["ffn_loaded"], 16)
            sp.dma_start(t["down"][:, :, :], d["down"][e]).then_inc(s["ffn_loaded"], 16)
            sp.wait_ge(s["out"], 1 + e * B + B)
            sp.sem_inc(s["sp_waited"], 1)
            sp.dma_start(rows[e], t["x"][:, :, :]).then_inc(s["out_stored"], 16)
        sp.wait_ge(s["out_stored"], 1 + 16 * E)

    def gpsimd(self, pool):
        t, s, B, E, nc = self.t, self.s, self.B, self.E, self.nc
        nc.gpsimd.memset(t["ones"][:, :], 1.0).then_inc(s["consts"], 1)
        nc.gpsimd.memset(t["ident"][:, :], 0.0).then_inc(s["consts"], 1)
        nc.gpsimd.memset(t["power"][:, :], -0.5).then_inc(s["consts"], 1)
        pool.wait_ge(s["consts"], 1 + 3)
        nc.gpsimd.affine_select(out=t["ident"][:, :], in_=t["ident"][:, :], compare_op=ALU.not_equal, fill=1.0,
                                base=0, pattern=[[-1, P]], channel_multiplier=1).then_inc(s["ident"], 1)
        with pool.Fori(0, B + E) as i:
            pool.wait_ge(s["mv"], 1 + i * 4 + 4)
            pool.sem_inc(s["pool_waited"], 1)
            nc.gpsimd.tensor_scalar(t["veps"][:, :], t["mv"][:, :, 1], LN_EPS, None, ALU.add)\
                .then_inc(s["veps"], 1)
            pool.wait_ge(s["veps"], 1 + i + 1)
            nc.gpsimd.tensor_tensor(t["rstd"][:, :], t["veps"][:, :], t["power"][:, :], ALU.pow)\
                .then_inc(s["rstd"], 1)

    def scalar(self, act):
        t, s, B, E, KC, H, nc, bank = self.t, self.s, self.B, self.E, self.KC, self.H, self.nc, self.bank
        with act.Fori(0, B) as b:
            for layer in range(2):
                for m in range(E):
                    n = self.layer_no(b, layer) * E + m
                    act.wait_ge(s["feat"], 1 + n + 1)
                    if m == 0:
                        act.wait_ge(s["att"], 1 + self.unit(b, layer, 0, 0))
                    nc.scalar.copy(t["feat"][:, m, :], bank[1][:, :]).then_inc(s["feat_made"], 1)
                with act.Fori(0, H) as h:
                    act.wait_ge(s["spread"], 1 + self.head_no(b, layer, h) + 1)
                    act.wait_ge(s["score"], 1 + self.layer_no(b, layer) * (2 * E) + 2 * E)
                    for e in range(E):
                        u = self.unit(b, layer, h, e)
                        act.wait_ge(s["leaky"], 1 + u)
                        nc.scalar.activation(t["z"][:, :], bank[2][:, :], ACT.Identity,
                                             bias=t["score"][:, 0, e, bass.ds(h, 1)]).then_inc(s["z_made"], 1)
                        act.wait_ge(s["neg_max"], 1 + u + 1)
                        act.wait_ge(s["prob_turned"], 1 + u)
                        act.wait_ge(s["inverse"], 1 + u)
                        nc.scalar.activation(t["prob"][:, :], t["logit"][:, :], ACT.Exp, bias=t["row"][:, 1:2],
                                             accum_out=t["row"][:, 2:3]).then_inc(s["prob_made"], 1)
                        act.wait_ge(s["prob_turned"], 1 + u + 1)
                        nc.scalar.copy(t["probT"][:, :, :].rearrange("p m g -> p (m g)"), bank[3][:, :])\
                            .then_inc(s["probT_made"], 1)
                act.wait_ge(s["att"], 1 + self.unit(b, layer, 0, 0) + H * E)
                act.wait_ge(s["elu"], 1 + self.layer_no(b, layer))
                nc.scalar.activation(t["exp"][:, :, :], t["att"][:, :, :], ACT.Exp).then_inc(s["att_exp"], 1)
        with act.Fori(0, E) as e:
            for c in range(KC):
                act.wait_ge(s["gate"], 1 + e * KC + (c + 1))
                act.wait_ge(s["inner"], 1 + e * KC + c)
                nc.scalar.activation(t["silu"][:, :], bank[1][:, :], ACT.Silu).then_inc(s["silu_made"], 1)

    def normalize(self, dve, i, load, loaded, free, dst):
        t, s, nc = self.t, self.s, self.nc
        dve.wait_ge(load, 1 + loaded)
        for e in range(self.E):
            nc.vector.bn_stats(t["stat"][:, e, :], t["x"][:, e, :]).then_inc(s["stat"], 1)
        dve.wait_ge(s["rstd"], 1 + i)
        dve.wait_ge(s["stat"], 1 + i * 4 + 4)
        dve.sem_inc(s["dve_waited"], 1)
        for e in range(self.E):
            nc.vector.bn_aggr(t["mv"][:, e, :], t["stat"][:, e, :]).then_inc(s["mv"], 1)
        dve.wait_ge(s["rstd"], 1 + i + 1)
        dve.wait_ge(s["mv"], 1 + i * 4 + 4)
        free()
        for e in range(self.E):
            src, to, signal = dst(e)
            nc.vector.tensor_scalar(to, src, t["mv"][:, e, 0:1], t["rstd"][:, e:e + 1], ALU.subtract, ALU.mult)\
                .then_inc(signal, 1)

    def vector(self, dve):
        t, s, B, E, KC, H, FO = self.t, self.s, self.B, self.E, self.KC, self.H, self.FO
        nc, bank, unit = self.nc, self.bank, self.unit
        every = lambda v: v.rearrange("p e d -> p (e d)")
        mask = t["mask"][:, :, :, :].rearrange("p e r g -> p (e r g)")
        dve.wait_ge(s["ident"], 1 + 1)
        with dve.Fori(0, B) as b:
            def adj(e):
                return (t["x"][:, e, :].rearrange("p (g r) -> p g r", r=E),
                        t["mask"][:, e, :, :].rearrange("p r g -> p g r"), s["adj"])

            self.normalize(dve, b, s["x_loaded"], b * 32 + 32, lambda: None, adj)
            dve.wait_ge(s["adj"], 1 + b * E + E)
            nc.vector.tensor_scalar(mask, mask, -1.0, 1.0, ALU.mult, ALU.add).then_inc(s["one_minus"], 1)
            dve.wait_ge(s["one_minus"], 1 + b + 1)
            nc.vector.tensor_scalar(mask, mask, -MASK, None, ALU.mult).then_inc(s["mask"], 1)
            dve.wait_ge(s["mask"], 1 + b + 1)
            for layer in range(2):
                for c in range(1 if layer == 0 else KC):
                    n = self.chunk_no(b, layer, c)
                    dve.wait_ge(s["turned"], 1 + n + 1)
                    nc.vector.tensor_copy(t["inT"][:, c, :], bank[0][:, :]).then_inc(s["inT_made"], 1)
                for m in range(E):
                    dve.wait_ge(s["feat_made"], 1 + self.layer_no(b, layer) * E + (m + 1))
                    for j in range(2):
                        n = self.layer_no(b, layer) * (2 * E) + (2 * m + j)
                        dve.wait_ge(s["score"], 1 + n)
                        nc.vector.tensor_tensor(t["prod"][:, :], t["feat"][:, m, :], t["a"][:, j, :], ALU.mult)\
                            .then_inc(s["prod"], 1)
                        dve.wait_ge(s["prod"], 1 + n + 1)
                        nc.vector.tensor_reduce(t["score"][:, j, m, :],
                                                t["prod"][:, :].rearrange("p (h o) -> p h o", h=H), AX.X, ALU.add)\
                            .then_inc(s["score"], 1)
                dve.wait_ge(s["score"], 1 + self.layer_no(b, layer) * (2 * E) + 2 * E)
                dve.sem_inc(s["dve_waited"], 1)
                with dve.Fori(0, H) as h:
                    dve.wait_ge(s["spread"], 1 + self.head_no(b, layer, h))
                    for m in range(E):
                        nc.vector.tensor_scalar(t["diag"][:, m, :], t["ident"][:, :],
                                                t["score"][:, 1, m, bass.ds(h, 1)], None, ALU.mult)\
                            .then_inc(s["diag"], 1)
                    for e in range(E):
                        u = unit(b, layer, h, e)
                        dve.wait_ge(s["z_made"], 1 + u + 1)
                        nc.vector.scalar_tensor_tensor(t["leaky"][:, :], t["z"][:, :], 0.2, t["z"][:, :],
                                                       ALU.mult, ALU.max).then_inc(s["leaky"], 1)
                        dve.wait_ge(s["leaky"], 1 + u + 1)
                        dve.wait_ge(s["prob_made"], 1 + u)
                        dve.sem_inc(s["dve_waited"], 1)
                        nc.vector.tensor_tensor_reduce(
                            t["logit"][:, :], t["leaky"][:, :],
                            t["mask"][:, e, :, :].rearrange("p r g -> p (r g)"), 1.0, -3e38, ALU.add, ALU.max,
                            t["row"][:, 0:1]).then_inc(s["logit"], 1)
                        dve.wait_ge(s["logit"], 1 + u + 1)
                        nc.vector.tensor_scalar(t["row"][:, 1:2], t["row"][:, 0:1], -1.0, None, ALU.mult)\
                            .then_inc(s["neg_max"], 1)
                        dve.wait_ge(s["prob_made"], 1 + u + 1)
                        nc.vector.reciprocal(t["row"][:, 3:4], t["row"][:, 2:3]).then_inc(s["inverse"], 1)
                        dve.wait_ge(s["inverse"], 1 + u + 1)
                        dve.wait_ge(s["att_done"], 1 + u + 1)
                        cols = bass.ds(h * FO, FO)
                        nc.vector.scalar_tensor_tensor(t["att"][:, e, cols], bank[4][:, 0:FO], t["row"][:, 3:4],
                                                       t["bias"][:, cols], ALU.mult, ALU.add).then_inc(s["att"], 1)
                n = self.layer_no(b, layer)
                dve.wait_ge(s["att_exp"], 1 + n + 1)
                nc.vector.tensor_scalar(every(t["exp"]), every(t["exp"]), 1.0, -1.0, ALU.min, ALU.add)\
                    .then_inc(s["att_neg"], 1)
                dve.wait_ge(s["att_neg"], 1 + n + 1)
                dve.wait_ge(s["att"], 1 + unit(b, layer, 0, 0) + H * E)
                nc.vector.tensor_tensor(every(t["att"]), every(t["att"]), every(t["exp"]), ALU.max)\
                    .then_inc(s["elu"], 1)
            dve.wait_ge(s["elu"], 1 + b * 2 + 2)
            nc.vector.tensor_tensor(every(t["x"]), every(t["x"]), every(t["att"]), ALU.add).then_inc(s["x2"], 1)
        with dve.Fori(0, E) as g:
            def free():
                dve.wait_ge(s["turned"], 1 + g * KC + B * (1 + KC))

            self.normalize(dve, g + B, s["ffn_loaded"], g * 48 + 48, free,
                           lambda b: (t["x"][:, b, :], t["xn"][:, b, :], s["xn"]))
            for k in range(KC):
                n = g * KC + (B * (1 + KC) + k)
                dve.wait_ge(s["turned"], 1 + n + 1)
                nc.vector.tensor_copy(t["inT"][:, k, :], bank[0][:, :]).then_inc(s["inT_made"], 1)
            for c in range(KC):
                dve.wait_ge(s["silu_made"], 1 + g * KC + (c + 1))
                dve.wait_ge(s["up"], 1 + g * KC + (c + 1))
                nc.vector.tensor_tensor(t["inner"][:, c, :], bank[2][:, :], t["silu"][:, :], ALU.mult)\
                    .then_inc(s["inner"], 1)
            for b in range(B):
                dve.wait_ge(s["down"], 1 + g * B + (b + 1))
                nc.vector.tensor_tensor(t["x"][:, b, :], t["x"][:, b, :], bank[3][:, :], ALU.add)\
                    .then_inc(s["out"], 1)

    def tensor(self, pe):
        t, s, B, E, KC, H, FO, DI = self.t, self.s, self.B, self.E, self.KC, self.H, self.FO, self.DI
        nc, bank = self.nc, self.bank
        pe.wait_ge(s["ident"], 1 + 1)
        pe.wait_ge(s["consts"], 1 + 3)
        with pe.Fori(0, B) as b:
            pe.wait_ge(s["x_loaded"], 1 + b * 32 + 32)
            for layer in range(2):
                chunks = 1 if layer == 0 else KC
                if layer == 1:
                    pe.wait_ge(s["elu"], 1 + b * 2 + 1)
                for c in range(chunks):
                    n = self.chunk_no(b, layer, c)
                    pe.wait_ge(s["inT_made"], 1 + n)
                    for m in range(E):
                        src = t["ctx"][:, m, :] if layer == 0 else t["att"][:, m, c * P:(c + 1) * P]
                        last = nc.tensor.transpose(bank[0][:, m * P:(m + 1) * P], src, t["ident"][:, :])
                    last.then_inc(s["turned"], 1)
                pe.wait_ge(s["inT_made"], 1 + self.chunk_no(b, layer, chunks))
                before = 0 if layer == 0 else self.loads[0]
                pe.wait_ge(s["layer_loaded"], 1 + b * (16 * sum(self.loads)) + 16 * (before + self.loads[layer]))
                for m in range(E):
                    pe.wait_ge(s["feat_made"], 1 + self.layer_no(b, layer) * E + m)
                    for c in range(chunks):
                        last = nc.tensor.matmul(bank[1][:, :], t["inT"][:, c, m * P:(m + 1) * P], t["W"][:, c, :],
                                                start=(c == 0), stop=(c == chunks - 1))
                    last.then_inc(s["feat"], 1)
                pe.wait_ge(s["feat_made"], 1 + self.layer_no(b, layer) * E + E)
                pe.sem_inc(s["pe_waited"], 1)
                with pe.Fori(0, H) as h:
                    pe.wait_ge(s["diag"], 1 + self.head_no(b, layer, h) * E + E)
                    pe.wait_ge(s["z_made"], 1 + self.unit(b, layer, h, 0))
                    nc.tensor.matmul(bank[2][:, :], t["ones"][:, :],
                                     t["diag"][:, :, :].rearrange("p m g -> p (m g)"), start=True, stop=True)\
                        .then_inc(s["spread"], 1)
                    for e in range(E):
                        u = self.unit(b, layer, h, e)
                        pe.wait_ge(s["prob_made"], 1 + u + 1)
                        for m in range(E):
                            last = nc.tensor.transpose(bank[3][:, m * P:(m + 1) * P],
                                                       t["prob"][:, m * P:(m + 1) * P], t["ident"][:, :])
                        last.then_inc(s["prob_turned"], 1)
                        pe.wait_ge(s["probT_made"], 1 + u + 1)
                        pe.wait_ge(s["att"], 1 + u)
                        for m in range(E):
                            last = nc.tensor.matmul(bank[4][:, 0:FO], t["probT"][:, m, :],
                                                    t["feat"][:, m, bass.ds(h * FO, FO)],
                                                    start=(m == 0), stop=(m == E - 1))
                        last.then_inc(s["att_done"], 1)
        with pe.Fori(0, E) as g:
            pe.wait_ge(s["ffn_loaded"], 1 + g * 48 + 48)
            pe.wait_ge(s["xn"], 1 + g * B + B)
            for k in range(KC):
                n = g * KC + (B * (1 + KC) + k)
                pe.wait_ge(s["inT_made"], 1 + n)
                for b in range(B):
                    last = nc.tensor.transpose(bank[0][:, b * P:(b + 1) * P], t["xn"][:, b, k * P:(k + 1) * P],
                                               t["ident"][:, :])
                last.then_inc(s["turned"], 1)
            pe.wait_ge(s["inT_made"], 1 + g * KC + (B * (1 + KC) + KC))
            for c in range(KC):
                pe.wait_ge(s["inner"], 1 + g * KC + c)
                for half, name in enumerate(("gate", "up")):
                    for k in range(KC):
                        last = nc.tensor.matmul(bank[1 + half][:, :],
                                                t["gate_up"][:, k, half * DI + c * P:half * DI + (c + 1) * P],
                                                t["inT"][:, k, :], start=(k == 0), stop=(k == KC - 1))
                    last.then_inc(s[name], 1)
            pe.wait_ge(s["inner"], 1 + g * KC + KC)
            for b in range(B):
                pe.wait_ge(s["out"], 1 + g * B + b)
                for i in range(KC):
                    last = nc.tensor.matmul(bank[3][:, :], t["inner"][:, i, b * P:(b + 1) * P], t["down"][:, i, :],
                                            start=(i == 0), stop=(i == KC - 1))
                last.then_inc(s["down"], 1)


def build(nc, x, ctx, W0, a_self0, a_neigh0, b0, W1, a_self1, a_neigh1, b1, gate_up, down, out):
    B, N, D = x.shape
    F_IN = ctx.shape[2]
    H, _, FO = W0.shape
    E = gate_up.shape[0]
    KC = D // P
    DI = down.shape[1]
    D2 = 2 * DI
    assert N == E * P and D == N == DI == H * FO and F_IN == P and KC == E == B

    x_rows = x.rearrange("b (g e) d -> b g e d", e=E)
    out_rows = out.rearrange("b (g e) d -> b e g d", e=E)
    ctx_rows = ctx.rearrange("b (g e) f -> b g e f", e=E)

    with ExitStack() as stack:
        def sem(name):
            return stack.enter_context(nc.semaphore(name))

        def sb_in(where):
            return lambda name, shape, dt=F32: where.enter_context(nc.sbuf_tensor(name, shape, dt))

        main = ExitStack()
        sb = sb_in(main)

        x_sb = sb("x_sb", [P, B, E, D])
        sel_ctx = sb("sel_ctx", [P, 2, E, B, P], F32R)
        W0p = sb("W0p", [P, 2, D], F32R)
        W1p = sb("W1p", [P, KC, 2, D], F32R)
        xnT = sb("xnT", [P, KC, 2, B * P], F32R)
        ctx_xn = sb("ctx_xn", [P, B, D])
        stage = sb("stage", [P, 4, 2 * D])
        ident = sb("ident", [P, P])
        ident_bf = sb("ident_bf", [P, P], BF16)
        ones = sb("ones", [P, 1])
        ones_bf = sb("ones_bf", [P, P], BF16)
        b0_col = sb("b0_col", [P, KC])
        b1_rows = sb("b1_rows", [P, D])
        a_abs = sb("a_abs", [H, 4, FO])
        top8 = sb("top8", [P, B, E, 8])
        xstat = sb("xstat", [P, B, E, 6])
        xmv = sb("xmv", [P, B * E, 2])
        x2stat = sb("x2stat", [P, B, 6])
        x2mv = sb("x2mv", [P, B, 2])
        veps = sb("veps", [P, B * E])
        rstd = sb("rstd", [P, B])
        xrstd = sb("xrstd", [P, B * E])
        minus_half = sb("minus_half", [P, B * E])
        rowmax = sb("rowmax", [P, B + 3])
        allmax = sb("allmax", [P, B + 3])
        ctxmax = sb("ctxmax", [P, 1])
        colmax = sb("colmax", [P, 2])
        bound = sb("bound", [P, 6])
        gap = sb("gap", [P, B * E])
        lead = sb("lead", [P, B * E])
        sure = sb("sure", [P, B * E])
        sure_n = sb("sure_n", [P, 1])
        flag = sb("flag", [1, 1], I32)
        ctx_sb = ctx_xn[:, :, :].rearrange("p b (e f) -> p b e f", e=E)
        xn = ctx_xn

        GUp = sb("GUp", [P, KC, 2, D2], F32R)
        DNp = sb("DNp", [P, KC, 2, D], F32R)

        with ExitStack() as early:
            sbe = sb_in(early)
            G = sbe("G", [P, 2, E, N], BF16)
            GT = sbe("GT", [P, 2, E, N], F32R)
            ctxp = sbe("ctxp", [P, 2, E, 2, F_IN], F32R)
            sel1 = sbe("sel1", [P, 2, E, 2, F_IN], F32R)
            absw = sbe("absw", [P, 1 + KC, D], BF16)
        parts = sb("parts", [P, KC + 2, 2, B * P], F32R)
        val = sb("val", [P, B, D])
        exps = sb("exps", [P, EXPS, D])
        sil = sb("sil", [P, 2, D])

        def h_slot(e, c):
            return (KC + c) % (KC + 2) if e == 1 else c

        def in_slot(n):
            return KC + n % 2

        exp_order = [("h", e, c) for e in range(2) for c in range(KC)] + [("y", 0, b) for b in range(B)]
        for e in range(1, E):
            if e + 1 < E:
                exp_order += [("h", e + 1, c) for c in range(KC)]
            exp_order += [("y", e, b) for b in range(B)]

        def exp_slot(kind, e, c):
            return exps[:, exp_order.index((kind, e, c)) % EXPS, :]

        def gu_parts(e, k):
            if e < E - 1:
                return GUp[:, k, :, :]
            if k < KC // 2:
                spare = sel_ctx[:, :, :, :, :].rearrange("p r e b g -> p (r e b g)")
            else:
                spare = W1p[:, :, :, :].rearrange("p c r d -> p (c r d)")
            return spare[:, (k % 2) * 2 * D2:(k % 2 + 1) * 2 * D2].rearrange("p (r d) -> p r d", r=2)

        main.close()

        gsb = sb_in(stack)
        gen = {
            "x": gsb("gen_x", [P, E, D]),
            "mask": gsb("gen_mask", [P, E, E, P]),
            "ctx": gsb("gen_ctx", [P, E, F_IN]),
            "W": gsb("gen_W", [P, KC, D]),
            "a": gsb("gen_a", [P, 2, D]),
            "bias": gsb("gen_bias", [P, D]),
            "inT": gsb("gen_inT", [P, KC, N]),
            "feat": gsb("gen_feat", [P, E, D]),
            "prod": gsb("gen_prod", [P, D]),
            "score": gsb("gen_score", [P, 2, E, H]),
            "diag": gsb("gen_diag", [P, E, P]),
            "z": gsb("gen_z", [P, N]),
            "leaky": gsb("gen_leaky", [P, N]),
            "logit": gsb("gen_logit", [P, N]),
            "prob": gsb("gen_prob", [P, N]),
            "probT": gsb("gen_probT", [P, E, P]),
            "row": gsb("gen_row", [P, 4]),
            "att": gsb("gen_att", [P, E, D]),
            "exp": gsb("gen_exp", [P, E, D]),
            "ident": gsb("gen_ident", [P, P]),
            "ones": gsb("gen_ones", [P, P]),
            "stat": gsb("gen_stat", [P, E, 6]),
            "mv": gsb("gen_mv", [P, E, 2]),
            "veps": gsb("gen_veps", [P, E]),
            "rstd": gsb("gen_rstd", [P, E]),
            "power": gsb("gen_power", [P, E]),
            "gate_up": gsb("gen_gate_up", [P, KC, D2]),
            "down": gsb("gen_down", [P, KC, D]),
            "xn": gsb("gen_xn", [P, B, D]),
            "silu": gsb("gen_silu", [P, D]),
            "inner": gsb("gen_inner", [P, KC, B * P]),
        }

        bank = [stack.enter_context(nc.psum_tensor(f"bank{i}", [P, 512], F32)) for i in range(8)]

        x_loaded = [[sem(f"x_loaded{b}_{piece}") for piece in range(E if b == 0 else 2)] for b in range(B)]
        ctx_loaded = [sem(f"ctx_loaded{b}") for b in range(B)]
        small_loaded = sem("small_loaded")
        stage_loaded = [sem(f"stage_loaded{s}") for s in range(4)]
        out_stored = sem("out_stored")
        consts_made = sem("consts_made")
        ident_made = sem("ident_made")
        ctx_lo = sem("ctx_lo")
        w_lo = sem("w_lo")
        veps_made = sem("veps_made")
        rstd_made = sem("rstd_made")
        allmax_made = sem("allmax_made")
        in_lo = sem("in_lo")
        last_in_lo = sem("last_in_lo")
        ctx_hi = sem("ctx_hi")
        w_hi = sem("w_hi")
        abs_made = sem("abs_made")
        GT_made = sem("GT_made")
        sel1_front = sem("sel1_front")
        sel_hi = sem("sel_hi")
        h_exp = sem("h_exp")
        h_hi = sem("h_hi")
        y_exp = sem("y_exp")
        xnT_hi = sem("xnT_hi")
        silu_made = sem("silu_made")
        in_hi = sem("in_hi")
        top_found = sem("top_found")
        G_made = sem("G_made")
        sel1_back = sem("sel1_back")
        sel_lo = sem("sel_lo")
        rowmax_clear = sem("rowmax_clear")
        rowmax_made = sem("rowmax_made")
        colmax_made = sem("colmax_made")
        h_read = sem("h_read")
        in_read = sem("in_read")
        h_neg = sem("h_neg")
        h_made = sem("h_made")
        h_lo = sem("h_lo")
        h_lo_pool = sem("h_lo_pool")
        y_made = sem("y_made")
        y_neg = sem("y_neg")
        y_elu = sem("y_elu")
        x2_made = sem("x2_made")
        xstat_made = sem("xstat_made")
        x2stat_made = sem("x2stat_made")
        x2mv_made = sem("x2mv_made")
        xmv_made = sem("xmv_made")
        xn_made = sem("xn_made")
        xnT_lo = sem("xnT_lo")
        in_made = sem("in_made")
        out_made = sem("out_made")
        bound_step = sem("bound_step")
        sure_made = sem("sure_made")
        flag_made = sem("flag_made")
        GT_turned = sem("GT_turned")
        sel1_done = sem("sel1_done")
        sel_done = sem("sel_done")
        colsum_done = sem("colsum_done")
        h_done = sem("h_done")
        y_done = sem("y_done")
        xn_turned = sem("xn_turned")
        gate_done = sem("gate_done")
        up_done = sem("up_done")
        down_done = sem("down_done")
        sure_counted = sem("sure_counted")

        W1_v = W1.rearrange("h (c p) o -> p c h o", p=P)
        GU_v = gate_up.rearrange("e (k p) d -> e p k d", p=P)
        DN_v = down.rearrange("e (i p) d -> e p i d", p=P)

        def halves(t):
            return t.rearrange("p (c d) -> p c d", c=2)

        fills = []
        fills.append(dict(
            dma=[(stage[:, 0, 0:D].rearrange("p (h o) -> p h o", h=H), W0.rearrange("h f o -> f h o"))],
            raw=stage[:, 0, 0:D], hi=W0p[:, HI, :], lo=W0p[:, LO, :], kind="W0"))
        for j in range(KC // 2):
            s = len(fills) % 4
            fills.append(dict(
                dma=[(stage[:, s, c * D:(c + 1) * D].rearrange("p (h o) -> p h o", h=H), W1_v[:, 2 * j + c])
                     for c in range(2)],
                raw=halves(stage[:, s, :]), hi=W1p[:, 2 * j:2 * j + 2, HI, :], lo=W1p[:, 2 * j:2 * j + 2, LO, :],
                kind="W1"))
        FIRST = len(fills)
        for e in range(E):
            for k in range(KC):
                s = len(fills) % 4
                fills.append(dict(dma=[(stage[:, s, :], GU_v[e, :, k, :])], raw=stage[:, s, :],
                                  hi=gu_parts(e, k)[:, HI, :], lo=gu_parts(e, k)[:, LO, :], kind="GU"))
            for j in range(KC // 2):
                s = len(fills) % 4
                fills.append(dict(dma=[(halves(stage[:, s, :]), DN_v[e, :, 2 * j:2 * j + 2, :])],
                                  raw=halves(stage[:, s, :]), hi=DNp[:, 2 * j:2 * j + 2, HI, :],
                                  lo=DNp[:, 2 * j:2 * j + 2, LO, :], kind="DN"))
        PER_E = KC + KC // 2
        slot_total = [0] * 4
        for f, fill in enumerate(fills):
            slot_total[f % 4] += 16 * len(fill["dma"])
            fill["landed"] = slot_total[f % 4]

        def gu_fill(e, k):
            return FIRST + PER_E * e + k

        def dn_fill(e, j):
            return FIRST + PER_E * e + KC + j

        def turned(b, pair):
            return bank[2 * (b % 2) + pair][:, :].bitcast(BF16).rearrange("p (m n) -> p m n", m=2)

        def sel1_bank(b, half):
            return bank[half] if b == B - 1 else bank[4 + half]

        def sel_bank(b, part):
            return bank[4 + part] if b == B - 1 else bank[6 + part]

        def h_bank(e, c):
            return bank[c] if e == 1 else bank[4 + c]

        def y_bank(e, b):
            return bank[4 + b] if e == 0 else bank[b]

        def wait_h_read(engine, e, c):
            if c < KC - 1:
                engine.wait_ge(h_read, (KC - 1) * e + c + 1)
            else:
                engine.wait_ge(y_done, B * (e + 1))

        def wait_in_read(engine, e, c):
            if c < KC - 1:
                engine.wait_ge(in_read, (KC - 1) * e + c + 1)
            else:
                engine.wait_ge(down_done, B * (e + 1))

        pool_lows = [(0, c) for c in range(KC // 2, KC)] + [(1, c) for c in range(KC)]
        dve_lows = [(e, c) for e in range(E) for c in range(KC) if (e, c) not in pool_lows]

        def wait_h_lo(engine, e, c):
            if (e, c) in pool_lows:
                engine.wait_ge(h_lo_pool, pool_lows.index((e, c)) + 1)
            else:
                engine.wait_ge(h_lo, dve_lows.index((e, c)) + 1)

        def wait_exp_slot(engine, kind, e, c):
            n = exp_order.index((kind, e, c))
            if n >= EXPS:
                old_kind, old_e, old_c = exp_order[n - EXPS]
                if old_kind == "h":
                    wait_h_lo(engine, old_e, old_c)
                else:
                    engine.wait_ge(y_elu, B * old_e + old_c + 1)

        def wait_in_lo(engine, n):
            if n < KC * E - 1:
                engine.wait_ge(in_lo, n + 1)
            else:
                engine.wait_ge(last_in_lo, 1)

        gen_sems = {name: sem("gen_" + name) for name in GENERAL_SIGNALS}
        general = General(nc, gen, gen_sems, bank, dict(
            x=x_rows, ctx=ctx_rows, W0=W0, a_self0=a_self0, a_neigh0=a_neigh0, b0=b0, W1=W1_v, a_self1=a_self1,
            a_neigh1=a_neigh1, b1=b1, gate_up=GU_v, down=DN_v, out=out), (B, N, D, F_IN, H, FO, E, KC, DI))

        def unless_sure(engine, program):
            engine.wait_ge(flag_made, 1)
            n_sure = engine.value_load(flag[0:1, 0:1])
            with engine.If(n_sure < B * N):
                engine.wait_ge(out_stored, 16 * B * E)
                program(engine)

        block = stack.enter_context(nc.Block())

        @block.sync
        def _(sp):
            def load_fill(f):
                if f >= 4:
                    sp.wait_ge(w_lo, f - 3)
                if 4 <= f < 4 + FIRST:
                    sp.wait_ge(abs_made, f - 3)
                for dst, src in fills[f]["dma"]:
                    sp.dma_start(dst, src).then_inc(stage_loaded[f % 4], 16)

            for b in range(B):
                width = E // len(x_loaded[b])
                for piece, loaded in enumerate(x_loaded[b]):
                    rows = slice(width * piece, width * (piece + 1))
                    sp.dma_start(x_sb[:, b, rows, :], x_rows[b][:, rows, :]).then_inc(loaded, 16)
                sp.dma_start(ctx_sb[:, b, :, :], ctx_rows[b]).then_inc(ctx_loaded[b], 16)
            for f in range(4):
                load_fill(f)
            sp.dma_start(b0_col[:, :], b0.rearrange("h o -> (h o)").rearrange("(c p) -> p c", p=P),
                         allow_slow_non_contiguous=True).then_inc(small_loaded, 16)
            sp.dma_start(b1_rows[:, :], b1.rearrange("h o -> (h o)").partition_broadcast(P))\
              .then_inc(small_loaded, 16)
            for j, a in enumerate((a_self0, a_neigh0, a_self1, a_neigh1)):
                sp.dma_start(a_abs[:, j, :], a).then_inc(small_loaded, 16)
            for f in range(4, len(fills)):
                load_fill(f)
            sp.wait_ge(out_stored, 16 * B * E)
            unless_sure(sp, general.sync)

        @block.gpsimd
        def _(pool):
            nc.gpsimd.memset(ident_bf[:, :], 0.0).then_inc(consts_made, 1)
            nc.gpsimd.memset(ident[:, :], 0.0).then_inc(consts_made, 1)
            nc.gpsimd.memset(ones[:, :], 1.0).then_inc(consts_made, 1)
            nc.gpsimd.memset(ones_bf[:, :], 1.0).then_inc(consts_made, 1)
            nc.gpsimd.memset(minus_half[:, :], -0.5).then_inc(consts_made, 1)
            pool.wait_ge(consts_made, 5)
            for m in (ident_bf, ident):
                nc.gpsimd.affine_select(out=m[:, :], in_=m[:, :], compare_op=ALU.not_equal, fill=1.0, base=0,
                                        pattern=[[-1, P]], channel_multiplier=1).then_inc(ident_made, 1)

            def w_low(f):
                pool.wait_ge(w_hi, f + 1)
                nc.gpsimd.tensor_tensor(fills[f]["lo"], fills[f]["raw"], fills[f]["hi"].bitcast(F32),
                                        ALU.subtract).then_inc(w_lo, 1)

            def ctx_low(b):
                pool.wait_ge(ctx_hi, b + 1)
                if b >= 2:
                    pool.wait_ge(sel1_done, 2 * (b - 1))
                nc.gpsimd.tensor_tensor(ctxp[:, b % 2, :, LO, :], ctx_sb[:, b, :, :],
                                        ctxp[:, b % 2, :, HI, :].bitcast(F32), ALU.subtract).then_inc(ctx_lo, 1)

            def residual(e, b):
                n = B * e + b
                pool.wait_ge(y_elu, n + 1)
                pool.wait_ge(xstat_made, n + 1)
                nc.gpsimd.tensor_tensor(x_sb[:, b, e, :], x_sb[:, b, e, :], val[:, b, :], ALU.add)\
                    .then_inc(x2_made, 1)

            def inverse_std(mv, cols, dst, turn):
                nc.gpsimd.tensor_scalar(veps[:, cols], mv[:, cols, 1], LN_EPS, None, ALU.add).then_inc(veps_made, 1)
                pool.wait_ge(veps_made, turn)
                nc.gpsimd.tensor_tensor(dst[:, cols], veps[:, cols], minus_half[:, cols], ALU.pow)\
                    .then_inc(rstd_made, 1)

            def x2_inverse_std(e, half):
                pool.wait_ge(x2mv_made, B * e + (half + 1) * B // 2)
                if e > 0:
                    pool.wait_ge(xn_made, B * e)
                inverse_std(x2mv, slice(half * B // 2, (half + 1) * B // 2), rstd, 2 * e + half + 1)

            def h_low(e, c):
                pool.wait_ge(h_hi, KC * e + c + 1)
                nc.gpsimd.tensor_tensor(parts[:, h_slot(e, c), LO, :], exp_slot("h", e, c),
                                        parts[:, h_slot(e, c), HI, :].bitcast(F32), ALU.subtract)\
                    .then_inc(h_lo_pool, 1)

            def inner_low(e, c):
                n = KC * e + c
                pool.wait_ge(in_hi, n + 1)
                nc.gpsimd.tensor_tensor(parts[:, in_slot(n), LO, :], sil[:, n % 2, :],
                                        parts[:, in_slot(n), HI, :].bitcast(F32), ALU.subtract).then_inc(in_lo, 1)

            for b in range(B):
                ctx_low(b)
            for f in range(gu_fill(0, KC // 2)):
                w_low(f)
            for e, c in pool_lows:
                h_low(e, c)
            for b in range(B):
                residual(0, b)
                if b == B - 2:
                    x2_inverse_std(0, 0)
            x2_inverse_std(0, 1)
            for k in range(KC // 2, KC):
                w_low(gu_fill(0, k))
            for e in range(E):
                for j in range(KC // 2):
                    w_low(dn_fill(e, j))
                for c in range(KC):
                    if e + 1 < E and c == KC // 2:
                        x2_inverse_std(e + 1, 0)
                        x2_inverse_std(e + 1, 1)
                    if KC * e + c < KC * E - 1:
                        inner_low(e, c)
                    if e + 1 < E and c < KC // 2:
                        residual(e + 1, 2 * c)
                        residual(e + 1, 2 * c + 1)
                    if e == E - 2:
                        w_low(gu_fill(E - 1, c))
                if e == 0:
                    pool.wait_ge(rowmax_made, B + 3)
                    nc.gpsimd.partition_all_reduce(allmax[:, :], rowmax[:, :], P, RMAX).then_inc(allmax_made, 1)
                if e + 1 < E - 1:
                    for k in range(KC):
                        w_low(gu_fill(e + 1, k))
                if e == E - 2:
                    pool.wait_ge(xmv_made, B * E)
                    inverse_std(xmv, slice(0, B * E), xrstd, 2 * E + 1)
            unless_sure(pool, general.gpsimd)

        @block.scalar
        def _(act):
            def w_high(f):
                act.wait_ge(stage_loaded[f % 4], fills[f]["landed"])
                e = (f - FIRST) // PER_E
                if fills[f]["kind"] == "GU" and 0 < e < E - 1:
                    act.wait_ge(up_done, KC * e)
                if fills[f]["kind"] == "GU" and e == E - 1:
                    act.wait_ge(h_done, KC * E)
                    act.wait_ge(y_done, B * E)
                if fills[f]["kind"] == "DN" and e > 0:
                    act.wait_ge(down_done, B * e)
                nc.scalar.copy(fills[f]["hi"], fills[f]["raw"]).then_inc(w_hi, 1)

            def weights_abs(f):
                dst = absw[:, 0, :] if f == 0 else absw[:, 2 * f - 1:2 * f + 1, :]
                nc.scalar.activation(dst, fills[f]["raw"], ACT.Abs).then_inc(abs_made, 1)

            def ctx_high(b):
                act.wait_ge(ctx_loaded[b], 16)
                if b >= 2:
                    act.wait_ge(sel1_done, 2 * (b - 1))
                nc.scalar.copy(ctxp[:, b % 2, :, HI, :], ctx_sb[:, b, :, :]).then_inc(ctx_hi, 1)

            def turned_G(b):
                for pair in range(2):
                    act.wait_ge(GT_turned, 2 * b + pair + 1)
                    if b >= 2:
                        act.wait_ge(sel_done, 2 * (b - 1))
                    nc.scalar.copy(GT[:, b % 2, 2 * pair:2 * pair + 2, :], turned(b, pair)).then_inc(GT_made, 1)

            def sel1_evac(b):
                act.wait_ge(sel1_done, 2 * b + 1)
                nc.scalar.copy(sel1[:, b % 2, 0:2, :, :].rearrange("p e r f -> p (e r f)"), sel1_bank(b, 0)[:, :])\
                    .then_inc(sel1_front, 1)

            def sel_evac(b):
                act.wait_ge(sel_done, 2 * b + 1)
                nc.scalar.copy(sel_ctx[:, HI, :, b, :], sel_bank(b, HI)[:, :].rearrange("p (e g) -> p e g", e=E))\
                    .then_inc(sel_hi, 1)

            ctx_high(0)
            turned_G(0)
            ctx_high(1)
            for b in range(B - 1):
                sel1_evac(b)
                if b == 0:
                    turned_G(1)
                if b + 2 < B:
                    ctx_high(b + 2)
                if b > 0:
                    w_high(b - 1)
                    weights_abs(b - 1)
                if b == B - 2:
                    sel1_evac(b + 1)
                    w_high(FIRST - 1)
                sel_evac(b)
                if b + 2 < B:
                    turned_G(b + 2)
            weights_abs(FIRST - 1)
            sel_evac(B - 1)
            w_high(gu_fill(0, 0))
            w_high(gu_fill(0, 1))

            def h_exp_of(e, c):
                n = KC * e + c
                act.wait_ge(h_done, n + 1)
                if n == 0:
                    act.wait_ge(small_loaded, 96)
                wait_exp_slot(act, "h", e, c)
                nc.scalar.activation(exp_slot("h", e, c), h_bank(e, c)[:, :], ACT.Exp, bias=b0_col[:, c:c + 1])\
                    .then_inc(h_exp, 1)

            def h_high(e, c):
                n = KC * e + c
                act.wait_ge(h_made, n + 1)
                if e == 1 and c >= 2:
                    wait_h_read(act, 0, c - 2)
                if e == 2 and c < 2:
                    wait_h_read(act, 1, c + 2)
                if e >= 3:
                    wait_h_read(act, e - 1, c)
                nc.scalar.copy(parts[:, h_slot(e, c), HI, :], exp_slot("h", e, c)).then_inc(h_hi, 1)

            def y_exp_of(e, b):
                act.wait_ge(y_made, B * e + b + 1)
                wait_exp_slot(act, "y", e, b)
                nc.scalar.activation(exp_slot("y", e, b), val[:, b, :], ACT.Exp).then_inc(y_exp, 1)

            def turned_xn(e, rows):
                for b in rows:
                    act.wait_ge(xn_turned, B * e + b + 1)
                    if e > 0:
                        act.wait_ge(up_done, KC * e)
                    nc.scalar.copy(xnT[:, :, HI, b * P:(b + 1) * P],
                                   bank[4 + b][:, :].rearrange("p (k g) -> p k g", k=KC)).then_inc(xnT_hi, 1)

            def silu_of(e, c):
                n = KC * e + c
                act.wait_ge(gate_done, n + 1)
                if n >= 2:
                    act.wait_ge(in_lo, n - 1)
                nc.scalar.activation(sil[:, n % 2, :], bank[4 + 2 * (c % 2)][:, :], ACT.Silu).then_inc(silu_made, 1)

            def inner_high(e, c):
                n = KC * e + c
                act.wait_ge(in_made, n + 1)
                if n < 2:
                    wait_h_read(act, 1, n)
                else:
                    wait_in_read(act, (n - 2) // KC, (n - 2) % KC)
                nc.scalar.copy(parts[:, in_slot(n), HI, :], sil[:, n % 2, :]).then_inc(in_hi, 1)

            def store(e):
                for b in range(B):
                    act.wait_ge(out_made, B * e + b + 1)
                    act.dma_start(out_rows[b, e], x_sb[:, b, e, :]).then_inc(out_stored, 16)

            for n in range(2 * KC + 1):
                if n < 2 * KC:
                    h_exp_of(n // KC, n % KC)
                if n >= 2 * KC - 1:
                    y_exp_of(0, n - 2 * KC + 1)
                if n > 0:
                    h_high((n - 1) // KC, (n - 1) % KC)
                if 2 <= n < KC:
                    w_high(gu_fill(0, n))
            for b in range(2, B):
                y_exp_of(0, b)
            for j in range(KC // 2):
                w_high(dn_fill(0, j))
            turned_xn(0, (0, 1))
            h_exp_of(2, 0)
            h_exp_of(2, 1)
            turned_xn(0, (2, 3))
            for e in range(E):
                if e > 0:
                    turned_xn(e, range(B))
                    if e < E - 1:
                        for k in range(KC):
                            w_high(gu_fill(e, k))
                    store(e - 1)
                    for j in range(KC // 2):
                        w_high(dn_fill(e, j))
                if e + 2 < E:
                    for c in range(KC + 1):
                        if c < KC and (e > 0 or c >= 2):
                            h_exp_of(e + 2, c)
                        if c > 0:
                            h_high(e + 2, c - 1)
                for c in range(KC):
                    silu_of(e, c)
                    inner_high(e, c)
                    if c == 0 and e + 1 < E:
                        for b in range(B):
                            y_exp_of(e + 1, b)
                    if e == E - 2:
                        w_high(gu_fill(E - 1, c))
            store(E - 1)
            unless_sure(act, general.scalar)

        @block.vector
        def _(dve):
            nc.vector.memset(rowmax[:, :], 0.0).then_inc(rowmax_clear, 1)

            def find_tops(b):
                width = E // len(x_loaded[b])
                for e in range(E + 1):
                    if e < E:
                        if e % width == 0:
                            dve.wait_ge(x_loaded[b][e // width], 16)
                        nc.vector.max(top8[:, b, e, :], x_sb[:, b, e, :]).then_inc(top_found, 1)
                    if e > 0:
                        dve.wait_ge(top_found, E * b + e)
                        if b >= 2 and e == 1:
                            dve.wait_ge(GT_turned, 2 * (b - 1))
                        nc.vector.tensor_scalar(G[:, b % 2, e - 1, :], x_sb[:, b, e - 1, :], top8[:, b, e - 1, 0:1],
                                                None, ALU.is_equal).then_inc(G_made, 1)

            def ctx_max(b):
                dve.wait_ge(ctx_loaded[b], 16)
                if b == 0:
                    dve.wait_ge(rowmax_clear, 1)
                nc.vector.tensor_reduce(rowmax[:, b:b + 1], ctx_xn[:, b, :], AX.X, ALU.max,
                                        apply_absolute_value=True).then_inc(rowmax_made, 1)

            def sel1_evac(b):
                dve.wait_ge(sel1_done, 2 * b + 2)
                nc.vector.tensor_copy(sel1[:, b % 2, 2:4, :, :].rearrange("p e r f -> p (e r f)"), sel1_bank(b, 1)[:, :])\
                    .then_inc(sel1_back, 1)

            def sel_evac(b):
                dve.wait_ge(sel_done, 2 * b + 2)
                nc.vector.tensor_copy(sel_ctx[:, LO, :, b, :], sel_bank(b, LO)[:, :].rearrange("p (e g) -> p e g", e=E))\
                    .then_inc(sel_lo, 1)

            def column_maxima():
                for j in range(2):
                    dve.wait_ge(colsum_done, j + 1)
                    nc.vector.tensor_reduce(colmax[:, j:j + 1], bank[2 + j][:, :], AX.X, ALU.max)\
                        .then_inc(colmax_made, 1)

            def x_stats(e, b):
                nc.vector.bn_stats(xstat[:, b, e, :], x_sb[:, b, e, :]).then_inc(xstat_made, 1)

            def small_maxima():
                dve.wait_ge(small_loaded, 96)
                for layer in range(2):
                    nc.vector.tensor_reduce(rowmax[0:H, B + layer:B + layer + 1],
                                            a_abs[:, 2 * layer:2 * layer + 2, :],
                                            AX.XY, ALU.add, apply_absolute_value=True).then_inc(rowmax_made, 1)
                nc.vector.tensor_reduce(rowmax[:, B + 2:B + 3], b0_col[:, :], AX.X, ALU.max,
                                        apply_absolute_value=True).then_inc(rowmax_made, 1)

            for b in range(B - 1):
                find_tops(b)
            sel1_evac(0)
            find_tops(B - 1)
            sel_evac(0)
            sel1_evac(1)
            ctx_max(0)
            ctx_max(1)
            sel_evac(1)
            x_stats(0, 0)
            sel1_evac(2)
            ctx_max(2)
            sel1_evac(3)
            ctx_max(3)
            sel_evac(2)
            x_stats(0, 1)
            x_stats(0, 2)
            sel_evac(3)
            column_maxima()
            x_stats(0, 3)

            def h_value(e, c):
                n = KC * e + c
                dve.wait_ge(h_exp, n + 1)
                nc.vector.tensor_scalar(exp_slot("h", e, c), exp_slot("h", e, c), 1.0, -1.0, ALU.min, ALU.add)\
                    .then_inc(h_neg, 1)
                dve.wait_ge(h_neg, n + 1)
                nc.vector.scalar_tensor_tensor(exp_slot("h", e, c), h_bank(e, c)[:, :], b0_col[:, c:c + 1],
                                               exp_slot("h", e, c), ALU.add, ALU.max).then_inc(h_made, 1)

            def h_low(e, c):
                n = KC * e + c
                dve.wait_ge(h_hi, n + 1)
                nc.vector.tensor_tensor(parts[:, h_slot(e, c), LO, :], exp_slot("h", e, c),
                                        parts[:, h_slot(e, c), HI, :].bitcast(F32), ALU.subtract).then_inc(h_lo, 1)

            def y_value(e, b):
                n = B * e + b
                dve.wait_ge(y_done, n + 1)
                if e > 0:
                    dve.wait_ge(x2_made, n - B + 1)
                nc.vector.tensor_tensor(val[:, b, :], y_bank(e, b)[:, :], b1_rows[:, :], ALU.add).then_inc(y_made, 1)

            def y_elus(e, b):
                n = B * e + b
                dve.wait_ge(y_exp, n + 1)
                nc.vector.tensor_scalar(exp_slot("y", e, b), exp_slot("y", e, b), 1.0, -1.0, ALU.min, ALU.add)\
                    .then_inc(y_neg, 1)
                dve.wait_ge(y_neg, n + 1)
                nc.vector.tensor_tensor(val[:, b, :], val[:, b, :], exp_slot("y", e, b), ALU.max).then_inc(y_elu, 1)

            def x2_stats(e, b):
                n = B * e + b
                dve.wait_ge(x2_made, n + 1)
                nc.vector.bn_stats(x2stat[:, b, :], x_sb[:, b, e, :]).then_inc(x2stat_made, 1)
                dve.wait_ge(x2stat_made, n + 1)
                if e > 0 and b == 0:
                    dve.wait_ge(rstd_made, 2 * e)
                    dve.wait_ge(xn_made, B * e)
                nc.vector.bn_aggr(x2mv[:, b, :], x2stat[:, b, :]).then_inc(x2mv_made, 1)

            def normalize(e, half):
                dve.wait_ge(rstd_made, 2 * e + half + 1)
                for b in range(half * B // 2, (half + 1) * B // 2):
                    if e > 0:
                        dve.wait_ge(xn_turned, B * (e - 1) + b + 1)
                    elif b == 0:
                        dve.wait_ge(rowmax_made, B)
                        dve.wait_ge(ctx_lo, B)
                    nc.vector.tensor_scalar(xn[:, b, :], x_sb[:, b, e, :], x2mv[:, b, 0:1], rstd[:, b:b + 1],
                                            ALU.subtract, ALU.mult).then_inc(xn_made, 1)

            def turned_low(e, b):
                dve.wait_ge(xnT_hi, B * e + b + 1)
                nc.vector.tensor_tensor(xnT[:, :, LO, b * P:(b + 1) * P],
                                        bank[4 + b][:, :].rearrange("p (k g) -> p k g", k=KC),
                                        xnT[:, :, HI, b * P:(b + 1) * P].bitcast(F32), ALU.subtract)\
                    .then_inc(xnT_lo, 1)

            def inner(e, c):
                n = KC * e + c
                dve.wait_ge(silu_made, n + 1)
                dve.wait_ge(up_done, n + 1)
                nc.vector.tensor_tensor(sil[:, n % 2, :], bank[5 + 2 * (c % 2)][:, :], sil[:, n % 2, :], ALU.mult)\
                    .then_inc(in_made, 1)

            def outputs(e):
                for b in range(B):
                    n = B * e + b
                    dve.wait_ge(down_done, n + 1)
                    dve.wait_ge(xn_made, n + 1)
                    nc.vector.tensor_tensor(x_sb[:, b, e, :], x_sb[:, b, e, :], bank[b][:, :], ALU.add)\
                        .then_inc(out_made, 1)

            def check_rows():
                steps = [0]

                def step(ins):
                    steps[0] += 1
                    ins.then_inc(bound_step, 1)
                    dve.wait_ge(bound_step, steps[0])

                dve.wait_ge(allmax_made, 1)
                dve.wait_ge(colmax_made, 2)
                step(nc.vector.tensor_reduce(ctxmax[:, :], allmax[:, 0:B], AX.X, ALU.max))
                step(nc.vector.tensor_tensor(bound[:, 0:1], ctxmax[:, :], colmax[:, 0:1], ALU.mult))
                step(nc.vector.tensor_tensor(bound[:, 1:2], bound[:, 0:1], allmax[:, B:B + 1], ALU.mult))
                step(nc.vector.scalar_tensor_tensor(bound[:, 2:3], bound[:, 0:1], 1.0, allmax[:, B + 2:B + 3],
                                                    ALU.add, ALU.add))
                step(nc.vector.tensor_tensor(bound[:, 3:4], bound[:, 2:3], colmax[:, 1:2], ALU.mult))
                step(nc.vector.tensor_tensor(bound[:, 4:5], bound[:, 3:4], allmax[:, B + 1:B + 2], ALU.mult))
                step(nc.vector.tensor_tensor(bound[:, 5:6], bound[:, 1:2], bound[:, 4:5], ALU.add))
                step(nc.vector.tensor_scalar(bound[:, 5:6], bound[:, 5:6], 2.1, UNDERFLOW, ALU.mult, ALU.add))
                tops = top8[:, :, :, :].rearrange("p b e t -> p (b e) t")
                step(nc.vector.tensor_tensor(gap[:, :], tops[:, :, 0], tops[:, :, 1], ALU.subtract))
                step(nc.vector.tensor_tensor(lead[:, :], tops[:, :, 0], xmv[:, :, 0], ALU.subtract))
                dve.wait_ge(rstd_made, 2 * E + 1)
                step(nc.vector.scalar_tensor_tensor(gap[:, :], gap[:, :], MASK, xrstd[:, :], ALU.mult, ALU.mult))
                step(nc.vector.tensor_tensor(lead[:, :], lead[:, :], xrstd[:, :], ALU.mult))
                step(nc.vector.tensor_scalar(lead[:, :], lead[:, :], 1.0, MASK * ROUNDINGS, ALU.add, ALU.mult))
                step(nc.vector.scalar_tensor_tensor(sure[:, :], lead[:, :], bound[:, 5:6], gap[:, :], ALU.add,
                                                    ALU.is_lt))
                nc.vector.tensor_reduce(sure_n[:, :], sure[:, :], AX.X, ALU.add).then_inc(sure_made, 1)

            for n in range(KC + 3):
                h_value(n // KC, n % KC)
                if n > 0 and (0, n - 1) in dve_lows:
                    h_low(0, n - 1)
            for b in range(B + 2):
                if b < B:
                    y_value(0, b)
                if b == 0:
                    h_value(1, KC - 1)
                if 0 < b <= B:
                    y_elus(0, b - 1)
                if b > B:
                    normalize(0, 0)
                if b > 1:
                    x2_stats(0, b - 2)
            turned_low(0, 0)
            turned_low(0, 1)
            normalize(0, 1)
            h_value(2, 0)
            turned_low(0, 2)
            turned_low(0, 3)
            for e in range(E):
                if 0 < e < E - 1:
                    outputs(e - 1)
                if e > 0:
                    for b in range(B):
                        turned_low(e, b)
                if e == E - 1:
                    outputs(e - 1)
                if e + 2 < E:
                    for c in range(KC + 1):
                        if c < KC and (e > 0 or c >= 1):
                            h_value(e + 2, c)
                        if c > 0:
                            h_low(e + 2, c - 1)
                if e + 1 < E:
                    y_value(e + 1, 0)
                    y_value(e + 1, 1)
                    inner(e, 0)
                    y_value(e + 1, 2)
                    y_value(e + 1, 3)
                    for b in range(B):
                        x_stats(e + 1, b)
                    y_elus(e + 1, 0)
                    y_elus(e + 1, 1)
                    inner(e, 1)
                    y_elus(e + 1, 2)
                    y_elus(e + 1, 3)
                    for b in range(B):
                        x2_stats(e + 1, b)
                    inner(e, 2)
                    normalize(e + 1, 0)
                    normalize(e + 1, 1)
                    if e == 0:
                        small_maxima()
                    if e == E - 2:
                        for t in range(B * E):
                            nc.vector.bn_aggr(xmv[:, t, :], xstat[:, t // E, t % E, :]).then_inc(xmv_made, 1)
                    inner(e, 3)
                else:
                    check_rows()
                    for c in range(KC):
                        inner(e, c)
                    dve.wait_ge(in_hi, KC * E)
                    n = KC * E - 1
                    nc.vector.tensor_tensor(parts[:, in_slot(n), LO, :], sil[:, n % 2, :],
                                            parts[:, in_slot(n), HI, :].bitcast(F32), ALU.subtract)\
                        .then_inc(last_in_lo, 1)
            outputs(E - 1)
            dve.wait_ge(sure_counted, 1)
            nc.vector.tensor_copy(flag[:, :], bank[4][0:1, 0:1]).then_inc(flag_made, 1)
            unless_sure(dve, general.vector)

        @block.tensor
        def _(pe):
            def turn(b):
                for e in range(E):
                    pe.wait_ge(G_made, E * b + e + 1)
                    for m in range(E):
                        if b >= 2 and e == 0 and m % 2 == 0:
                            pe.wait_ge(GT_made, 2 * (b - 2) + m // 2 + 1)
                        last = nc.tensor.transpose(turned(b, m // 2)[:, m % 2, e * P:(e + 1) * P],
                                                   G[:, b % 2, e, m::E], ident_bf[:, :])
                        if e == E - 1 and m % 2:
                            last.then_inc(GT_turned, 1)

            def select1(b):
                pe.wait_ge(ctx_lo, b + 1)
                pe.wait_ge(GT_made, 2 * (b + 1))
                if 0 < b < B - 1:
                    pe.wait_ge(sel1_front, b)
                    pe.wait_ge(sel1_back, b)
                for e in range(E):
                    dst = sel1_bank(b, e // 2)[:, (e % 2) * 2 * F_IN:(e % 2 + 1) * 2 * F_IN]
                    for k in range(E):
                        last = nc.tensor.matmul(dst, GT[:, b % 2, k, e * P:(e + 1) * P],
                                                ctxp[:, b % 2, k, :, :].rearrange("p r f -> p (r f)"),
                                                start=(k == 0), stop=(k == E - 1))
                    if e % 2:
                        last.then_inc(sel1_done, 1)

            def select2(b):
                pe.wait_ge(sel1_front, b + 1)
                pe.wait_ge(sel1_back, b + 1)
                if 0 < b < B - 1:
                    pe.wait_ge(sel_hi, b)
                    pe.wait_ge(sel_lo, b)
                for part in (HI, LO):
                    for k in range(E):
                        last = nc.tensor.matmul(sel_bank(b, part)[:, :], sel1[:, b % 2, k, part, :], GT[:, b % 2, k, :],
                                                start=(k == 0), stop=(k == E - 1))
                    last.then_inc(sel_done, 1)

            def column_sums():
                pe.wait_ge(abs_made, 3)
                nc.tensor.matmul(bank[2][:, :], ones_bf[:, :], absw[:, 0, :], start=True, stop=True)\
                    .then_inc(colsum_done, 1)
                for c in range(KC):
                    last = nc.tensor.matmul(bank[3][:, :], ones_bf[:, :], absw[:, 1 + c, :],
                                            start=(c == 0), stop=(c == KC - 1))
                last.then_inc(colsum_done, 1)

            pe.wait_ge(ident_made, 2)
            turn(0)
            select1(0)
            turn(1)
            turn(2)
            select2(0)
            select1(1)
            turn(3)
            select2(1)
            select1(2)
            select1(3)
            select2(2)
            select2(3)
            column_sums()

            def layer0(e, chunks):
                if e == 0:
                    pe.wait_ge(sel_hi, B)
                    pe.wait_ge(sel_lo, B)
                    pe.wait_ge(w_lo, 1)
                for c in chunks:
                    if e == 1 and c >= 2:
                        pe.wait_ge(colmax_made, c - 1)
                    if e >= 2:
                        pe.wait_ge(xnT_lo, B * (e - 2) + c + 1)
                    for j, (w, v) in enumerate(TERMS):
                        last = nc.tensor.matmul(h_bank(e, c)[:, :], W0p[:, w, c * P:(c + 1) * P],
                                                sel_ctx[:, v, e, :, :].rearrange("p b g -> p (b g)"),
                                                start=(j == 0), stop=(j == 2))
                    last.then_inc(h_done, 1)

            layer1_steps = [(c, b) for c in range(KC - 2) for b in range(B)]
            layer1_steps += [(c, b) for b in range(B) for c in (KC - 2, KC - 1)]

            def layer1(e, steps):
                for c, b in steps:
                    if e == 0 and c == 0 and b == 0:
                        pe.wait_ge(w_lo, FIRST)
                    if b == 0:
                        wait_h_lo(pe, e, c)
                    if c == 0 and e < 2:
                        pe.wait_ge(h_made, KC * e + b + 1)
                    if c == 0 and e >= 2:
                        pe.wait_ge(out_made, B * (e - 2) + b + 1)
                    for j, (w, v) in enumerate(TERMS):
                        last = nc.tensor.matmul(y_bank(e, b)[:, :], parts[:, h_slot(e, c), w, b * P:(b + 1) * P],
                                                W1p[:, c, v, :],
                                                start=(c == 0 and j == 0), stop=(c == KC - 1 and j == 2))
                    if c == KC - 1:
                        last.then_inc(y_done, 1)
                    elif b == B - 1:
                        last.then_inc(h_read, 1)

            def turn_xn(e, rows):
                for b in rows:
                    if e == 0:
                        pe.wait_ge(y_made, b + 1)
                    else:
                        pe.wait_ge(in_made, KC * e - 1 + b // 2)
                    pe.wait_ge(xn_made, B * e + b + 1)
                    for k in range(KC):
                        last = nc.tensor.transpose(bank[4 + b][:, k * P:(k + 1) * P], xn[:, b, k * P:(k + 1) * P],
                                                   ident[:, :])
                    last.then_inc(xn_turned, 1)

            def gate_and_up(e, c):
                if c == 0:
                    pe.wait_ge(xnT_lo, B * (e + 1))
                for half, done in ((0, gate_done), (1, up_done)):
                    if c < 2 and e + 2 < E:
                        pe.wait_ge(h_made, KC * (e + 2) + 2 * c + half + 1)
                    if c >= 2:
                        pe.wait_ge(in_made, KC * e + c - 1)
                    col = half * DI + c * P
                    for k in range(KC):
                        if c == 0 and half == 0:
                            pe.wait_ge(w_lo, gu_fill(e, k) + 1)
                        for j, (w, v) in enumerate(TERMS):
                            last = nc.tensor.matmul(bank[4 + 2 * (c % 2) + half][:, :],
                                                    gu_parts(e, k)[:, w, col:col + P], xnT[:, k, v, :],
                                                    start=(k == 0 and j == 0), stop=(k == KC - 1 and j == 2))
                    last.then_inc(done, 1)

            def project_down(e, i):
                n = KC * e + i
                if i % 2 == 0:
                    pe.wait_ge(w_lo, dn_fill(e, i // 2) + 1)
                wait_in_lo(pe, n)
                for b in range(B):
                    if i == 0:
                        if e < E - 1:
                            pe.wait_ge(y_made, B * (e + 1) + b + 1)
                        else:
                            pe.wait_ge(out_made, B * (e - 1) + b + 1)
                    for j, (w, v) in enumerate(TERMS):
                        last = nc.tensor.matmul(bank[b][:, :], parts[:, in_slot(n), w, b * P:(b + 1) * P],
                                                DNp[:, i, v, :],
                                                start=(i == 0 and j == 0), stop=(i == KC - 1 and j == 2))
                    if i == KC - 1:
                        last.then_inc(down_done, 1)
                if i < KC - 1:
                    last.then_inc(in_read, 1)

            layer0(0, range(KC))
            layer0(1, range(KC))
            layer1(0, layer1_steps)
            layer1(1, layer1_steps[:-2])
            turn_xn(0, (0, 1))
            layer1(1, layer1_steps[-2:])
            layer0(2, (0, 1))
            turn_xn(0, (2, 3))
            layer0(2, (2, 3))
            for e in range(E):
                for c in range(KC):
                    gate_and_up(e, c)
                    if c > 0:
                        project_down(e, c - 1)
                if e + 1 < E:
                    turn_xn(e + 1, range(B))
                else:
                    pe.wait_ge(sure_made, 1)
                    pe.wait_ge(in_made, KC * e + 3)
                    nc.tensor.matmul(bank[4][0:1, 0:1], sure_n[:, 0:1], ones[:, 0:1], start=True, stop=True)\
                        .then_inc(sure_counted, 1)
                project_down(e, KC - 1)
                if e + 2 < E:
                    layer1(e + 2, layer1_steps)
                if e + 3 < E:
                    layer0(e + 3, range(KC))
            unless_sure(pe, general.tensor)


_INS = ['x', 'ctx_512', 'L0_xattn_W0', 'L0_xattn_a_self0', 'L0_xattn_a_neigh0', 'L0_xattn_b0', 'L0_xattn_W1',
        'L0_xattn_a_self1', 'L0_xattn_a_neigh1', 'L0_xattn_b1', 'L0_ffn_gate_up_proj', 'L0_ffn_down_proj']


def kernel(**inputs):
    import numpy as _np
    import concourse.bacc as _bacc
    from concourse import mybir as _mybir
    from concourse.bass_utils import run_bass_kernel_spmd as _run

    nc = _bacc.Bacc("TRN2", target_bir_lowering=False, num_devices=1)
    arrays, args = {}, []
    for name in _INS:
        a = _np.ascontiguousarray(inputs[name])
        arrays[f"in_{name}"] = a
        args.append(nc.dram_tensor(f"in_{name}", a.shape, _mybir.dt.from_np(a.dtype), kind="ExternalInput").ap())
    shape = inputs['x'].shape
    args.append(nc.dram_tensor("out_0", shape, _mybir.dt.float32, kind="ExternalOutput").ap())
    build(nc, *args)
    r = _run(nc, [arrays], core_ids=[0])
    return r.results[0]["out_0"]
```
